# Optimizing a Trainium2 kernel written in Bass

```python
import numpy as np
import jax
import jax.numpy as jnp

def _softmax(x, axis=-1):
    return jax.nn.softmax(x, axis=axis)

def _gelu(x):
    return jax.nn.gelu(x, approximate=True)

def _silu(x):
    return jax.nn.silu(x)

def _sigmoid(x):
    return jax.nn.sigmoid(x)

def _layernorm(x, axis=-1, eps=1e-05):
    m = jnp.mean(x, axis=axis, keepdims=True)
    v = jnp.var(x, axis=axis, keepdims=True)
    return (x - m) / jnp.sqrt(v + eps)

def _scatter_add(tgt, idx, src, axis=0):
    return tgt.at[idx].add(src)

def _segment_sum(src, seg, n):
    return jax.ops.segment_sum(src, seg, n)
kernel_name = 'mk_xattn_ffn_d2_seqx_r4_cc87ab'

def setup_inputs(seed: int=0):
    np.random.seed(seed)
    _w = jnp.asarray

    def _rec_inputs():
        import jax
        import jax.numpy as jnp
        _rk = jax.random.key(seed)
        x = -0.0002928 + 1 * jax.random.normal(jax.random.fold_in(_rk, 1), (8, 256, 256), jnp.float32)
        _lenS = 256 - jax.random.randint(jax.random.fold_in(_rk, 7), (8,), 0, max(1, 256 // 4) + 1, jnp.int32)
        _lenS2 = 256 - jax.random.randint(jax.random.fold_in(_rk, 8), (8,), 0, max(1, 256 // 4) + 1, jnp.int32)
        _ctx_1024P = jax.random.normal(jax.random.fold_in(_rk, 11), (8, 16, 256), jnp.float32)
        _ctx_1024c = jax.random.dirichlet(jax.random.fold_in(_rk, 511), 0.3 * jnp.ones((16,), jnp.float32), (8, 256))
        _ctx_1024t = jnp.einsum('bsk,bkd->bsd', _ctx_1024c, _ctx_1024P)
        _ctx_1024t = _ctx_1024t * jax.lax.rsqrt(jnp.mean(jnp.square(_ctx_1024t)) + 1e-12) * 0.953939
        ctx_1024 = -1.39393e-06 + 0.999914 * (_ctx_1024t + 0.3 * jax.random.normal(jax.random.fold_in(_rk, 611), (8, 256, 256), jnp.float32))
        _validS = jnp.arange(256)[None, :] < _lenS[:, None]
        _validS2 = jnp.arange(256)[None, :] < _lenS2[:, None]
        _causal = jnp.tril(jnp.ones((256, 256), dtype=bool))
        mask_Bx1xSxS2_ik1 = jnp.where(jnp.broadcast_to(_validS2[:, None, None, :], (8, 1, 256, 256)), 1, 0).astype(jnp.int32)
        mask_BxS2_bf1 = jnp.ones((8, 256), dtype=bool)
        return (x, ctx_1024, mask_Bx1xSxS2_ik1, mask_BxS2_bf1)
    x, ctx_1024, mask_Bx1xSxS2_ik1, mask_BxS2_bf1 = _rec_inputs()

    def _L0_xattn_setup():
        import jax, jax.numpy as jnp
        import numpy as np
        EMBED = 256
        HEADS = 16
        HEAD_DIM = EMBED // HEADS
        key = jax.random.key(seed)
        ks = jax.random.split(key, 12)
        B, S, E = (2, 512, EMBED)
        s = 1.0 / np.sqrt(E)
        inp = {'queries': jax.random.normal(ks[0], (B, S, E), jnp.float32), 'keys': jax.random.normal(ks[1], (B, S, E), jnp.float32), 'values': jax.random.normal(ks[2], (B, S, E), jnp.float32), 'mask': jax.random.randint(ks[3], (B, 1, S, S), 0, 2, jnp.int32), 'Wq': jax.random.normal(ks[4], (E, E), jnp.float32) * s, 'bq': jax.random.normal(ks[5], (E,), jnp.float32) * s, 'Wk': jax.random.normal(ks[6], (E, E), jnp.float32) * s, 'bk': jax.random.normal(ks[7], (E,), jnp.float32) * s, 'Wv': jax.random.normal(ks[8], (E, E), jnp.float32) * s, 'bv': jax.random.normal(ks[9], (E,), jnp.float32) * s, 'Wo': jax.random.normal(ks[10], (E, E), jnp.float32) * s, 'bo': jax.random.normal(ks[11], (E,), jnp.float32) * s}
        return inp
    _L0_xattn_all = _L0_xattn_setup()
    _L0_xattn_in = {k: v for k, v in _L0_xattn_all.items() if k in ('Wq', 'bq', 'Wk', 'bk', 'Wv', 'bv', 'Wo', 'bo')}
    del _L0_xattn_all

    def _L0_ffn_setup():
        import jax, jax.numpy as jnp
        import numpy as np
        EMBED = 256
        NUM_EXPERTS = 8
        TOP_K = 2
        key = jax.random.key(seed)
        ks = jax.random.split(key, 6)
        scale = EMBED ** (-0.5)
        return {'x': jax.random.normal(ks[0], (4, 1024, EMBED), jnp.float32), 'router_w': jax.random.normal(ks[1], (EMBED, NUM_EXPERTS), jnp.float32) * scale, 'router_b': jnp.zeros((NUM_EXPERTS,), jnp.float32), 'we_gate': jax.random.normal(ks[2], (NUM_EXPERTS, EMBED, EMBED), jnp.float32) * scale, 'we_up': jax.random.normal(ks[3], (NUM_EXPERTS, EMBED, EMBED), jnp.float32) * scale, 'we_down': jax.random.normal(ks[4], (NUM_EXPERTS, EMBED, EMBED), jnp.float32) * scale}
    _L0_ffn_all = _L0_ffn_setup()
    _L0_ffn_in = {k: v for k, v in _L0_ffn_all.items() if k in ('router_w', 'router_b', 'we_gate', 'we_up', 'we_down')}
    del _L0_ffn_all

    def _L1_xattn_setup():
        import jax, jax.numpy as jnp
        import numpy as np
        D_MODEL = 256
        N_HEADS = 16
        HEAD_DIM = D_MODEL // N_HEADS
        key = jax.random.key(seed)
        ks = jax.random.split(key, 9)
        B, T, S, D = (4, 512, 128, D_MODEL)
        sc = 1.0 / np.sqrt(D)
        return {'x': jax.random.normal(ks[0], (B, T, D), dtype=jnp.float32), 'context': jax.random.normal(ks[1], (B, S, D), dtype=jnp.float32), 'context_mask': jnp.ones((B, S), dtype=bool), 'Wq': jax.random.normal(ks[2], (D, D), dtype=jnp.float32) * sc, 'bq': jnp.zeros((D,), dtype=jnp.float32), 'Wkv': jax.random.normal(ks[3], (D, 2 * D), dtype=jnp.float32) * sc, 'bkv': jnp.zeros((2 * D,), dtype=jnp.float32), 'Wp': jax.random.normal(ks[4], (D, D), dtype=jnp.float32) * sc, 'bp': jnp.zeros((D,), dtype=jnp.float32)}
    _L1_xattn_all = _L1_xattn_setup()
    _L1_xattn_in = {k: v for k, v in _L1_xattn_all.items() if k in ('Wq', 'bq', 'Wkv', 'bkv', 'Wp', 'bp')}
    del _L1_xattn_all

    def _L1_ffn_setup():
        import jax, jax.numpy as jnp
        import numpy as np
        N_EXPERTS = 8
        CAP_FACTOR = 1.25
        BATCH, SEQ, DMODEL, DFF = (4, 512, 256, 1024)
        key = jax.random.key(seed)
        k0, k1, k2, k3 = jax.random.split(key, 4)
        x = jax.random.normal(k0, (BATCH, SEQ, DMODEL), dtype=jnp.float32)
        Wr = jax.random.normal(k1, (DMODEL, N_EXPERTS), dtype=jnp.float32) * 0.02
        W1 = jax.random.normal(k2, (N_EXPERTS, DMODEL, DFF), dtype=jnp.float32) * 0.02
        W2 = jax.random.normal(k3, (N_EXPERTS, DFF, DMODEL), dtype=jnp.float32) * 0.02
        return {'x': x, 'Wr': Wr, 'W1': W1, 'W2': W2}
    _L1_ffn_all = _L1_ffn_setup()
    _L1_ffn_in = {k: v for k, v in _L1_ffn_all.items() if k in ('Wr', 'W1', 'W2')}
    del _L1_ffn_all
    return {'x': x, 'ctx_1024': ctx_1024, 'mask_Bx1xSxS2_ik1': mask_Bx1xSxS2_ik1, 'mask_BxS2_bf1': mask_BxS2_bf1, 'L0_xattn_Wq': _L0_xattn_in['Wq'], 'L0_xattn_bq': _L0_xattn_in['bq'], 'L0_xattn_Wk': _L0_xattn_in['Wk'], 'L0_xattn_bk': _L0_xattn_in['bk'], 'L0_xattn_Wv': _L0_xattn_in['Wv'], 'L0_xattn_bv': _L0_xattn_in['bv'], 'L0_xattn_Wo': _L0_xattn_in['Wo'], 'L0_xattn_bo': _L0_xattn_in['bo'], 'L0_ffn_router_w': _L0_ffn_in['router_w'], 'L0_ffn_router_b': _L0_ffn_in['router_b'], 'L0_ffn_we_gate': _L0_ffn_in['we_gate'], 'L0_ffn_we_up': _L0_ffn_in['we_up'], 'L0_ffn_we_down': _L0_ffn_in['we_down'], 'L1_xattn_Wq': _L1_xattn_in['Wq'], 'L1_xattn_bq': _L1_xattn_in['bq'], 'L1_xattn_Wkv': _L1_xattn_in['Wkv'], 'L1_xattn_bkv': _L1_xattn_in['bkv'], 'L1_xattn_Wp': _L1_xattn_in['Wp'], 'L1_xattn_bp': _L1_xattn_in['bp'], 'L1_ffn_Wr': _L1_ffn_in['Wr'], 'L1_ffn_W1': _L1_ffn_in['W1'], 'L1_ffn_W2': _L1_ffn_in['W2']}

def reference(x, ctx_1024, mask_Bx1xSxS2_ik1, mask_BxS2_bf1, L0_xattn_Wq, L0_xattn_bq, L0_xattn_Wk, L0_xattn_bk, L0_xattn_Wv, L0_xattn_bv, L0_xattn_Wo, L0_xattn_bo, L0_ffn_router_w, L0_ffn_router_b, L0_ffn_we_gate, L0_ffn_we_up, L0_ffn_we_down, L1_xattn_Wq, L1_xattn_bq, L1_xattn_Wkv, L1_xattn_bkv, L1_xattn_Wp, L1_xattn_bp, L1_ffn_Wr, L1_ffn_W1, L1_ffn_W2):
    import jax
    import jax.numpy as jnp

    def _L0_xattn_ref(queries, keys, values, mask, Wq, bq, Wk, bk, Wv, bv, Wo, bo):
        import jax, jax.numpy as jnp
        import numpy as np
        EMBED = 256
        HEADS = 16
        HEAD_DIM = EMBED // HEADS
        B, Q, E = queries.shape
        K = keys.shape[1]
        q = (queries @ Wq.T + bq).reshape(B, Q, HEADS, HEAD_DIM)
        k = (keys @ Wk.T + bk).reshape(B, K, HEADS, HEAD_DIM)
        v = (values @ Wv.T + bv).reshape(B, K, HEADS, HEAD_DIM)
        energy = jnp.einsum('nqhd,nkhd->nhqk', q, k)
        energy = jnp.where(mask == 0, jnp.float32(-1e+20), energy)
        attn = jax.nn.softmax(energy / jnp.sqrt(jnp.float32(E)), axis=3)
        out = jnp.einsum('nhqk,nkhd->nqhd', attn, v).reshape(B, Q, E)
        return out @ Wo.T + bo

    def _L0_ffn_ref(x, router_w, router_b, we_gate, we_up, we_down):
        import jax, jax.numpy as jnp
        import numpy as np
        EMBED = 256
        NUM_EXPERTS = 8
        TOP_K = 2
        x_shape = x.shape
        x_flat = x.reshape(-1, x_shape[-1])
        num_tokens = x_flat.shape[0]
        router_logits = x_flat @ router_w + router_b
        topk_weights, topk_indices = jax.lax.top_k(router_logits, k=TOP_K)
        topk_weights = jax.nn.softmax(topk_weights, axis=-1)
        token_idx_mesh = jnp.repeat(jnp.arange(num_tokens), TOP_K)
        expert_idx_mesh = topk_indices.reshape(-1)
        sort_permutation = jnp.argsort(expert_idx_mesh)
        sorted_expert_idx = expert_idx_mesh[sort_permutation]
        sorted_token_idx = token_idx_mesh[sort_permutation]
        group_sizes = jnp.bincount(sorted_expert_idx, length=NUM_EXPERTS)
        sorted_tokens = x_flat[sorted_token_idx]
        ff_gate = jax.lax.ragged_dot(sorted_tokens, we_gate, group_sizes)
        ff_up = jax.lax.ragged_dot(sorted_tokens, we_up, group_sizes)
        activated = jax.nn.silu(ff_gate) * ff_up
        ff_out = jax.lax.ragged_dot(activated, we_down, group_sizes)
        sorted_weights = topk_weights.reshape(-1)[sort_permutation]
        ff_out = ff_out * sorted_weights[:, None]
        output_flat = jnp.zeros_like(x_flat).at[sorted_token_idx].add(ff_out)
        return output_flat.reshape(x_shape)

    def _L1_xattn_ref(x, context, context_mask, Wq, bq, Wkv, bkv, Wp, bp):
        import jax, jax.numpy as jnp
        import numpy as np
        D_MODEL = 256
        N_HEADS = 16
        HEAD_DIM = D_MODEL // N_HEADS
        B, T, D = x.shape
        S = context.shape[1]
        H, Hd = (N_HEADS, HEAD_DIM)
        q = (x @ Wq + bq).reshape(B, T, H, Hd).transpose(0, 2, 1, 3)
        kv = (context @ Wkv + bkv).reshape(B, S, 2, H, Hd)
        k = kv[:, :, 0].transpose(0, 2, 1, 3)
        v = kv[:, :, 1].transpose(0, 2, 1, 3)
        scores = jnp.einsum('bhtd,bhsd->bhts', q, k) / np.sqrt(Hd)
        neg_inf = jnp.finfo(scores.dtype).min
        scores = jnp.where(context_mask[:, None, None, :], scores, neg_inf)
        attn = jax.nn.softmax(scores, axis=-1)
        out = jnp.einsum('bhts,bhsd->bthd', attn, v).reshape(B, T, D)
        return out @ Wp + bp

    def _L1_ffn_ref(x, Wr, W1, W2):
        import jax, jax.numpy as jnp
        import numpy as np
        N_EXPERTS = 8
        CAP_FACTOR = 1.25
        BATCH, SEQ, DMODEL, DFF = (4, 512, 256, 1024)
        B, S, D = x.shape
        E = W1.shape[0]
        cap = int(CAP_FACTOR * B * S / E)
        t = x.reshape(-1, D)
        probs = jax.nn.softmax(t @ Wr, axis=-1)
        idx = jnp.argmax(probs, axis=-1)
        pmax = jnp.max(probs, axis=-1)
        onehot = jax.nn.one_hot(idx, E, dtype=jnp.int32)
        pos = jnp.sum(jnp.cumsum(onehot, axis=0) * onehot, axis=-1) - 1
        kept = pos < cap
        flat = idx * cap + jnp.minimum(pos, cap - 1)
        disp = jnp.zeros((E * cap, D), t.dtype).at[flat].add(t * kept[:, None].astype(t.dtype))
        ein = disp.reshape(E, cap, D)
        h = jax.nn.relu(jnp.einsum('ecd,edf->ecf', ein, W1))
        eout = jnp.einsum('ecf,efd->ecd', h, W2).reshape(E * cap, D)
        comb = jnp.where(kept[:, None], eout[flat], t)
        factor = jnp.where(kept, pmax, jnp.ones_like(pmax))
        out = (comb * factor[:, None]).reshape(B, S, D)
        return out
    x = x + _L0_xattn_ref(_layernorm(x, axis=-1), ctx_1024, ctx_1024, mask_Bx1xSxS2_ik1, L0_xattn_Wq, L0_xattn_bq, L0_xattn_Wk, L0_xattn_bk, L0_xattn_Wv, L0_xattn_bv, L0_xattn_Wo, L0_xattn_bo)
    x = x + _L0_ffn_ref(_layernorm(x, axis=-1), L0_ffn_router_w, L0_ffn_router_b, L0_ffn_we_gate, L0_ffn_we_up, L0_ffn_we_down)
    x = x + _L1_xattn_ref(_layernorm(x, axis=-1), ctx_1024, mask_BxS2_bf1, L1_xattn_Wq, L1_xattn_bq, L1_xattn_Wkv, L1_xattn_bkv, L1_xattn_Wp, L1_xattn_bp)
    x = x + _L1_ffn_ref(_layernorm(x, axis=-1), L1_ffn_Wr, L1_ffn_W1, L1_ffn_W2)
    return x

_drawn_inputs = setup_inputs


def setup_inputs(seed=0):
    import zlib

    import numpy as np

    out = dict(_drawn_inputs(seed))
    spreads = {'L0_ffn_router_b': (0.0, 0.1),
     'L1_xattn_bq': (0.0, 0.1),
     'L1_xattn_bkv': (0.0, 0.1),
     'L1_xattn_bp': (0.0, 0.1)}
    factors = {'L0_xattn_bk': 8.0, 'L1_ffn_W1': 3.539, 'L1_ffn_W2': 2.953}
    for name, (base, spread) in spreads.items():
        noise = np.random.default_rng([zlib.crc32(name.encode()), seed]).standard_normal(out[name].shape)
        drawn = base * np.exp(spread * noise) if base else spread * noise
        out[name] = jnp.asarray(drawn.astype(out[name].dtype))
    for name, factor in factors.items():
        out[name] = (out[name] * factor).astype(out[name].dtype)
    return out
```

```python
from contextlib import ExitStack

import numpy as np

import concourse.bass as bass
from concourse import mybir

ALU = mybir.AluOpType
ACT = mybir.ActivationFunctionType
AX_X = mybir.AxisListType.X
F32 = mybir.dt.float32
BF16 = mybir.dt.bfloat16
I32 = mybir.dt.int32
U32 = mybir.dt.uint32
U8 = mybir.dt.uint8

P = 128
B, S, D = 8, 256, 256
H, HD = 16, 16
C = D // P
QC = S // P
T = B * S // P
G = 4
HG = H // G
UNITS = G * QC
MAXU = H // 2 * QC
NE = 8
CAP = int(1.25 * B * S / NE)
FF = 1024
TERM = 3
ROW_MASK = 6 * HD
ROW_MAX = ROW_MASK + 1
ROWS = ROW_MAX + TERM
NEG = -float(np.float32(1e20).view(np.uint32) >> 16 << 16 and np.array([int(np.float32(1e20).view(np.uint32)) & 0xFFFF0000], np.uint32).view(np.float32)[0])
EPS = 1e-5
TWO_ONES = float(np.array([0x3F803F80], np.uint32).view(np.float32)[0])
SCALE = (1.0 / D ** 0.5, 1.0 / HD ** 0.5)
SKIP = 1 << 20
ST_CREDIT, PV_CREDIT = 2, 4


class Batch:

    def __init__(self, pair, offset):
        self.pair, self.offset = pair, offset
        self.p = offset % 2
        self.use = pair + offset // 2
        self.n = pair * 2 + offset
        self.tile = None

    def plus(self, k):
        return Batch(self.pair, self.offset + k)


def build(nc, x, ctx_t, mask, mask_t, valid, attn, l0, l1, out):
    stack = ExitStack()
    with stack:
        def sb(name, shape, dt=F32):
            return stack.enter_context(nc.sbuf_tensor(name, shape, dt))

        def sem(name):
            return stack.enter_context(nc.semaphore(name))

        def dram(name, shape, dt):
            return nc.dram_tensor(name, shape, dt, kind="Internal").ap()

        q_parts = dram("q_parts", (2 * B, TERM, D, S), BF16)
        k_parts = dram("k_parts", (2 * B, TERM, D, S), BF16)
        m_parts = dram("m_parts", (2 * B, TERM, H, S), BF16)
        slots_in = dram("slots_in", (NE * CAP, D), F32)
        slots_out = dram("slots_out", (NE * CAP, D), F32)

        xs = sb("xs", [P, T, D])
        xn_all = sb("xn_all", [P, T, D])
        ctxT = sb("ctxT", [P, C, B * S])
        wq = [sb(f"wq{i}", [P, C, D]) for i in range(2)]
        wk = [sb(f"wk{i}", [P, C, D]) for i in range(2)]
        wv = [sb(f"wv{i}", [P, C, D]) for i in range(2)]
        wo = [sb(f"wo{i}", [P, G, D]) for i in range(2)]
        bq = [sb(f"bq{i}", [P, C]) for i in range(2)]
        bk = [sb(f"bk{i}", [P, C]) for i in range(2)]
        bv = [sb(f"bv{i}", [P, D]) for i in range(2)]
        wr = [sb(f"wr{i}", [P, C, NE]) for i in range(2)]
        br = sb("br", [P, NE])
        key_ok = sb("key_ok", [P, B * S], U8)
        all_ok = sb("all_ok", [P, S], U8)
        ok_row = sb("ok_row", [1, B * S], U8)
        ident = sb("ident", [P, P])
        ident16 = sb("ident16", [P, P], BF16)
        below = sb("below", [P, P], BF16)
        ones16 = sb("ones16", [P, P], BF16)
        iota8 = sb("iota8", [P, NE])

        ctxv = sb("ctxv", [P, C, S])
        stats = sb("stats", [P, QC, 6])
        mean_var = sb("mean_var", [P, QC, 2])
        rstd = sb("rstd", [P, QC])
        root = sb("root", [P, 3, QC])
        xn = sb("xn", [P, 2, QC, D])
        xnT = sb("xnT", [P, C, S])
        kf = sb("kf", [P, C, S])
        kr = sb("kr", [P, C, S])
        ks = sb("ks", [P, TERM, C, S], BF16)
        qf = sb("qf", [P, C, S])
        qr = sb("qr", [P, C, S])
        qs = sb("qs", [P, TERM, C, S], BF16)
        qk = sb("qk", [P, 2, 2, H, S], BF16)
        mask_i = sb("mask_i", [P, 2, QC, S], I32)
        neg_row = mask_i[0:1, :, :, :].rearrange("p a c s -> p (a c s)").bitcast(BF16)
        mask_q = sb("mask_q", [P, 2, QC, S], BF16)
        mask_k = sb("mask_k", [P, 2, QC, S], BF16)
        mx = sb("mx", [P, QC, H])
        m_rest = sb("m_rest", [P, QC, H])
        m_split = sb("m_split", [P, QC, TERM, H], BF16)
        m_T = sb("m_T", [TERM * H, S], BF16)
        prob = sb("prob", [P, 4, HG, S])
        v = sb("v", [P, 2, QC, H, 2 * HD])
        oT = sb("oT", [P, S // 32, 32])
        o_inv = sb("o_inv", [P, S // 32])
        osb = sb("osb", [P, G, S])

        ring = sb("ring", [P, 2, 2 * C * FF])
        big = qk[:, :, :, :, :].rearrange("p a b h s -> p (a b h s)").bitcast(F32)
        xnT_all = big[:, 0:C * B * S].rearrange("p (c s) -> p c s", c=C)
        h0 = big[:, 4096:4096 + 2 * C * 512].rearrange("p (r f s) -> p r f s", r=2, f=C)
        silu = big[:, 6144:6144 + 2 * 512].rearrange("p (r s) -> p r s", r=2)
        hT = big[:, 0:FF // P * CAP].rearrange("p (f s) -> p f s", f=FF // P)
        eT = big[:, 2560:2560 + 2 * C * CAP].rearrange("p (r c s) -> p r c s", r=2, c=C)
        erow = big[:, 3840:3840 + 2 * 3 * D].rearrange("p (r a d) -> p r a d", r=2, a=3)
        eo = big[:, 5376:5376 + 2 * 3 * D].rearrange("p (r a d) -> p r a d", r=2, a=3)
        pr = prob[:, :, :, :].rearrange("p a h s -> p (a h s)")
        got = pr[:, 0:8 * D].rearrange("p (r d) -> p r d", r=8)
        fin = pr[:, 8 * D:16 * D].rearrange("p (r d) -> p r d", r=8)
        xnT_tile = sb("xnT_tile", [P, 2, C, P])
        lg = qr[:, :, :].rearrange("p c s -> p (c s)")[:, 0:T * NE].rearrange("p (t e) -> p t e", t=T)
        small = [a[:, :, :].rearrange("p c s -> p (c s)") for a in (kf, kr)]
        table = T * NE
        lgb = small[0][:, 0:table].rearrange("p (t e) -> p t e", t=T)
        top = small[0][:, table:2 * table].rearrange("p (t e) -> p t e", t=T)
        top_i = small[0][:, 2 * table:3 * table].bitcast(U32).rearrange("p (t e) -> p t e", t=T)
        pick = sb("pick", [P, 2, T])
        hot = qf[:, :, :].rearrange("p c s -> p (c s)")[:, 0:2 * table].rearrange("p (r t e) -> p r t e", r=2, t=T)
        hot16 = sb("hot16", [P, T, NE], BF16)
        wts = sb("wts", [P, 4, T])
        gate = sb("gate", [P, 2, T, NE])
        cnt = small[1][:, 0:2 * table].rearrange("p (r t e) -> p r t e", r=2, t=T)
        rank = small[1][:, 2 * table:3 * table].rearrange("p (t e) -> p t e", t=T)
        pos = sb("pos", [P, 4, T])
        slot = sb("slot", [P, 2, T], U32)

        ps = [stack.enter_context(nc.psum_tensor(f"ps{i}", [P, 512], F32)) for i in range(8)]
        misc, pv_bank = ps[7], ps[6]
        mps = [ps[4], ps[5]]

        names = """ones_again settled const_pool ident_done weights_in ctx_in0 ctx_in x_in0 x_in ffn_bias_in valid_in wo_zero
            ones_set neg_done slots_zero
            ln rstd_ready xn_ready xnT_psum xnT_ready k_psum kf_ready ks_act ks_pool k_written
            q_psum qf_ready qs_act qs_pool q_written
            mask_in mask_t_in mask_q_ready mask_k_ready
            ctxv_ready v_psum v_ready
            max_psum mx_done m_chain mT_psum mT_ready m_written
            st_ready exp_done pv_done o_read o_chain o_ready oproj resid
            rt_ln rt_rstd rt_xn rt_T rt_Tcopy rt_Tall rt_lg rt_lgcopy
            route_vec route_act route_pe
            w0_in0 w0_in1 gu_psum silu_done h_done down_psum acc_done
            scattered w1_in0 w1_in1 er_in0 er_in1 eT_psum eT_done hid_psum hid_act hid_vec
            eo_psum eo_done eo_stored0 eo_stored1 x_plus fin_done""".split()
        s = {n: sem(n) for n in names}
        qk_loaded = [[sem(f"qk_loaded{p}{g}") for g in range(G)] for p in range(2)]
        m_loaded = [sem(f"m_loaded{p}") for p in range(2)]
        gathered = [sem(f"gathered{r}") for r in range(8)]
        out_stored = [sem(f"out_stored{r}") for r in range(8)]
        w0_in = [s["w0_in0"], s["w0_in1"]]
        w1_in = [s["w1_in0"], s["w1_in1"]]
        er_in = [s["er_in0"], s["er_in1"]]
        eo_stored = [s["eo_stored0"], s["eo_stored1"]]
        block = stack.enter_context(nc.Block())

        def wait(eng, name, value):
            if not isinstance(value, int) or value > 0:
                eng.wait_ge(s[name] if isinstance(name, str) else name, value)

        def settle(eng):
            eng.sem_inc(s["settled"], 1)

        def qk_value(b, layer):
            return b.use * 96 + 96 if layer == 0 else (b.use - B // 2) * 112 + 96 * (B // 2) + 112

        def batches(eng, layer, prologue, iteration):
            prologue(layer)
            base = layer * B // 2
            with eng.Fori(0, (B - 2) // 2) as i:
                for k in range(2):
                    iteration(layer, Batch(i + base, k), i * 2 + k, True, True)
            iteration(layer, Batch(base, B - 2), B - 2, True, False)
            iteration(layer, Batch(base, B - 1), B - 1, False, False)

        @block.sync
        def _(sp):
            sp.dma_start(ctxT[:, :, 0:2 * S], ctx_t.rearrange("(c p) s -> p c s", p=P)[:, :, 0:2 * S]).then_inc(s["ctx_in0"], 16)
            for t in range(2):
                sp.dma_start(xs[:, t * QC:(t + 1) * QC, :],
                             x[t].rearrange("(t p) d -> p t d", p=P)).then_inc(s["x_in0"], 16)
            sp.dma_start(ctxT[:, :, 2 * S:], ctx_t.rearrange("(c p) s -> p c s", p=P)[:, :, 2 * S:]).then_inc(s["ctx_in"], 16)
            sp.dma_start(xs[:, 2 * QC:, :],
                         x[2:B].rearrange("b (t p) d -> p (b t) d", p=P)).then_inc(s["x_in"], 16)

            def load_mask_q(b, at):
                wait(sp, "mask_q_ready", b.n)
                sp.dma_start(mask_i[:, 0, :, :], mask[at].rearrange("(c p) k -> p c k", p=P)).then_inc(s["mask_in"], 16)

            def load_mask_k(b, at):
                wait(sp, "mask_k_ready", b.n)
                sp.dma_start(mask_i[:, 1, :, :], mask_t[at].rearrange("(c p) q -> p c q", p=P)).then_inc(s["mask_t_in"], 16)

            def write_parts(b):
                sp.wait_ge(s["ks_pool"], b.n * 2 + 2)
                sp.dma_start(k_parts[b.n].rearrange("t (c p) s -> p t c s", p=P), ks[:, :, :, :]).then_inc(s["k_written"], 16)
                sp.wait_ge(s["qs_pool"], b.n * 2 + 2)
                sp.dma_start(q_parts[b.n].rearrange("t (c p) s -> p t c s", p=P), qs[:, :, :, :]).then_inc(s["q_written"], 16)

            def load_groups(b, layer, groups):
                sp.wait_ge(s["k_written"], b.n * 16 + 16)
                sp.wait_ge(s["q_written"], b.n * 16 + 16)
                settle(sp)
                for g in groups:
                    wait(sp, "st_ready", b.n * UNITS - 2 * UNITS + 2 * g + 2)
                    h0_, h1_ = g * HG, (g + 1) * HG
                    for side, parts in ((0, q_parts), (1, k_parts)):
                        src = parts[b.n].rearrange("t (d h) s -> (t d) h s", h=H)
                        for to, n, frm in ((0, 3, 0), (3, 2, side), (5, 1, 2 * side)):
                            sp.dma_start(qk[to * HD:(to + n) * HD, b.p, side, h0_:h1_, :],
                                         src[frm * HD:(frm + n) * HD, h0_:h1_, :]).then_inc(qk_loaded[b.p][g], 16)

            def load_key_mask(b, at, g):
                row = neg_row[0:1, bass.ds(at * S, S)]
                sp.dma_start(qk[ROW_MASK:ROW_MASK + 1, b.p, 1, g * HG:(g + 1) * HG, :],
                             row.rearrange("o (a s) -> o a s", a=1).broadcast_to([1, HG, S])).then_inc(qk_loaded[b.p][g], 16)

            def load_batch(b, at, layer, groups):
                for g in groups:
                    load_groups(b, layer, (g,))
                    if layer == 1:
                        load_key_mask(b, at, g)

            def write_max(b):
                sp.wait_ge(s["mT_ready"], b.n + 1)
                sp.dma_start(m_parts[b.n].rearrange("t h s -> (t h) s"), m_T[:, :]).then_inc(s["m_written"], 16)

            def load_max(b):
                sp.wait_ge(s["m_written"], b.n * 16 + 16)
                wait(sp, "st_ready", b.n * UNITS - UNITS)
                sp.dma_start(qk[ROW_MAX:ROWS, b.p, 0, :, :],
                             m_parts[b.n]).then_inc(m_loaded[b.p], 16)

            def prologue(layer):
                base = layer * B // 2
                b0, b1 = Batch(base, 0), Batch(base, 1)
                if layer == 0:
                    load_mask_q(b0, 0)
                    load_mask_k(b0, 0)
                    load_mask_q(b1, 1)
                    sp.wait_ge(s["ones_set"], 3)
                else:
                    sp.wait_ge(s["acc_done"], FFN0_ACC)
                    sp.wait_ge(s["neg_done"], 1)
                    sp.wait_ge(s["ones_again"], 1)
                write_parts(b0)
                load_batch(b0, 0, layer, range(G))
                write_parts(b1)
                load_batch(b1, 1, layer, range(G))
                write_max(b0)
                load_max(b0)

            def iteration(layer, b, at, more, prep):
                if layer == 0 and prep:
                    load_mask_q(b.plus(2), at + 2)
                if layer == 0 and more:
                    load_mask_k(b.plus(1), at + 1)
                if prep:
                    write_parts(b.plus(2))
                if more:
                    write_max(b.plus(1))
                if prep:
                    load_batch(b.plus(2), at + 2, layer, (0, 1))
                if more:
                    load_max(b.plus(1))
                if prep:
                    load_batch(b.plus(2), at + 2, layer, (2, 3))

            batches(sp, 0, prologue, iteration)

            gate_v = l0["gate"].rearrange("e (c p) f -> e p c f", p=P)
            up_v = l0["up"].rearrange("e (c p) f -> e p c f", p=P)
            down_v = l0["down"].rearrange("e (c p) f -> e p c f", p=P)
            with sp.Fori(0, NE // 2) as i:
                for k in range(2):
                    sp.wait_ge(s["acc_done"], (i * 2 + k) * T - T + ACC_CREDIT)
                    for j, w in enumerate((gate_v, up_v, down_v)):
                        sp.dma_start(ring[:, k, j * 512:(j + 1) * 512].rearrange("p (c f) -> p c f", c=C),
                                     w[i * 2 + k]).then_inc(w0_in[k], 16)

            batches(sp, 1, prologue, iteration)

            w1_v = l1["w1"].rearrange("e (c p) f -> e p c f", p=P)
            w2_v = l1["w2"].rearrange("e (c p) d -> e p c d", p=P)
            with sp.Fori(0, NE // 2) as i:
                for k in range(2):
                    e = i * 2 + k
                    sp.wait_ge(s["eo_done"], e * 3 - 3 + EO_CREDIT)
                    sp.dma_start(ring[:, k, 0:C * FF].rearrange("p (c f) -> p c f", c=C), w1_v[e]).then_inc(w1_in[k], 16)
                    sp.dma_start(ring[:, k, C * FF:].rearrange("p (c d) -> p c d", d=D), w2_v[e]).then_inc(w1_in[k], 16)
                    sp.wait_ge(s["scattered"], 16 * T)
                    rows = slots_in[bass.ds(e * CAP, CAP), :]
                    sp.dma_start(erow[:, k, 0:2, :], rows[0:2 * P, :].rearrange("(a p) d -> p a d", p=P)).then_inc(er_in[k], 16)
                    sp.dma_start(erow[0:CAP - 2 * P, k, 2, :], rows[2 * P:CAP, :]).then_inc(er_in[k], 16)
            for t in range(T):
                sp.wait_ge(s["fin_done"], t + 1)
                sp.dma_start(out[t // QC, (t % QC) * P:(t % QC + 1) * P, :], fin[:, t % 8, :]).then_inc(out_stored[t % 8], 16)
            for r in range(8):
                sp.wait_ge(out_stored[r], 16 * T // 8)

        @block.gpsimd
        def _(pool):
            for m in (ident, ident16):
                pool.memset(m[:, :], 0.0).then_inc(s["const_pool"], 1)
            pool.memset(below[:, :], 1.0).then_inc(s["const_pool"], 1)
            pool.memset(ones16[:, :], 1.0).then_inc(s["const_pool"], 1)
            pool.wait_ge(s["const_pool"], 4)
            for m in (ident, ident16):
                pool.affine_select(out=m[:, :], in_=m[:, :], compare_op=ALU.not_equal, fill=1.0, base=0,
                                   pattern=[[-1, P]], channel_multiplier=1).then_inc(s["ident_done"], 1)
            pool.affine_select(out=below[:, :], in_=below[:, :], compare_op=ALU.is_gt, fill=0.0, base=0,
                               pattern=[[1, P]], channel_multiplier=-1).then_inc(s["ident_done"], 1)
            pool.iota(iota8[:, :], pattern=[[1, NE]], base=0, channel_multiplier=0,
                      allow_small_or_imprecise_dtypes=True).then_inc(s["ident_done"], 1)

            def inverse_root(chain, start):
                var, y, t = root[:, 0, :], root[:, 1, :], root[:, 2, :]
                settle(pool)
                pool.tensor_scalar(var, mean_var[:, :, 1], EPS, None, ALU.add).then_inc(chain, 1)
                pool.wait_ge(chain, start + 1)
                settle(pool)
                pool.tensor_scalar(y.bitcast(I32), var.bitcast(I32), -0.5, float(0x5F3759DF), ALU.mult, ALU.add).then_inc(chain, 1)
                for k in range(ROOT_NEWTON):
                    pool.wait_ge(chain, start + 2 + 4 * k)
                    pool.tensor_tensor(t, y, y, ALU.mult).then_inc(chain, 1)
                    pool.wait_ge(chain, start + 3 + 4 * k)
                    pool.tensor_tensor(t, t, var, ALU.mult).then_inc(chain, 1)
                    pool.wait_ge(chain, start + 4 + 4 * k)
                    settle(pool)
                    pool.tensor_scalar(t, t, -0.5, 1.5, ALU.mult, ALU.add).then_inc(chain, 1)
                    pool.wait_ge(chain, start + 5 + 4 * k)
                    to = rstd[:, :] if k == ROOT_NEWTON - 1 else y
                    pool.tensor_tensor(to, y, t, ALU.mult).then_inc(chain, 1)

            def inv_std(b):
                pool.wait_ge(s["ln"], b.n * 4 + 4)
                inverse_root(s["rstd_ready"], b.n * ROOT_STEPS)

            def k_rest(b):
                pool.wait_ge(s["ks_act"], b.n * 2 + 1)
                pool.tensor_tensor(kr[:, :, :], kf[:, :, :], ks[:, 2, :, :], ALU.subtract).then_inc(s["ks_pool"], 1)
                pool.wait_ge(s["ks_act"], b.n * 2 + 2)
                pool.tensor_tensor(ks[:, 0, :, :], kr[:, :, :], ks[:, 1, :, :], ALU.subtract).then_inc(s["ks_pool"], 1)

            def q_rest(b):
                pool.wait_ge(s["qs_act"], b.n * 2 + 1)
                pool.tensor_tensor(qr[:, :, :], qf[:, :, :], qs[:, 0, :, :], ALU.subtract).then_inc(s["qs_pool"], 1)
                pool.wait_ge(s["qs_act"], b.n * 2 + 2)
                pool.tensor_tensor(qs[:, 2, :, :], qr[:, :, :], qs[:, 1, :, :], ALU.subtract).then_inc(s["qs_pool"], 1)

            def copy_ctx(b, at):
                wait(pool, "v_psum", b.n)
                pool.tensor_copy(ctxv[:, :, :], ctxT[:, :, bass.ds(at * S, S)]).then_inc(s["ctxv_ready"], 1)

            def mask_for_q(b):
                pool.wait_ge(s["mask_in"], b.n * 16 + 16)
                wait(pool, "mx_done", b.n * MAXU - MAXU)
                settle(pool)
                pool.tensor_scalar(mask_q[:, b.p, :, :], mask_i[:, 0, :, :], 0.0, NEG, ALU.is_equal, ALU.mult).then_inc(s["mask_q_ready"], 1)

            def mask_for_k(b):
                pool.wait_ge(s["mask_t_in"], b.n * 16 + 16)
                wait(pool, "st_ready", b.n * UNITS - UNITS)
                settle(pool)
                pool.tensor_scalar(mask_k[:, b.p, :, :], mask_i[:, 1, :, :], 0.0, NEG, ALU.is_equal, ALU.mult).then_inc(s["mask_k_ready"], 1)

            def prologue(layer):
                base = layer * B // 2
                if layer == 1:
                    pool.wait_ge(s["acc_done"], FFN0_ACC)
                    pool.memset(big[ROW_MASK:P, :], TWO_ONES).then_inc(s["ones_again"], 1)
                    pool.wait_ge(s["ones_again"], 1)
                for k in range(2):
                    b = Batch(base, k)
                    if layer == 0:
                        mask_for_q(b)
                        if k == 0:
                            mask_for_k(b)
                    inv_std(b)
                    k_rest(b)
                    q_rest(b)
                    if k == 0:
                        if layer == 0:
                            pool.wait_ge(s["ctx_in0"], 16)
                        copy_ctx(b, 0)
                if layer == 0:
                    pool.wait_ge(s["ctx_in"], 16)

            def iteration(layer, b, at, more, prep):
                if prep:
                    inv_std(b.plus(2))
                    k_rest(b.plus(2))
                if more:
                    copy_ctx(b.plus(1), at + 1)
                if layer == 0 and more:
                    mask_for_k(b.plus(1))
                if layer == 0 and prep:
                    mask_for_q(b.plus(2))
                if prep:
                    q_rest(b.plus(2))

            def route_std():
                with pool.Fori(0, T // 2) as i:
                    pool.wait_ge(s["rt_ln"], i * 4 + 4 + rt["base"] * 2)
                    inverse_root(s["rt_rstd"], (i + rt["base"] // 2) * ROOT_STEPS)
                rt["base"] += T

            rt = {"base": 0}
            batches(pool, 0, prologue, iteration)
            route_std()
            pool.wait_ge(s["valid_in"], 32)
            pool.tensor_scalar(neg_row[:, :], ok_row[:, :], 0.0, NEG, ALU.is_equal, ALU.mult).then_inc(s["neg_done"], 1)
            batches(pool, 1, prologue, iteration)
            route_std()
            pool.wait_ge(s["slots_zero"], 16)
            pool.wait_ge(s["route_vec"], ROUTE1_SLOTS)
            for t in range(T):
                pool.indirect_dma_start(slots_in[:, :], bass.IndirectOffsetOnAxis(ap=slot[:, 0, t:t + 1], axis=0),
                                        xn_all[:, t, :], None, bounds_check=NE * CAP - 1, oob_is_err=False).then_inc(s["scattered"], 16)
            for k in range(2):
                pool.wait_ge(eo_stored[k], 32 * (NE // 2))
            for t in range(T):
                if t >= 8:
                    pool.wait_ge(s["fin_done"], t - 7)
                pool.indirect_dma_start(got[:, t % 8, :], None, slots_out[:, :],
                                        bass.IndirectOffsetOnAxis(ap=slot[:, 1, t:t + 1], axis=0)).then_inc(gathered[t % 8], 16)

        @block.scalar
        def _(act):
            for i in range(2):
                for w, name in ((wk, "wk"), (wq, "wq"), (wv, "wv")):
                    act.dma_start(w[i][:, :, :], attn[i][name].rearrange("(c p) n -> p c n", p=P)).then_inc(s["weights_in"], 16)
                for w, name in ((bk, "bk"), (bq, "bq")):
                    act.dma_start(w[i][:, :], attn[i][name].rearrange("(c p) -> p c", p=P),
                                  allow_slow_non_contiguous=True).then_inc(s["weights_in"], 16)
                act.dma_start(bv[i][:, :], attn[i]["bv"].rearrange("(o n) -> o n", o=1).broadcast_to([P, D])).then_inc(s["weights_in"], 16)
            act.wait_ge(s["wo_zero"], 2)
            for i in range(2):
                wo_v = attn[i]["wo"].rearrange("(g j d) n -> j d g n", g=G, j=HG)
                for j in range(HG):
                    act.dma_start(wo[i][32 * j:32 * j + HD, :, :], wo_v[j]).then_inc(s["weights_in"], 16)
                act.dma_start(wo[i][HD:HD + 1, 0, :], attn[i]["bo"].rearrange("(o n) -> o n", o=1)).then_inc(s["weights_in"], 16)
                act.dma_start(wr[i][:, :, :], (l0, l1)[i]["wr"].rearrange("(c p) n -> p c n", p=P)).then_inc(s["weights_in"], 16)
            act.dma_start(br[:, :], l0["br"].rearrange("(o n) -> o n", o=1).broadcast_to([P, NE])).then_inc(s["weights_in"], 16)
            act.dma_start(key_ok[:, :], valid.rearrange("(o b) s -> o (b s)", o=1).broadcast_to([P, B * S])).then_inc(s["valid_in"], 16)
            act.dma_start(ok_row[:, :], valid.rearrange("(o b) s -> o (b s)", o=1)).then_inc(s["valid_in"], 16)
            act.sem_inc(s["exp_done"], ST_CREDIT)
            act.sem_inc(s["eo_done"], EO_CREDIT)
            act.sem_inc(s["rt_lgcopy"], LG_CREDIT)
            act.wait_ge(s["wo_zero"], 3)
            act.dma_start(slots_in.rearrange("(a p) d -> p a d", p=P), xn_all[:, 0:1, :].broadcast_to([P, NE * CAP // P, D])).then_inc(s["slots_zero"], 16)

            def k_high(b):
                act.wait_ge(s["kf_ready"], b.n * 2 + 2)
                wait(act, "k_written", b.n * 16)
                act.activation(ks[:, 2, :, :], kf[:, :, :], ACT.Copy).then_inc(s["ks_act"], 1)

            def k_mid(b):
                act.wait_ge(s["ks_pool"], b.n * 2 + 1)
                act.activation(ks[:, 1, :, :], kr[:, :, :], ACT.Copy).then_inc(s["ks_act"], 1)

            def q_evac(b, layer):
                act.wait_ge(s["q_psum"], b.n + 1)
                wait(act, "qs_pool", b.n * 2)
                for c in range(C):
                    act.activation(qf[:, c, :], misc[:, c * S:(c + 1) * S], ACT.Identity, bias=bq[layer][:, c:c + 1]).then_inc(s["qf_ready"], 1)

            def q_high(b):
                act.wait_ge(s["qf_ready"], b.n * 2 + 2)
                wait(act, "q_written", b.n * 16)
                act.activation(qs[:, 0, :, :], qf[:, :, :], ACT.Copy).then_inc(s["qs_act"], 1)

            def q_mid(b):
                act.wait_ge(s["qs_pool"], b.n * 2 + 1)
                act.activation(qs[:, 1, :, :], qr[:, :, :], ACT.Copy).then_inc(s["qs_act"], 1)

            def xnT_evac(b):
                act.wait_ge(s["xnT_psum"], b.n + 1)
                wait(act, "q_psum", b.n)
                act.activation(xnT[:, :, :], misc[:, :].rearrange("p (c s) -> p c s", c=C), ACT.Copy).then_inc(s["xnT_ready"], 1)

            def exp(b, u, layer):
                unit = b.n * UNITS + u
                act.wait_ge(s["st_ready"], unit + 1)
                act.wait_ge(s["pv_done"], unit - 3 + PV_CREDIT)
                for half in range(2):
                    ins = act.activation(prob[:, u % 4, 2 * half:2 * half + 2, :],
                                         ps[2 * (u % 2) + half][:, :].rearrange("p (h s) -> p h s", h=2), ACT.Exp, scale=SCALE[layer])
                ins.then_inc(s["exp_done"], 1)

            def prologue(layer):
                for k in range(2):
                    b = Batch(layer * B // 2, k)
                    if layer == 0 and k == 0:
                        act.wait_ge(s["weights_in"], 16 * WEIGHT_LOADS)
                    k_high(b)
                    xnT_evac(b)
                    k_mid(b)
                    q_evac(b, layer)
                    q_high(b)
                    q_mid(b)

            def iteration(layer, b, at, more, prep):
                b2 = b.plus(2)
                exp(b, 0, layer)
                exp(b, 1, layer)
                if prep:
                    k_high(b2)
                    xnT_evac(b2)
                exp(b, 2, layer)
                if prep:
                    k_mid(b2)
                exp(b, 3, layer)
                if prep:
                    q_evac(b2, layer)
                    q_high(b2)
                exp(b, 4, layer)
                if prep:
                    q_mid(b2)
                for u in range(5, UNITS):
                    exp(b, u, layer)

            def route_evac():
                with act.Fori(0, T // 2) as i:
                    for k in range(2):
                        n = i * 2 + k + rt["base"]
                        act.wait_ge(s["rt_T"], n + 1)
                        act.activation(xnT_tile[:, k, :, :], ps[k][:, 0:C * P].rearrange("p (c s) -> p c s", c=C), ACT.Copy).then_inc(s["rt_Tcopy"], 1)
                    for k in range(2):
                        n = i * 2 + k + rt["base"]
                        act.wait_ge(s["rt_lg"], n + 1)
                        act.activation(lg[:, bass.ds(i * 2 + k, 1), :], ps[2 + k][:, 0:NE].rearrange("p (a e) -> p a e", a=1), ACT.Copy).then_inc(s["rt_lgcopy"], 1)
                rt["base"] += T

            rt = {"base": 0}
            batches(act, 0, prologue, iteration)
            route_evac()
            act.wait_ge(s["route_vec"], ROUTE0_DIFF)
            act.activation(wts[:, 1, :], wts[:, 0, :], ACT.Exp).then_inc(s["route_act"], 1)
            with act.Fori(0, NE * T // 4) as i:
                for f in range(C):
                    n = i * C + f
                    act.wait_ge(s["gu_psum"], n + 1)
                    act.wait_ge(s["h_done"], n + GU_CREDIT - 1)
                    act.activation(silu[:, f, :], ps[2 * f][:, :], ACT.Silu).then_inc(s["silu_done"], 1)
            batches(act, 1, prologue, iteration)
            route_evac()
            act.wait_ge(s["route_vec"], ROUTE1_DIFF)
            act.activation(gate[:, 0, :, :], gate[:, 1, :, :], ACT.Exp).then_inc(s["route_act"], 1)
            act.wait_ge(s["route_vec"], ROUTE1_SLOTS)
            with act.Fori(0, NE // 2) as i:
                for k in range(2):
                    e = i * 2 + k
                    act.wait_ge(s["eT_psum"], e + 1)
                    for c in range(C):
                        ins = act.activation(eT[:, k, c, :], ps[c][:, 0:CAP], ACT.Copy)
                    ins.then_inc(s["eT_done"], 1)
                    for f in range(0, FF // P, 2):
                        act.wait_ge(s["hid_psum"], e * (FF // P) + f + 1)
                        act.activation(hT[:, f, :], ps[2][:, 0:CAP], ACT.Relu).then_inc(s["hid_act"], 1)
                    act.wait_ge(eo_stored[k], i * 32)
                    for a in range(3):
                        n = P if a < 2 else CAP - 2 * P
                        act.wait_ge(s["eo_psum"], e * 3 + a + 1)
                        act.activation(eo[0:n, k, a, :], ps[4 + a][0:n, 0:D], ACT.Copy).then_inc(s["eo_done"], 1)
                    act.wait_ge(s["eo_done"], e * 3 + 3 + EO_CREDIT)
                    rows = slots_out[bass.ds(e * CAP, CAP), :]
                    act.dma_start(rows[0:2 * P, :].rearrange("(a p) d -> p a d", p=P), eo[:, k, 0:2, :]).then_inc(eo_stored[k], 16)
                    act.dma_start(rows[2 * P:CAP, :], eo[0:CAP - 2 * P, k, 2, :]).then_inc(eo_stored[k], 16)

        @block.tensor
        def _(pe):
            def k_proj(b, at, layer):
                wait(pe, "resid", b.n - 2)
                wait(pe, "v_ready", b.n - 1)
                for m in range(C):
                    for c in range(C):
                        ins = pe.matmul(misc[:, m * S:(m + 1) * S], wk[layer][:, c, m * P:(m + 1) * P],
                                        ctxT[:, c, bass.ds(at * S, S)], start=(c == 0), stop=(c == C - 1), skip_group_check=True)
                ins.then_inc(s["k_psum"], 1)

            def xn_transpose(b):
                pe.wait_ge(s["xn_ready"], b.n * 2 + 2)
                pe.wait_ge(s["kf_ready"], b.n * 2 + 2)
                for c in range(C):
                    for t in range(QC):
                        ins = pe.transpose(misc[:, c * S + t * P:c * S + (t + 1) * P], xn[:, b.p, t, c * P:(c + 1) * P], ident[:, :])
                ins.then_inc(s["xnT_psum"], 1)

            def q_proj(b, layer):
                pe.wait_ge(s["xnT_ready"], b.n + 1)
                for m in range(C):
                    for c in range(C):
                        ins = pe.matmul(misc[:, m * S:(m + 1) * S], wq[layer][:, c, m * P:(m + 1) * P],
                                        xnT[:, c, :], start=(c == 0), stop=(c == C - 1), skip_group_check=True)
                ins.then_inc(s["q_psum"], 1)

            def v_proj(b, layer):
                pe.wait_ge(s["ctxv_ready"], b.n + 1)
                pe.wait_ge(s["mT_ready"], b.n + 1)
                for t in range(QC):
                    for c in range(C):
                        ins = pe.matmul(misc[:, t * D:(t + 1) * D], ctxv[:, c, t * P:(t + 1) * P], wv[layer][:, c, :],
                                        start=(c == 0), stop=(c == C - 1), skip_group_check=True)
                ins.then_inc(s["v_psum"], 1)

            def max_pass(b, g, layer):
                pe.wait_ge(qk_loaded[b.p][g], qk_value(b, layer))
                if layer == 0 and g == 0:
                    pe.wait_ge(s["mask_q_ready"], b.n + 1)
                for k in range(4):
                    pair, c = k // 2, k % 2
                    unit = b.n * MAXU + 4 * g + k
                    wait(pe, "mx_done", unit - 1)
                    bank = mps[k % 2]
                    for j in range(2):
                        h = g * HG + 2 * pair + j
                        ins = pe.matmul(bank[:, j * S:(j + 1) * S], qk[0:ROW_MASK + 1, b.p, 0, h, c * P:(c + 1) * P],
                                        qk[0:ROW_MASK + 1, b.p, 1, h, :], start=(j == 0), stop=(layer == 1), skip_group_check=True)
                    if layer == 0:
                        ins = pe.matmul(bank[:, :].rearrange("p (h s) -> p h s", h=2), ident16[:, :],
                                        mask_q[:, b.p, c:c + 1, :].broadcast_to([P, 2, S]), start=False, stop=True, skip_group_check=True)
                    ins.then_inc(s["max_psum"], 1)

            def max_transpose(b):
                pe.wait_ge(s["m_chain"], b.n * 4 + 4)
                wait(pe, "qf_ready", b.n * 2 + 2)
                settle(pe)
                for c in range(QC):
                    ins = pe.transpose(misc[0:TERM * H, :].bitcast(BF16)[:, c * P:(c + 1) * P],
                                       m_split[:, c, :, :].rearrange("p t h -> p (t h)"), ident16[:, :])
                ins.then_inc(s["mT_psum"], 1)

            def scores(b, u, layer):
                g, c = u // QC, u % QC
                if u == 0:
                    pe.wait_ge(m_loaded[b.p], b.use * 16 + 16)
                    if layer == 0:
                        pe.wait_ge(s["mask_k_ready"], b.n + 1)
                pe.wait_ge(s["exp_done"], b.n * UNITS + u - 1 + ST_CREDIT)
                for half in range(2):
                    bank = ps[2 * (u % 2) + half]
                    for j in range(2):
                        h = g * HG + 2 * half + j
                        ins = pe.matmul(bank[:, j * S:(j + 1) * S], qk[0:ROWS, b.p, 1, h, c * P:(c + 1) * P],
                                        qk[0:ROWS, b.p, 0, h, :], start=(j == 0), stop=(layer == 1), skip_group_check=True)
                    if layer == 0:
                        ins = pe.matmul(bank[:, :].rearrange("p (h s) -> p h s", h=2), ident16[:, :],
                                        mask_k[:, b.p, c:c + 1, :].broadcast_to([P, 2, S]), start=False, stop=True, skip_group_check=True)
                ins.then_inc(s["st_ready"], 1)

            def values(b, u):
                g, c = u // QC, u % QC
                if u == 0:
                    pe.wait_ge(s["v_ready"], b.n + 1)
                pe.wait_ge(s["exp_done"], b.n * UNITS + u + 1 + ST_CREDIT)
                if c == 0:
                    pe.wait_ge(s["o_read"], b.n * G + g)
                for j in range(HG):
                    ins = pe.matmul(pv_bank[32 * j:32 * j + 32, 0:S], v[:, b.p, c, g * HG + j, :],
                                    prob[:, u % 4, j, :], start=(c == 0), stop=(c == QC - 1), tile_position=(0, 32 * j), skip_group_check=True)
                ins.then_inc(s["pv_done"], 1)

            def o_proj(b, layer):
                pe.wait_ge(s["o_ready"], b.n * G + G)
                for t in range(QC):
                    for g in range(G):
                        ins = pe.matmul(misc[:, t * D:(t + 1) * D], osb[:, g, t * P:(t + 1) * P], wo[layer][:, g, :],
                                        start=(g == 0), stop=(g == G - 1), skip_group_check=True)
                ins.then_inc(s["oproj"], 1)

            def prologue(layer):
                base = layer * B // 2
                if layer == 0:
                    pe.wait_ge(s["ident_done"], 4)
                    pe.wait_ge(s["weights_in"], 16 * WEIGHT_LOADS)
                    pe.wait_ge(s["ctx_in0"], 16)
                else:
                    pe.wait_ge(s["acc_done"], FFN0_ACC)
                for k in range(2):
                    b = Batch(base, k)
                    if k == 1:
                        pe.wait_ge(s["qf_ready"], b.n * 2)
                    k_proj(b, k, layer) if k == 0 else k_again(b, k, layer)
                    xn_transpose(b)
                    q_proj(b, layer)
                b = Batch(base, 0)
                for g in range(G):
                    max_pass(b, g, layer)
                pe.wait_ge(s["qf_ready"], b.n * 2 + 4)
                max_transpose(b)
                v_proj(b, layer)
                if layer == 0:
                    pe.wait_ge(s["ctx_in"], 16)

            def k_again(b, at, layer):
                for m in range(C):
                    for c in range(C):
                        ins = pe.matmul(misc[:, m * S:(m + 1) * S], wk[layer][:, c, m * P:(m + 1) * P],
                                        ctxT[:, c, at * S:(at + 1) * S], start=(c == 0), stop=(c == C - 1), skip_group_check=True)
                ins.then_inc(s["k_psum"], 1)

            def iteration(layer, b, at, more, prep):
                b1, b2 = b.plus(1), b.plus(2)
                for u in range(UNITS):
                    scores(b, u, layer)
                    if more and u < G:
                        max_pass(b1, u, layer)
                    if u > 0:
                        values(b, u - 1)
                    if prep and u == 0:
                        k_proj(b2, at + 2, layer)
                    if prep and u == 1:
                        xn_transpose(b2)
                    if prep and u == 2:
                        q_proj(b2, layer)
                    if more and u == 5:
                        if prep:
                            pe.wait_ge(s["qf_ready"], b2.n * 2 + 2)
                        else:
                            pe.wait_ge(s["resid"], b.n)
                            pe.wait_ge(s["v_ready"], b.n + 1)
                        max_transpose(b1)
                if more:
                    v_proj(b1, layer)
                values(b, UNITS - 1)
                if more:
                    pe.wait_ge(s["v_ready"], b.n + 2)
                else:
                    pe.wait_ge(s["resid"], b.n)
                o_proj(b, layer)

            def route(layer):
                pe.wait_ge(s["resid"], (layer + 1) * B)
                with pe.Fori(0, T // 2) as i:
                    for k in range(2):
                        n = i * 2 + k + layer * T
                        pe.wait_ge(s["rt_xn"], n + 1)
                        if layer == 0:
                            pe.wait_ge(s["rt_Tall"], n + 1)
                        else:
                            pe.wait_ge(s["rt_Tcopy"], n - 1)
                        for c in range(C):
                            ins = pe.transpose(ps[k][:, c * P:(c + 1) * P], route_in[:, k, c * P:(c + 1) * P], ident[:, :])
                        ins.then_inc(s["rt_T"], 1)
                    for k in range(2):
                        n = i * 2 + k + layer * T
                        pe.wait_ge(s["rt_Tcopy"], n + 1)
                        pe.wait_ge(s["rt_lgcopy"], n - 1 + LG_CREDIT)
                        for c in range(C):
                            ins = pe.matmul(ps[2 + k][:, 0:NE], xnT_tile[:, k, c, :], wr[layer][:, c, :],
                                            start=(c == 0), stop=(c == C - 1), skip_group_check=True)
                        ins.then_inc(s["rt_lg"], 1)

            route_in = xn[:, 0, :, :]
            pe.sem_inc(s["pv_done"], PV_CREDIT)
            batches(pe, 0, prologue, iteration)
            route(0)
            pe.wait_ge(s["rt_Tall"], T + 2)
            pe.wait_ge(s["rt_lgcopy"], T + LG_CREDIT)

            def gate_up(i, k, blk, f):
                for j in range(2):
                    for c in range(C):
                        base = j * 512 + c * D + f * P
                        ins = pe.matmul(ps[2 * f + j][:, :], ring[:, k, base:base + P], xnT_all[:, c, blk * 512:(blk + 1) * 512],
                                        start=(c == 0), stop=(c == C - 1), skip_group_check=True)
                ins.then_inc(s["gu_psum"], 1)

            def down(n, k, r):
                pe.wait_ge(s["h_done"], n * C + C + GU_CREDIT)
                for t in range(4):
                    pe.wait_ge(s["acc_done"], n * 4 + t - 3 + ACC_CREDIT)
                    for f in range(C):
                        base = 2 * 512 + f * D
                        ins = pe.matmul(ps[4 + t][:, 0:D], h0[:, r, f, t * P:(t + 1) * P],
                                        ring[:, k, base:base + D], start=(f == 0), stop=(f == C - 1), skip_group_check=True)
                    ins.then_inc(s["down_psum"], 1)

            with pe.Fori(0, NE // 2) as i:
                for k in range(2):
                    pe.wait_ge(w0_in[k], i * 48 + 48)
                    for blk in range(4):
                        n = (i * 2 + k) * 4 + blk
                        for f in range(C):
                            pe.wait_ge(s["h_done"], n * C + f - 1 + GU_CREDIT)
                            gate_up(i, k, blk, f)
                        if blk > 0:
                            down(n - 1, k, (blk - 1) % 2)
                    down((i * 2 + k) * 4 + 3, k, 1)

            batches(pe, 1, prologue, iteration)
            route(1)
            pe.wait_ge(s["route_vec"], ROUTE1_HOT)
            hot_v = hot16[:, :, :].rearrange("p t e -> p (t e)")
            pe.matmul(ps[4][:, 0:T * NE], below[:, :], hot_v, start=True, stop=True)
            pe.matmul(ps[5][:, 0:T * NE], ones16[:, :], hot_v, start=True, stop=True).then_inc(s["route_pe"], 1)
            pe.wait_ge(s["route_vec"], ROUTE1_SLOTS)
            pe.wait_ge(s["rt_lgcopy"], 2 * T + LG_CREDIT)
            with pe.Fori(0, NE // 2) as i:
                for k in range(2):
                    e = i * 2 + k
                    pe.wait_ge(er_in[k], i * 32 + 32)
                    pe.wait_ge(s["eT_done"], e)
                    for c in range(C):
                        for a in range(3):
                            n = P if a < 2 else CAP - 2 * P
                            ins = pe.transpose(ps[c][:, a * P:a * P + n], erow[0:n, k, a, c * P:(c + 1) * P], ident[0:n, 0:n])
                    ins.then_inc(s["eT_psum"], 1)
                    pe.wait_ge(w1_in[k], i * 32 + 32)
                    pe.wait_ge(s["eT_done"], e + 1)
                    for f in range(FF // P):
                        if f % 2 == 0:
                            pe.wait_ge(s["hid_act"], e * (FF // P // 2) + f // 2)
                        else:
                            pe.wait_ge(s["hid_vec"], e * (FF // P // 2) + f // 2)
                        for c in range(C):
                            ins = pe.matmul(ps[2 + f % 2][:, 0:CAP], ring[:, k, c * FF + f * P:c * FF + (f + 1) * P],
                                            eT[:, k, c, :], start=(c == 0), stop=(c == C - 1))
                        ins.then_inc(s["hid_psum"], 1)
                    pe.wait_ge(s["hid_act"], e * (FF // P // 2) + FF // P // 2)
                    pe.wait_ge(s["hid_vec"], e * (FF // P // 2) + FF // P // 2)
                    for a in range(3):
                        n = P if a < 2 else CAP - 2 * P
                        pe.wait_ge(s["eo_done"], e * 3 + a - 2 + EO_CREDIT)
                        for f in range(FF // P):
                            ins = pe.matmul(ps[4 + a][0:n, 0:D], hT[:, f, a * P:a * P + n],
                                            ring[:, k, C * FF + f * D:C * FF + (f + 1) * D],
                                            start=(f == 0), stop=(f == FF // P - 1))
                        ins.then_inc(s["eo_psum"], 1)

        @block.vector
        def _(dve):
            dve.memset(qk[ROW_MASK:P, :, :, :, :], 1.0).then_inc(s["ones_set"], 1)
            dve.memset(v[:, :, :, :, HD:2 * HD], 1.0).then_inc(s["ones_set"], 1)
            dve.wait_ge(s["ones_set"], 1)
            dve.memset(qk[ROW_MASK:ROW_MASK + 1, :, 1, :, :], 0.0).then_inc(s["ones_set"], 1)
            for i in range(2):
                dve.memset(wo[i][:, :, :], 0.0).then_inc(s["wo_zero"], 1)
            dve.memset(xn_all[:, 0, :], 0.0).then_inc(s["wo_zero"], 1)
            dve.memset(all_ok[:, :], 1).then_inc(s["ones_set"], 1)

            def norm_stats(b, at):
                for t in range(QC):
                    dve.bn_stats(stats[:, t, :], xs[:, bass.ds(at * QC + t, 1), :].rearrange("p a d -> p (a d)")).then_inc(s["ln"], 1)
                dve.wait_ge(s["ln"], b.n * 4 + 2)
                settle(dve)
                for t in range(QC):
                    dve.bn_aggr(mean_var[:, t, :], stats[:, t, :]).then_inc(s["ln"], 1)

            def norm_apply(b, at):
                dve.wait_ge(s["rstd_ready"], (b.n + 1) * ROOT_STEPS)
                wait(dve, "xnT_psum", b.n - 1)
                for t in range(QC):
                    dve.tensor_scalar(xn[:, b.p, t, :], xs[:, bass.ds(at * QC + t, 1), :].rearrange("p a d -> p (a d)"),
                                      mean_var[:, t, 0:1], rstd[:, t:t + 1], ALU.subtract, ALU.mult).then_inc(s["xn_ready"], 1)

            def k_evac(b, at, layer):
                dve.wait_ge(s["k_psum"], b.n + 1)
                wait(dve, "ks_pool", b.n * 2)
                ok = all_ok[:, :] if layer == 0 else key_ok[:, bass.ds(at * S, S)]
                for c in range(C):
                    dve.scalar_tensor_tensor(out=kf[:, c, :], in0=misc[:, c * S:(c + 1) * S], scalar=bk[layer][:, c:c + 1], in1=ok,
                                             op0=ALU.add, op1=ALU.mult).then_inc(s["kf_ready"], 1)

            def v_evac(b, layer):
                dve.wait_ge(s["v_psum"], b.n + 1)
                dve.tensor_tensor(v[:, b.p, :, :, 0:HD], misc[:, :].rearrange("p (t h d) -> p t h d", t=QC, h=H),
                                  bv[layer][:, :].rearrange("p (o h d) -> p o h d", o=1, h=H).broadcast_to([P, QC, H, HD]), ALU.add).then_inc(s["v_ready"], 1)

            def reduce_max(b, g):
                for k in range(4):
                    pair, c = 2 * g + k // 2, k % 2
                    dve.wait_ge(s["max_psum"], b.n * MAXU + 4 * g + k + 1)
                    dve.tensor_reduce(mx[:, c, 2 * pair:2 * pair + 2], mps[k % 2][:, :].rearrange("p (h s) -> p h s", h=2),
                                      AX_X, ALU.max).then_inc(s["mx_done"], 1)

            def split_max(b):
                dve.wait_ge(s["mx_done"], b.n * MAXU + MAXU)
                wait(dve, "mT_psum", b.n)
                dve.tensor_scalar(m_split[:, :, 0, :], mx[:, :, :], -1.0, None, ALU.mult).then_inc(s["m_chain"], 1)
                dve.wait_ge(s["m_chain"], b.n * 4 + 1)
                dve.scalar_tensor_tensor(out=m_rest[:, :, :], in0=mx[:, :, :], scalar=-1.0, in1=m_split[:, :, 0, :],
                                         op0=ALU.mult, op1=ALU.subtract).then_inc(s["m_chain"], 1)
                dve.wait_ge(s["m_chain"], b.n * 4 + 2)
                dve.tensor_copy(m_split[:, :, 1, :], m_rest[:, :, :]).then_inc(s["m_chain"], 1)
                dve.wait_ge(s["m_chain"], b.n * 4 + 3)
                dve.tensor_tensor(m_split[:, :, 2, :], m_rest[:, :, :], m_split[:, :, 1, :], ALU.subtract).then_inc(s["m_chain"], 1)

            def max_evac(b):
                dve.wait_ge(s["mT_psum"], b.n + 1)
                wait(dve, "m_written", b.n * 16)
                dve.tensor_copy(m_T[:, :], misc[0:TERM * H, :].bitcast(BF16)[:, 0:S]).then_inc(s["mT_ready"], 1)

            def normalise(b, g):
                dve.wait_ge(s["pv_done"], b.n * UNITS + 2 * g + 2 + PV_CREDIT)
                dve.wait_ge(s["o_ready"], b.n * G + g)
                dve.transpose(oT[:, :, :].rearrange("p a r -> p (a r)"), pv_bank[:, 0:S]).then_inc(s["o_read"], 1)
                dve.wait_ge(s["o_read"], b.n * G + g + 1)
                dve.reciprocal(o_inv[:, :], oT[:, :, HD]).then_inc(s["o_chain"], 1)
                dve.wait_ge(s["o_chain"], b.n * 2 * G + 2 * g + 1)
                dve.tensor_tensor(oT[:, :, :], oT[:, :, :], o_inv[:, :].rearrange("p (a o) -> p a o", o=1).broadcast_to([P, S // 32, 32]), ALU.mult).then_inc(s["o_chain"], 1)
                dve.wait_ge(s["o_chain"], b.n * 2 * G + 2 * g + 2)
                if g == 0:
                    wait(dve, "oproj", b.n)
                dve.transpose(osb[:, g, :], oT[:, :, :].rearrange("p a r -> p (a r)")).then_inc(s["o_ready"], 1)

            def residual(b, at):
                dve.wait_ge(s["oproj"], b.n + 1)
                xv = xs[:, bass.ds(at * QC, QC), :]
                dve.tensor_tensor(xv, misc[:, :].rearrange("p (t d) -> p t d", t=QC), xv, ALU.add).then_inc(s["resid"], 1)

            def prologue(layer):
                base = layer * B // 2
                if layer == 0:
                    dve.wait_ge(s["x_in0"], 32)
                    dve.wait_ge(s["ones_set"], 4)
                    dve.wait_ge(s["weights_in"], 16 * WEIGHT_LOADS)
                else:
                    dve.wait_ge(s["acc_done"], FFN0_ACC)
                    dve.wait_ge(s["valid_in"], 32)
                for k in range(2):
                    b = Batch(base, k)
                    norm_stats(b, k)
                    norm_apply(b, k)
                    k_evac(b, k, layer)
                b = Batch(base, 0)
                for g in range(G):
                    reduce_max(b, g)
                split_max(b)
                max_evac(b)
                v_evac(b, layer)
                if layer == 0:
                    dve.wait_ge(s["x_in"], 16)

            def iteration(layer, b, at, more, prep):
                b1, b2 = b.plus(1), b.plus(2)
                if more:
                    reduce_max(b1, 0)
                if prep:
                    norm_stats(b2, at + 2)
                    k_evac(b2, at + 2, layer)
                    norm_apply(b2, at + 2)
                if more:
                    reduce_max(b1, 1)
                    reduce_max(b1, 2)
                normalise(b, 0)
                if more:
                    reduce_max(b1, 3)
                    split_max(b1)
                normalise(b, 1)
                if more:
                    max_evac(b1)
                normalise(b, 2)
                if more:
                    v_evac(b1, layer)
                normalise(b, 3)
                residual(b, at)

            def route(layer):
                dve.wait_ge(s["resid"], (layer + 1) * B)
                if layer == 1:
                    dve.wait_ge(s["slots_zero"], 16)
                with dve.Fori(0, T // 2) as i:
                    n = i + layer * (T // 2)
                    for k in range(2):
                        dve.bn_stats(stats[:, k, :], xs[:, bass.ds(i * 2 + k, 1), :].rearrange("p a d -> p (a d)")).then_inc(s["rt_ln"], 1)
                    dve.wait_ge(s["rt_ln"], n * 4 + 2)
                    settle(dve)
                    for k in range(2):
                        dve.bn_aggr(mean_var[:, k, :], stats[:, k, :]).then_inc(s["rt_ln"], 1)
                    dve.wait_ge(s["rt_rstd"], (n + 1) * ROOT_STEPS)
                    dve.wait_ge(s["rt_T"], n * 2)
                    for k in range(2):
                        dve.tensor_scalar(xn[:, 0, k, :], xs[:, bass.ds(i * 2 + k, 1), :].rearrange("p a d -> p (a d)"),
                                          mean_var[:, k, 0:1], rstd[:, k:k + 1], ALU.subtract, ALU.mult).then_inc(s["rt_xn"], 1)
                    if layer == 0:
                        for k in range(2):
                            dve.wait_ge(s["rt_Tcopy"], i * 2 + k + 1)
                            dve.tensor_copy(xnT_all[:, :, bass.ds((i * 2 + k) * P, P)], xnT_tile[:, k, :, :]).then_inc(s["rt_Tall"], 1)
                    else:
                        dve.wait_ge(s["rt_xn"], n * 2 + 2)
                        dve.tensor_copy(xn_all[:, bass.ds(i * 2, 2), :], xn[:, 0, :, :]).then_inc(s["x_plus"], 1)
                dve.wait_ge(s["rt_lgcopy"], (layer + 1) * T + LG_CREDIT)

            route_count = [0]

            def link(ins):
                ins.then_inc(s["route_vec"], 1)
                route_count[0] += 1
                dve.wait_ge(s["route_vec"], route_count[0])

            def bc(a):
                return a.rearrange("p (t o) -> p t o", o=1).broadcast_to([P, T, NE])

            def per_e(a):
                return a.rearrange("p (o e) -> p o e", o=1).broadcast_to([P, T, NE])

            dve.sem_inc(s["rt_Tall"], 2)
            batches(dve, 0, prologue, iteration)
            route(0)
            link(dve.tensor_tensor(lgb[:, :, :], lg[:, :, :], per_e(br[:, :]), ALU.add))
            for t in range(T):
                ins = dve.max(top[:, t, :], lgb[:, t, :])
            link(ins)
            for t in range(T):
                ins = dve.max_index(top_i[:, t, :], top[:, t, :], lgb[:, t, :])
            link(ins)
            for k in range(2):
                link(dve.tensor_copy(pick[:, k, :], top_i[:, :, k]))
                link(dve.tensor_tensor(hot[:, k, :, :], per_e(iota8[:, :]), bc(pick[:, k, :]), ALU.is_equal))
            link(dve.tensor_tensor(wts[:, 0, :], top[:, :, 1], top[:, :, 0], ALU.subtract))
            assert route_count[0] == ROUTE0_DIFF
            dve.wait_ge(s["route_act"], 1)
            link(dve.tensor_scalar(wts[:, 2, :], wts[:, 1, :], 1.0, None, ALU.add))
            link(dve.reciprocal(wts[:, 3, :], wts[:, 2, :]))
            link(dve.tensor_tensor(wts[:, 2, :], wts[:, 1, :], wts[:, 3, :], ALU.mult))
            link(dve.tensor_tensor(gate[:, 0, :, :], hot[:, 0, :, :], bc(wts[:, 3, :]), ALU.mult))
            link(dve.tensor_tensor(gate[:, 1, :, :], hot[:, 1, :, :], bc(wts[:, 2, :]), ALU.mult))
            link(dve.tensor_tensor(gate[:, 0, :, :], gate[:, 0, :, :], gate[:, 1, :, :], ALU.add))

            def add_down(n, e, blk):
                for t in range(4):
                    tile = blk * 4 + t
                    dve.wait_ge(s["down_psum"], n * 4 + t + 1)
                    dve.wait_ge(s["acc_done"], n * 4 + t - T + ACC_CREDIT + 1)
                    dve.scalar_tensor_tensor(out=xs[:, tile, :], in0=ps[4 + t][:, 0:D],
                                             scalar=gate[:, 0, tile, bass.ds(e, 1)], in1=xs[:, tile, :], op0=ALU.mult, op1=ALU.add).then_inc(s["acc_done"], 1)

            dve.sem_inc(s["acc_done"], ACC_CREDIT)
            dve.sem_inc(s["h_done"], GU_CREDIT)
            with dve.Fori(0, NE // 2) as i:
                for k in range(2):
                    for blk in range(4):
                        n = (i * 2 + k) * 4 + blk
                        for f in range(C):
                            dve.wait_ge(s["silu_done"], n * C + f + 1)
                            dve.tensor_tensor(h0[:, blk % 2, f, :], silu[:, f, :], ps[2 * f + 1][:, :], ALU.mult).then_inc(s["h_done"], 1)
                        if blk > 0:
                            add_down(n - 1, i * 2 + k, blk - 1)
                    add_down((i * 2 + k) * 4 + 3, i * 2 + k, 3)

            batches(dve, 1, prologue, iteration)
            route(1)
            for t in range(T):
                ins = dve.max(top[:, t, :], lg[:, t, :])
            link(ins)
            for t in range(T):
                ins = dve.max_index(top_i[:, t, :], top[:, t, :], lg[:, t, :])
            link(ins)
            link(dve.tensor_copy(pick[:, 0, :], top_i[:, :, 0]))
            link(dve.tensor_tensor(hot[:, 0, :, :], per_e(iota8[:, :]), bc(pick[:, 0, :]), ALU.is_equal))
            link(dve.tensor_copy(hot16[:, :, :], hot[:, 0, :, :]))
            assert route_count[0] == ROUTE1_HOT
            link(dve.tensor_tensor(gate[:, 1, :, :], lg[:, :, :], top[:, :, 0:1].broadcast_to([P, T, NE]), ALU.subtract))
            assert route_count[0] == ROUTE1_DIFF
            dve.wait_ge(s["route_act"], 2)
            link(dve.tensor_reduce(wts[:, 0, :], gate[:, 0, :, :], AX_X, ALU.add))
            link(dve.reciprocal(wts[:, 1, :], wts[:, 0, :]))
            dve.wait_ge(s["route_pe"], 1)
            link(dve.tensor_copy(cnt[:, 0, :, :], ps[5][:, 0:T * NE].rearrange("p (t e) -> p t e", t=T)))
            cur = 0
            step = 1
            while step < T:
                link(dve.tensor_tensor(cnt[:, 1 - cur, step:T, :], cnt[:, cur, step:T, :], cnt[:, cur, 0:T - step, :], ALU.add))
                link(dve.tensor_copy(cnt[:, 1 - cur, 0:step, :], cnt[:, cur, 0:step, :]))
                cur, step = 1 - cur, step * 2
            link(dve.tensor_tensor(rank[:, :, :], cnt[:, cur, :, :], ps[5][:, 0:T * NE].rearrange("p (t e) -> p t e", t=T), ALU.subtract))
            link(dve.tensor_tensor(rank[:, :, :], rank[:, :, :], ps[4][:, 0:T * NE].rearrange("p (t e) -> p t e", t=T), ALU.add))
            link(dve.tensor_tensor(rank[:, :, :], rank[:, :, :], hot[:, 0, :, :], ALU.mult))
            link(dve.tensor_reduce(pos[:, 0, :], rank[:, :, :], AX_X, ALU.add))
            link(dve.tensor_scalar(pos[:, 1, :], pos[:, 0, :], float(CAP), None, ALU.is_lt))
            link(dve.tensor_scalar(pos[:, 2, :], pos[:, 0, :], float(CAP - 1), None, ALU.min))
            link(dve.scalar_tensor_tensor(out=pos[:, 2, :], in0=pick[:, 0, :], scalar=float(CAP), in1=pos[:, 2, :], op0=ALU.mult, op1=ALU.add))
            link(dve.tensor_scalar(pos[:, 3, :], pos[:, 1, :], -float(SKIP), float(SKIP), ALU.mult, ALU.add))
            link(dve.tensor_tensor(pos[:, 3, :], pos[:, 3, :], pos[:, 2, :], ALU.add))
            link(dve.tensor_copy(slot[:, 1, :], pos[:, 2, :]))
            link(dve.tensor_copy(slot[:, 0, :], pos[:, 3, :]))
            assert route_count[0] == ROUTE1_SLOTS
            link(dve.tensor_tensor(wts[:, 2, :], wts[:, 1, :], pos[:, 1, :], ALU.mult))
            link(dve.tensor_scalar(wts[:, 3, :], pos[:, 1, :], -1.0, 1.0, ALU.mult, ALU.add))

            def plain_rows(a, z):
                for t in range(a, z):
                    dve.scalar_tensor_tensor(out=xs[:, t, :], in0=xn_all[:, t, :], scalar=wts[:, 3, t:t + 1], in1=xs[:, t, :],
                                             op0=ALU.mult, op1=ALU.add).then_inc(s["x_plus"], 1)

            dve.wait_ge(s["x_plus"], T // 2)
            with dve.Fori(0, NE // 2) as i:
                for k in range(2):
                    e = i * 2 + k
                    for f in range(1, FF // P, 2):
                        dve.wait_ge(s["hid_psum"], e * (FF // P) + f + 1)
                        dve.tensor_scalar(hT[:, f, :], ps[3][:, 0:CAP], 0.0, None, ALU.max).then_inc(s["hid_vec"], 1)
            plain_rows(0, T)
            dve.wait_ge(s["x_plus"], T // 2 + T)
            for t in range(T):
                dve.wait_ge(gathered[t % 8], 16 * (t // 8 + 1))
                if t >= 8:
                    dve.wait_ge(out_stored[t % 8], 16 * (t // 8))
                dve.scalar_tensor_tensor(out=fin[:, t % 8, :], in0=got[:, t % 8, :], scalar=wts[:, 2, t:t + 1], in1=xs[:, t, :],
                                         op0=ALU.mult, op1=ALU.add).then_inc(s["fin_done"], 1)


WEIGHT_LOADS = 2 * 6 + 2 * 6 + 1
ROOT_NEWTON = 3
ROOT_STEPS = 2 + 4 * ROOT_NEWTON
GU_CREDIT, ACC_CREDIT, EO_CREDIT, LG_CREDIT = 2, 16, 3, 2
FFN0_ACC = ACC_CREDIT + NE * T
ROUTE0_DIFF = 8
ROUTE1_HOT = ROUTE0_DIFF + 6 + 5
ROUTE1_DIFF = ROUTE1_HOT + 1
ROUTE1_SLOTS = ROUTE1_DIFF + 3 + 8 + 4 + 7


def _by_channel(w):
    return w.reshape(w.shape[:-1] + (H, HD)).swapaxes(-1, -2).reshape(w.shape)


def kernel(**inputs):
    import concourse.bacc as _bacc
    from concourse.bass_utils import run_bass_kernel_spmd as _run

    nc = _bacc.Bacc("TRN2", target_bir_lowering=False, num_devices=1)
    a = {k: np.asarray(v) for k, v in inputs.items()}
    wkv, bkv = a["L1_xattn_Wkv"], a["L1_xattn_bkv"]
    lay = {
        "x": a["x"], "ctx_t": a["ctx_1024"].reshape(B * S, D).T,
        "mask": a["mask_Bx1xSxS2_ik1"][:, 0], "mask_t": a["mask_Bx1xSxS2_ik1"][:, 0].swapaxes(1, 2),
        "valid": a["mask_BxS2_bf1"],
        "wq0": _by_channel(a["L0_xattn_Wq"].T), "bq0": _by_channel(a["L0_xattn_bq"]),
        "wk0": _by_channel(a["L0_xattn_Wk"].T), "bk0": _by_channel(a["L0_xattn_bk"]),
        "wv0": a["L0_xattn_Wv"].T, "bv0": a["L0_xattn_bv"], "wo0": a["L0_xattn_Wo"].T, "bo0": a["L0_xattn_bo"],
        "wq1": _by_channel(a["L1_xattn_Wq"]), "bq1": _by_channel(a["L1_xattn_bq"]),
        "wk1": _by_channel(wkv[:, :D]), "bk1": _by_channel(bkv[:D]),
        "wv1": wkv[:, D:], "bv1": bkv[D:], "wo1": a["L1_xattn_Wp"], "bo1": a["L1_xattn_bp"],
        "wr0": a["L0_ffn_router_w"], "br0": a["L0_ffn_router_b"],
        "gate": a["L0_ffn_we_gate"], "up": a["L0_ffn_we_up"], "down": a["L0_ffn_we_down"],
        "wr1": a["L1_ffn_Wr"], "w1": a["L1_ffn_W1"], "w2": a["L1_ffn_W2"],
    }
    arrays, ap = {}, {}
    for name, arr in lay.items():
        arr = np.ascontiguousarray(arr)
        arrays[f"in_{name}"] = arr
        ap[name] = nc.dram_tensor(f"in_{name}", arr.shape, mybir.dt.from_np(arr.dtype), kind="ExternalInput").ap()
    out = nc.dram_tensor("out_0", (B, S, D), F32, kind="ExternalOutput").ap()
    attn = [{k: ap[f"{k}{i}"] for k in ("wq", "bq", "wk", "bk", "wv", "bv", "wo", "bo")} for i in range(2)]
    l0 = {"wr": ap["wr0"], "br": ap["br0"], "gate": ap["gate"], "up": ap["up"], "down": ap["down"]}
    l1 = {"wr": ap["wr1"], "w1": ap["w1"], "w2": ap["w2"]}
    build(nc, ap["x"], ap["ctx_t"], ap["mask"], ap["mask_t"], ap["valid"], attn, l0, l1, out)
    r = _run(nc, [arrays], core_ids=[0])
    return r.results[0]["out_0"]
```

```python
from contextlib import ExitStack

import numpy as np

import concourse.bass as bass
from concourse import mybir

ALU = mybir.AluOpType
ACT = mybir.ActivationFunctionType
AX_X = mybir.AxisListType.X
F32 = mybir.dt.float32
F32R = mybir.dt.float32r
BF16 = mybir.dt.bfloat16
I32 = mybir.dt.int32
U32 = mybir.dt.uint32
U8 = mybir.dt.uint8

P = 128
B, S, D = 8, 256, 256
H, HD = 16, 16
C = D // P
RB = 4
QC = S // P
T = B * S // P
RBLOCKS = T // RB
RT_CREDIT = 4
G = 4
HG = H // G
UNITS = G * QC
MAXU = H // 2 * QC
NE = 8
BLK = 512
CAP = int(1.25 * B * S / NE)
FF = 1024
TERM = 3
ROW_MASK = 6 * HD
ROW_MAX = ROW_MASK + 1
ROWS = ROW_MAX + TERM
NEG = -float(np.float32(1e20).view(np.uint32) >> 16 << 16 and np.array([int(np.float32(1e20).view(np.uint32)) & 0xFFFF0000], np.uint32).view(np.float32)[0])
EPS = 1e-5
TWO_ONES = float(np.array([0x3F803F80], np.uint32).view(np.float32)[0])
SCALE = (1.0 / D ** 0.5, 1.0 / HD ** 0.5)
SKIP = 1 << 20
ST_CREDIT, PV_CREDIT, O_CREDIT = 2, 4, 1


class Batch:

    def __init__(self, pair, offset):
        self.pair, self.offset = pair, offset
        self.p = offset % 2
        self.use = pair + offset // 2
        self.n = pair * 2 + offset
        self.tile = None

    def plus(self, k):
        return Batch(self.pair, self.offset + k)


def build(nc, x, ctx_t, mask, mask_t, valid, attn, l0, l1, out):
    stack = ExitStack()
    with stack:
        def sb(name, shape, dt=F32):
            return stack.enter_context(nc.sbuf_tensor(name, shape, dt))

        def sem(name):
            return stack.enter_context(nc.semaphore(name))

        def dram(name, shape, dt):
            return nc.dram_tensor(name, shape, dt, kind="Internal").ap()

        q_parts = dram("q_parts", (2 * B, TERM, D, S), BF16)
        k_parts = dram("k_parts", (2 * B, TERM, D, S), BF16)
        m_parts = dram("m_parts", (2 * B, TERM, H, S), BF16)
        slots_in = dram("slots_in", (NE * CAP, D), F32)
        slots_out = dram("slots_out", (NE * CAP, D), F32)

        xs = sb("xs", [P, T, D])
        ctxT = sb("ctxT", [P, C, B * S])
        wq = [sb(f"wq{i}", [P, C, D]) for i in range(2)]
        wk = [sb(f"wk{i}", [P, C, D]) for i in range(2)]
        wv = [sb(f"wv{i}", [P, C, D]) for i in range(2)]
        wo = [sb(f"wo{i}", [P, G, D]) for i in range(2)]
        bq = [sb(f"bq{i}", [P, C]) for i in range(2)]
        bk = [sb(f"bk{i}", [P, C]) for i in range(2)]
        bv = [sb(f"bv{i}", [P, D]) for i in range(2)]
        wr = [sb(f"wr{i}", [P, C, NE]) for i in range(2)]
        br = sb("br", [P, NE])
        key_ok = sb("key_ok", [P, B * S], U8)
        all_ok = sb("all_ok", [P, S], U8)
        ok_row = sb("ok_row", [1, B * S], U8)
        ident = sb("ident", [P, P])
        ident16 = sb("ident16", [P, P], BF16)
        below = sb("below", [P, P], BF16)
        ones16 = sb("ones16", [P, P], BF16)
        iota8 = sb("iota8", [P, NE])

        w0_size = 3 * C * D
        with ExitStack() as first:
            def fsb(name, shape, dt=F32):
                return first.enter_context(nc.sbuf_tensor(name, shape, dt))

            w0_part = [[fsb(f"w0_{k}{n}", [P, w0_size], F32R) for n in range(2)] for k in range(2)]
            w0_raw = fsb("w0_raw", [P, w0_size])
            fsb("w0_rest", [P, 2 * 2 * C * FF - 5 * w0_size])
            xnT_part = [fsb(f"xnT_{n}", [P, C, B * S], F32R) for n in range(2)]
            silu = fsb("silu", [P, 2, BLK])
            h0 = fsb("h0", [P, C, BLK])
            h0_high = fsb("h0_high", [P, 2, C, BLK], F32R)
            fsb("h0_rest", [P, 2 * C * BLK])
            h0_part = [h0_high, fsb("h0_low", [P, 2, C, BLK], F32R)]
        ring = sb("ring", [P, 2, 2 * C * FF])
        qk = sb("qk", [P, 2, 2, H, S], BF16)
        prob = sb("prob", [P, 4, HG, S])
        xn_all = sb("xn_all", [P, T, D])

        ctxv = sb("ctxv", [P, C, S])
        stats = sb("stats", [P, QC, 6])
        mean_var = sb("mean_var", [P, QC, 2])
        rstd = sb("rstd", [P, QC])
        root = sb("root", [P, 3, QC])
        xn = sb("xn", [P, 2, QC, D])
        xnT = sb("xnT", [P, C, S])
        kf = sb("kf", [P, C, S])
        kr = sb("kr", [P, C, S])
        ks = sb("ks", [P, TERM, C, S], BF16)
        qf = sb("qf", [P, C, S])
        qr = sb("qr", [P, C, S])
        qs = sb("qs", [P, TERM, C, S], BF16)
        mask_i = sb("mask_i", [P, 2, QC, S], I32)
        neg_row = mask_i[0:1, :, :, :].rearrange("p a c s -> p (a c s)").bitcast(BF16)
        mask_q = sb("mask_q", [P, 2, QC, S], BF16)
        mask_k = sb("mask_k", [P, 2, QC, S], BF16)
        mx = sb("mx", [P, QC, H])
        m_rest = sb("m_rest", [P, QC, H])
        m_split = sb("m_split", [P, QC, TERM, H], BF16)
        m_T = sb("m_T", [TERM * H, S], BF16)
        v = sb("v", [P, 2, QC, H, 2 * HD])
        oT = sb("oT", [P, S // 32, 32])
        o_inv = sb("o_inv", [P, S // 32])
        osb = sb("osb", [P, G, S])

        big = qk[:, :, :, :, :].rearrange("p a b h s -> p (a b h s)").bitcast(F32)
        big_k = big.rearrange("p (a b n) -> p a b n", a=2, b=2)[:, :, 1, :]
        hT = big[:, 0:FF // P * CAP].rearrange("p (f s) -> p f s", f=FF // P)
        eT = big[:, 2560:2560 + 2 * C * CAP].rearrange("p (r c s) -> p r c s", r=2, c=C)
        erow = big[:, 3840:3840 + 2 * 3 * D].rearrange("p (r a d) -> p r a d", r=2, a=3)
        eo = big[:, 5376:5376 + 2 * 3 * D].rearrange("p (r a d) -> p r a d", r=2, a=3)
        pr = prob[:, :, :, :].rearrange("p a h s -> p (a h s)")
        got = pr[:, 0:8 * D].rearrange("p (r d) -> p r d", r=8)
        fin = pr[:, 8 * D:16 * D].rearrange("p (r d) -> p r d", r=8)
        rn = pr[:, 0:2 * RB * D].rearrange("p (r t d) -> p r t d", r=2, t=RB)
        rnT = pr[:, 2 * RB * D:4 * RB * D].rearrange("p (r t c s) -> p r t c s", r=2, t=RB, c=C)
        lg = qr[:, :, :].rearrange("p c s -> p (c s)")[:, 0:T * NE].rearrange("p (t e) -> p t e", t=T)
        small = [a[:, :, :].rearrange("p c s -> p (c s)") for a in (kf, kr)]
        table = T * NE
        lgb = small[0][:, 0:table].rearrange("p (t e) -> p t e", t=T)
        top = small[0][:, table:2 * table].rearrange("p (t e) -> p t e", t=T)
        top_i = small[0][:, 2 * table:3 * table].bitcast(U32).rearrange("p (t e) -> p t e", t=T)
        mv_all = small[1][:, 3 * table:3 * table + 2 * T].rearrange("p (t k) -> p t k", t=T)
        rstd_all = small[1][:, 3 * table + 2 * T:3 * table + 3 * T]
        root_all = small[1][:, 3 * table + 3 * T:3 * table + 6 * T].rearrange("p (k t) -> p k t", k=3)
        stats_all = sb("stats_all", [P, T, 6])
        pick = sb("pick", [P, 2, T])
        hot = qf[:, :, :].rearrange("p c s -> p (c s)")[:, 0:2 * table].rearrange("p (r t e) -> p r t e", r=2, t=T)
        hot16 = sb("hot16", [P, T, NE], BF16)
        wts = sb("wts", [P, 4, T])
        gate = sb("gate", [P, 2, T, NE])
        cnt = small[1][:, 0:2 * table].rearrange("p (r t e) -> p r t e", r=2, t=T)
        rank = small[1][:, 2 * table:3 * table].rearrange("p (t e) -> p t e", t=T)
        pos = sb("pos", [P, 4, T])
        slot = sb("slot", [P, 2, T], U32)

        ps = [stack.enter_context(nc.psum_tensor(f"ps{i}", [P, 512], F32)) for i in range(8)]
        misc, pv_bank = ps[7], ps[6]
        mps = [ps[4], ps[5]]
        o_bank = ps[4]

        names = """ones_again settled const_pool ident_done router_bias_in ctx_in0 ctx_in x_in0 x_in ffn_bias_in valid_in wo_zero
 qk_ones
            ones_set neg_done slots_zero
            ln rstd_ready xn_ready xnT_psum xnT_ready k_psum kf_ready ks_act ks_pool k_written
            q_psum qf_ready qs_act qs_pool q_written
            mask_in mask_t_in mask_q_ready mask_k_ready
            ctxv_ready v_psum v_ready
            max_psum mx_done m_chain mT_psum mT_ready m_written
            st_ready exp_done pv_done o_read o_chain o_ready oproj resid
            rt_stats rt_high rt_ln rt_rstd rt_xn rt_T rt_Tcopy rt_copy rt_lg rt_lgcopy
            route_vec route_act route_pe
            w0_in w0_high w0_low gu_psum silu_done h_done h_high h_low down_psum acc_done
            scattered w1_in0 w1_in1 er_in0 er_in1 eT_psum eT_done hid_psum hid_act hid_vec
            eo_psum eo_done eo_stored0 eo_stored1 x_plus fin_done""".split()
        s = {n: sem(n) for n in names}
        qk_loaded = [[sem(f"qk_loaded{p}{g}") for g in range(2)] for p in range(2)]
        m_loaded = [sem(f"m_loaded{p}") for p in range(2)]
        gathered = [sem(f"gathered{r}") for r in range(8)]
        out_stored = [sem(f"out_stored{r}") for r in range(8)]
        weights_in = [[sem(f"weights{i}{k}_in") for k in range(2)] for i in range(2)]
        w1_in = [s["w1_in0"], s["w1_in1"]]
        er_in = [s["er_in0"], s["er_in1"]]
        eo_stored = [s["eo_stored0"], s["eo_stored1"]]
        block = stack.enter_context(nc.Block())

        def wait(eng, name, value):
            if not isinstance(value, int) or value > 0:
                eng.wait_ge(s[name] if isinstance(name, str) else name, value)

        def settle(eng):
            eng.sem_inc(s["settled"], 1)

        def qk_value(b, layer):
            return b.use * 96 + 96 if layer == 0 else (b.use - B // 2) * 112 + 96 * (B // 2) + 112

        def load_weights(eng, i, stage):
            done = weights_in[i][stage]
            if stage == 0:
                for w, name in ((wk, "wk"), (wq, "wq"), (wv, "wv")):
                    eng.dma_start(w[i][:, :, :], attn[i][name].rearrange("(c p) n -> p c n", p=P)).then_inc(done, 16)
                for w, name in ((bk, "bk"), (bq, "bq")):
                    eng.dma_start(w[i][:, :], attn[i][name].rearrange("(c p) -> p c", p=P),
                                  allow_slow_non_contiguous=True).then_inc(done, 16)
                eng.dma_start(bv[i][:, :], attn[i]["bv"].rearrange("(o n) -> o n", o=1).broadcast_to([P, D])).then_inc(done, 16)
            else:
                wo_v = attn[i]["wo"].rearrange("(g j d) n -> j d g n", g=G, j=HG)
                for j in range(HG):
                    eng.dma_start(wo[i][32 * j:32 * j + HD, :, :], wo_v[j]).then_inc(done, 16)
                eng.dma_start(wo[i][HD:HD + 1, 0, :], attn[i]["bo"].rearrange("(o n) -> o n", o=1)).then_inc(done, 16)
                eng.dma_start(wr[i][:, :, :], (l0, l1)[i]["wr"].rearrange("(c p) n -> p c n", p=P)).then_inc(done, 16)

        def batches(eng, layer, prologue, iteration):
            prologue(layer)
            base = layer * B // 2
            with eng.Fori(0, (B - 2) // 2) as i:
                for k in range(2):
                    iteration(layer, Batch(i + base, k), i * 2 + k, True, True)
            iteration(layer, Batch(base, B - 2), B - 2, True, False)
            iteration(layer, Batch(base, B - 1), B - 1, False, False)

        @block.sync
        def _(sp):
            sp.dma_start(ctxT[:, :, 0:2 * S], ctx_t.rearrange("(c p) s -> p c s", p=P)[:, :, 0:2 * S]).then_inc(s["ctx_in0"], 16)
            for t in range(2):
                sp.dma_start(xs[:, t * QC:(t + 1) * QC, :],
                             x[t].rearrange("(t p) d -> p t d", p=P)).then_inc(s["x_in0"], 16)
            sp.dma_start(ctxT[:, :, 2 * S:], ctx_t.rearrange("(c p) s -> p c s", p=P)[:, :, 2 * S:]).then_inc(s["ctx_in"], 16)
            sp.dma_start(xs[:, 2 * QC:, :],
                         x[2:B].rearrange("b (t p) d -> p (b t) d", p=P)).then_inc(s["x_in"], 16)

            def load_mask_q(b, at):
                wait(sp, "mask_q_ready", b.n)
                sp.dma_start(mask_i[:, 0, :, :], mask[at].rearrange("(c p) k -> p c k", p=P)).then_inc(s["mask_in"], 16)

            def load_mask_k(b, at):
                wait(sp, "mask_k_ready", b.n)
                sp.dma_start(mask_i[:, 1, :, :], mask_t[at].rearrange("(c p) q -> p c q", p=P)).then_inc(s["mask_t_in"], 16)

            def write_parts(b):
                sp.wait_ge(s["ks_pool"], b.n * 2 + 2)
                sp.dma_start(k_parts[b.n].rearrange("t (c p) s -> p t c s", p=P), ks[:, :, :, :]).then_inc(s["k_written"], 16)
                sp.wait_ge(s["qs_pool"], b.n * 2 + 2)
                sp.dma_start(q_parts[b.n].rearrange("t (c p) s -> p t c s", p=P), qs[:, :, :, :]).then_inc(s["q_written"], 16)

            def load_half(b, at, layer, half):
                sp.wait_ge(s["k_written"], b.n * 16 + 16)
                sp.wait_ge(s["q_written"], b.n * 16 + 16)
                settle(sp)
                wait(sp, "st_ready", b.n * UNITS - 2 * UNITS + (half + 1) * UNITS // 2)
                heads = slice(half * H // 2, (half + 1) * H // 2)
                for side, parts in ((0, q_parts), (1, k_parts)):
                    src = parts[b.n].rearrange("t (d h) s -> (t d) h s", h=H)
                    for to, n, frm in ((0, 3, 0), (3, 2, side), (5, 1, 2 * side)):
                        sp.dma_start(qk[to * HD:(to + n) * HD, b.p, side, heads, :],
                                     src[frm * HD:(frm + n) * HD, heads, :]).then_inc(qk_loaded[b.p][half], 16)
                if layer == 1:
                    row = neg_row[0:1, bass.ds(at * S, S)]
                    sp.dma_start(qk[ROW_MASK:ROW_MASK + 1, b.p, 1, heads, :],
                                 row.rearrange("o (a s) -> o a s", a=1).broadcast_to([1, H // 2, S])).then_inc(qk_loaded[b.p][half], 16)

            def write_max(b):
                sp.wait_ge(s["mT_ready"], b.n + 1)
                settle(sp)
                sp.dma_start(m_parts[b.n].rearrange("t h s -> (t h) s"), m_T[:, :]).then_inc(s["m_written"], 16)

            def load_max(b):
                sp.wait_ge(s["m_written"], b.n * 16 + 16)
                settle(sp)
                wait(sp, "st_ready", b.n * UNITS - UNITS + 1)
                settle(sp)
                sp.dma_start(qk[ROW_MAX:ROWS, b.p, 0, :, :],
                             m_parts[b.n]).then_inc(m_loaded[b.p], 16)

            def prologue(layer):
                base = layer * B // 2
                b0, b1 = Batch(base, 0), Batch(base, 1)
                if layer == 0:
                    load_mask_q(b0, 0)
                    load_mask_k(b0, 0)
                    sp.wait_ge(s["qk_ones"], 2)
                else:
                    sp.wait_ge(s["acc_done"], FFN0_ACC)
                    sp.wait_ge(s["neg_done"], 1)
                    sp.wait_ge(s["ones_again"], 1)
                write_parts(b0)
                for half in range(2):
                    load_half(b0, 0, layer, half)
                if layer == 0:
                    load_mask_q(b1, 1)
                write_parts(b1)
                write_max(b0)
                load_max(b0)
                for half in range(2):
                    load_half(b1, 1, layer, half)

            def iteration(layer, b, at, more, prep):
                if layer == 0 and prep:
                    load_mask_q(b.plus(2), at + 2)
                if layer == 0 and more:
                    load_mask_k(b.plus(1), at + 1)
                if prep:
                    write_parts(b.plus(2))
                if more:
                    write_max(b.plus(1))
                    load_max(b.plus(1))
                if prep:
                    for half in range(2):
                        load_half(b.plus(2), at + 2, layer, half)

            batches(sp, 0, prologue, iteration)

            sp.dma_start(br[:, :], l0["br"].rearrange("(o n) -> o n", o=1).broadcast_to([P, NE])).then_inc(s["router_bias_in"], 16)
            gate_v = l0["gate"].rearrange("e (c p) f -> e p c f", p=P)
            up_v = l0["up"].rearrange("e (c p) f -> e p c f", p=P)
            down_v = l0["down"].rearrange("e (c p) f -> e p c f", p=P)
            with sp.Fori(0, NE) as e:
                sp.wait_ge(s["w0_low"], e * 3 + W0_CREDIT)
                for j, w in enumerate((gate_v, up_v, down_v)):
                    sp.dma_start(w0_raw[:, j * C * D:(j + 1) * C * D].rearrange("p (c f) -> p c f", c=C), w[e]).then_inc(s["w0_in"], 16)
            for stage in range(2):
                load_weights(sp, 1, stage)
            sp.dma_start(key_ok[:, :], valid.rearrange("(o b) s -> o (b s)", o=1).broadcast_to([P, B * S])).then_inc(s["valid_in"], 16)
            sp.dma_start(ok_row[:, :], valid.rearrange("(o b) s -> o (b s)", o=1)).then_inc(s["valid_in"], 16)
            sp.dma_start(slots_in.rearrange("(a p) d -> p a d", p=P), xn_all[:, 0:1, :].broadcast_to([P, NE * CAP // P, D])).then_inc(s["slots_zero"], 16)

            batches(sp, 1, prologue, iteration)

            w1_v = l1["w1"].rearrange("e (c p) f -> e p c f", p=P)
            w2_v = l1["w2"].rearrange("e (c p) d -> e p c d", p=P)
            with sp.Fori(0, NE // 2) as i:
                for k in range(2):
                    e = i * 2 + k
                    sp.wait_ge(s["eo_done"], e * 3 - 3 + EO_CREDIT)
                    sp.dma_start(ring[:, k, 0:C * FF].rearrange("p (c f) -> p c f", c=C), w1_v[e]).then_inc(w1_in[k], 16)
                    sp.dma_start(ring[:, k, C * FF:].rearrange("p (c d) -> p c d", d=D), w2_v[e]).then_inc(w1_in[k], 16)
                    sp.wait_ge(s["scattered"], 16 * T)
                    rows = slots_in[bass.ds(e * CAP, CAP), :]
                    sp.dma_start(erow[:, k, 0:2, :], rows[0:2 * P, :].rearrange("(a p) d -> p a d", p=P)).then_inc(er_in[k], 16)
                    sp.dma_start(erow[0:CAP - 2 * P, k, 2, :], rows[2 * P:CAP, :]).then_inc(er_in[k], 16)
            for t in range(T):
                sp.wait_ge(s["fin_done"], t + 1)
                sp.dma_start(out[t // QC, (t % QC) * P:(t % QC + 1) * P, :], fin[:, t % 8, :]).then_inc(out_stored[t % 8], 16)
            for r in range(8):
                sp.wait_ge(out_stored[r], 16 * T // 8)

        @block.gpsimd
        def _(pool):
            for m in (ident, ident16):
                pool.memset(m[:, :], 0.0).then_inc(s["const_pool"], 1)
            pool.memset(below[:, :], 1.0).then_inc(s["const_pool"], 1)
            pool.memset(ones16[:, :], 1.0).then_inc(s["const_pool"], 1)
            pool.wait_ge(s["const_pool"], 4)
            for m in (ident, ident16):
                pool.affine_select(out=m[:, :], in_=m[:, :], compare_op=ALU.not_equal, fill=1.0, base=0,
                                   pattern=[[-1, P]], channel_multiplier=1).then_inc(s["ident_done"], 1)
            pool.affine_select(out=below[:, :], in_=below[:, :], compare_op=ALU.is_gt, fill=0.0, base=0,
                               pattern=[[1, P]], channel_multiplier=-1).then_inc(s["ident_done"], 1)
            pool.wait_ge(s["ident_done"], 3)
            pool.memset(big[ROW_MASK:P, :], TWO_ONES).then_inc(s["qk_ones"], 1)
            pool.wait_ge(s["qk_ones"], 1)
            pool.memset(big_k[ROW_MASK:ROW_MASK + 1, :, :], 0.0).then_inc(s["qk_ones"], 1)
            pool.wait_ge(s["qk_ones"], 2)
            pool.iota(iota8[:, :], pattern=[[1, NE]], base=0, channel_multiplier=0,
                      allow_small_or_imprecise_dtypes=True).then_inc(s["ident_done"], 1)

            def inverse_root(chain, start, root, mean_var, rstd):
                var, y, t = root[:, 0, :], root[:, 1, :], root[:, 2, :]
                settle(pool)
                pool.tensor_scalar(var, mean_var[:, :, 1], EPS, None, ALU.add).then_inc(chain, 1)
                pool.wait_ge(chain, start + 1)
                settle(pool)
                pool.tensor_scalar(y.bitcast(I32), var.bitcast(I32), -0.5, float(0x5F3759DF), ALU.mult, ALU.add).then_inc(chain, 1)
                for k in range(ROOT_NEWTON):
                    pool.wait_ge(chain, start + 2 + 4 * k)
                    pool.tensor_tensor(t, y, y, ALU.mult).then_inc(chain, 1)
                    pool.wait_ge(chain, start + 3 + 4 * k)
                    pool.tensor_tensor(t, t, var, ALU.mult).then_inc(chain, 1)
                    pool.wait_ge(chain, start + 4 + 4 * k)
                    settle(pool)
                    pool.tensor_scalar(t, t, -0.5, 1.5, ALU.mult, ALU.add).then_inc(chain, 1)
                    pool.wait_ge(chain, start + 5 + 4 * k)
                    to = rstd[:, :] if k == ROOT_NEWTON - 1 else y
                    pool.tensor_tensor(to, y, t, ALU.mult).then_inc(chain, 1)

            def inv_std(b):
                pool.wait_ge(s["ln"], b.n * 4 + 4)
                inverse_root(s["rstd_ready"], b.n * ROOT_STEPS, root, mean_var, rstd)

            def k_rest(b):
                pool.wait_ge(s["ks_act"], b.n * 2 + 1)
                pool.tensor_tensor(kr[:, :, :], kf[:, :, :], ks[:, 2, :, :], ALU.subtract).then_inc(s["ks_pool"], 1)
                pool.wait_ge(s["ks_act"], b.n * 2 + 2)
                pool.tensor_tensor(ks[:, 0, :, :], kr[:, :, :], ks[:, 1, :, :], ALU.subtract).then_inc(s["ks_pool"], 1)

            def q_rest(b):
                pool.wait_ge(s["qs_act"], b.n * 2 + 1)
                pool.tensor_tensor(qr[:, :, :], qf[:, :, :], qs[:, 0, :, :], ALU.subtract).then_inc(s["qs_pool"], 1)
                pool.wait_ge(s["qs_act"], b.n * 2 + 2)
                pool.tensor_tensor(qs[:, 2, :, :], qr[:, :, :], qs[:, 1, :, :], ALU.subtract).then_inc(s["qs_pool"], 1)

            def copy_ctx(b, at):
                wait(pool, "v_psum", b.n)
                pool.tensor_copy(ctxv[:, :, :], ctxT[:, :, bass.ds(at * S, S)]).then_inc(s["ctxv_ready"], 1)

            def mask_for_q(b):
                pool.wait_ge(s["mask_in"], b.n * 16 + 16)
                wait(pool, "mx_done", b.n * MAXU - MAXU)
                settle(pool)
                pool.tensor_scalar(mask_q[:, b.p, :, :], mask_i[:, 0, :, :], 0.0, NEG, ALU.is_equal, ALU.mult).then_inc(s["mask_q_ready"], 1)

            def mask_for_k(b):
                pool.wait_ge(s["mask_t_in"], b.n * 16 + 16)
                wait(pool, "st_ready", b.n * UNITS - UNITS + 1)
                settle(pool)
                pool.tensor_scalar(mask_k[:, b.p, :, :], mask_i[:, 1, :, :], 0.0, NEG, ALU.is_equal, ALU.mult).then_inc(s["mask_k_ready"], 1)

            def prologue(layer):
                base = layer * B // 2
                if layer == 1:
                    pool.wait_ge(s["acc_done"], FFN0_ACC)
                    pool.memset(big[ROW_MASK:P, :], TWO_ONES).then_inc(s["ones_again"], 1)
                    pool.wait_ge(s["ones_again"], 1)
                b0, b1 = Batch(base, 0), Batch(base, 1)
                inv_std(b0)
                if layer == 0:
                    mask_for_q(b0)
                k_rest(b0)
                inv_std(b1)
                q_rest(b0)
                k_rest(b1)
                if layer == 0:
                    pool.wait_ge(s["ctx_in0"], 16)
                q_rest(b1)
                copy_ctx(b0, 0)
                if layer == 0:
                    mask_for_k(b0)
                    mask_for_q(b1)
                if layer == 0:
                    pool.wait_ge(s["ctx_in"], 16)

            def iteration(layer, b, at, more, prep):
                if prep:
                    inv_std(b.plus(2))
                    k_rest(b.plus(2))
                if more:
                    copy_ctx(b.plus(1), at + 1)
                if prep:
                    q_rest(b.plus(2))
                if layer == 0 and more:
                    mask_for_k(b.plus(1))
                if layer == 0 and prep:
                    mask_for_q(b.plus(2))

            def route_std(layer):
                pool.wait_ge(s["rt_ln"], (layer + 1) * T)
                inverse_root(s["rt_rstd"], layer * ROOT_STEPS, root_all, mv_all, rstd_all)

            pool.sem_inc(s["w0_low"], W0_CREDIT)
            pool.sem_inc(s["h_low"], GU_CREDIT)
            batches(pool, 0, prologue, iteration)
            route_std(0)
            def w0_low(e, k, j):
                part = slice(j * C * D, (j + 1) * C * D)
                pool.wait_ge(s["w0_high"], e * 3 + j + 1)
                pool.tensor_tensor(w0_part[k][1][:, part], w0_raw[:, part], w0_part[k][0][:, part], ALU.subtract).then_inc(s["w0_low"], 1)

            def expert0(i, k, more):
                e = i * 2 + k
                for blk in range(T // 4):
                    for f in range(C):
                        pool.wait_ge(s["h_high"], (e * 4 + blk) * C + f + 1)
                        pool.tensor_tensor(h0_part[1][:, blk % 2, f, :], h0[:, f, :], h0_part[0][:, blk % 2, f, :], ALU.subtract).then_inc(s["h_low"], 1)
                    if more and blk > 0:
                        w0_low(e + 1, 1 - k, blk - 1)

            for j in range(3):
                w0_low(0, 0, j)
            with pool.Fori(0, NE // 2 - 1) as i:
                for k in range(2):
                    expert0(i, k, True)
            expert0(NE // 2 - 1, 0, True)
            expert0(NE // 2 - 1, 1, False)
            pool.wait_ge(s["valid_in"], 32)
            pool.tensor_scalar(neg_row[:, :], ok_row[:, :], 0.0, NEG, ALU.is_equal, ALU.mult).then_inc(s["neg_done"], 1)
            batches(pool, 1, prologue, iteration)
            route_std(1)
            pool.wait_ge(s["route_vec"], ROUTE1_SLOTS)
            pool.wait_ge(s["rt_copy"], 2 * RBLOCKS + RT_CREDIT)
            for t in range(T):
                pool.indirect_dma_start(slots_in[:, :], bass.IndirectOffsetOnAxis(ap=slot[:, 0, t:t + 1], axis=0),
                                        xn_all[:, t, :], None, bounds_check=NE * CAP - 1, oob_is_err=False).then_inc(s["scattered"], 16)
            for k in range(2):
                pool.wait_ge(eo_stored[k], 32 * (NE // 2) + HID_CREDIT)
            for t in range(T):
                if t >= 8:
                    pool.wait_ge(s["fin_done"], t - 7)
                pool.indirect_dma_start(got[:, t % 8, :], None, slots_out[:, :],
                                        bass.IndirectOffsetOnAxis(ap=slot[:, 1, t:t + 1], axis=0)).then_inc(gathered[t % 8], 16)

        @block.scalar
        def _(act):
            load_weights(act, 0, 0)
            act.wait_ge(s["wo_zero"], 2)
            load_weights(act, 0, 1)
            act.sem_inc(s["exp_done"], ST_CREDIT)
            act.sem_inc(s["eo_done"], EO_CREDIT)
            for name in ("eT_done", "hid_act"):
                act.sem_inc(s[name], HID_CREDIT)
            for k in range(2):
                act.sem_inc(eo_stored[k], HID_CREDIT)
            def k_high(b):
                act.wait_ge(s["kf_ready"], b.n * 2 + 2)
                wait(act, "k_written", b.n * 16)
                act.activation(ks[:, 2, :, :], kf[:, :, :], ACT.Copy).then_inc(s["ks_act"], 1)

            def k_mid(b):
                act.wait_ge(s["ks_pool"], b.n * 2 + 1)
                act.activation(ks[:, 1, :, :], kr[:, :, :], ACT.Copy).then_inc(s["ks_act"], 1)

            def q_evac(b, layer):
                act.wait_ge(s["q_psum"], b.n + 1)
                wait(act, "qs_pool", b.n * 2)
                for c in range(C):
                    act.activation(qf[:, c, :], misc[:, c * S:(c + 1) * S], ACT.Identity, bias=bq[layer][:, c:c + 1]).then_inc(s["qf_ready"], 1)

            def q_high(b):
                act.wait_ge(s["qf_ready"], b.n * 2 + 2)
                wait(act, "q_written", b.n * 16)
                act.activation(qs[:, 0, :, :], qf[:, :, :], ACT.Copy).then_inc(s["qs_act"], 1)

            def q_mid(b):
                act.wait_ge(s["qs_pool"], b.n * 2 + 1)
                act.activation(qs[:, 1, :, :], qr[:, :, :], ACT.Copy).then_inc(s["qs_act"], 1)

            def xnT_evac(b):
                act.wait_ge(s["xnT_psum"], b.n + 1)
                wait(act, "q_psum", b.n)
                act.activation(xnT[:, :, :], misc[:, :].rearrange("p (c s) -> p c s", c=C), ACT.Copy).then_inc(s["xnT_ready"], 1)

            def exp(b, u, layer):
                unit = b.n * UNITS + u
                act.wait_ge(s["st_ready"], unit + 1)
                act.wait_ge(s["pv_done"], unit - 3 + PV_CREDIT)
                for half in range(2):
                    ins = act.activation(prob[:, u % 4, 2 * half:2 * half + 2, :],
                                         ps[2 * (u % 2) + half][:, :].rearrange("p (h s) -> p h s", h=2), ACT.Exp, scale=SCALE[layer])
                ins.then_inc(s["exp_done"], 1)

            def prologue(layer):
                for k in range(2):
                    b = Batch(layer * B // 2, k)
                    if k == 0:
                        act.wait_ge(weights_in[layer][0], 16 * 6)
                    k_high(b)
                    xnT_evac(b)
                    k_mid(b)
                    q_evac(b, layer)
                    q_high(b)
                    q_mid(b)

            def iteration(layer, b, at, more, prep):
                b2 = b.plus(2)
                exp(b, 0, layer)
                exp(b, 1, layer)
                if prep:
                    k_high(b2)
                exp(b, 2, layer)
                if prep:
                    k_mid(b2)
                    xnT_evac(b2)
                exp(b, 3, layer)
                if prep:
                    q_evac(b2, layer)
                    q_high(b2)
                exp(b, 4, layer)
                if prep:
                    q_mid(b2)
                for u in range(5, UNITS):
                    exp(b, u, layer)

            def route_evac(layer):
                with act.Fori(0, RBLOCKS // 2) as i:
                    for k in range(2):
                        n = i * 2 + k + layer * RBLOCKS
                        act.wait_ge(s["rt_lg"], n - 1 + RT_CREDIT)
                        act.wait_ge(s["rt_copy"], n - 1 + RT_CREDIT)
                        for half in range(2):
                            act.wait_ge(s["rt_T"], n * 2 + half + 1 + RT_CREDIT)
                            act.activation(rnT[:, k, 2 * half:2 * half + 2, :, :],
                                           ps[2 * k + half][:, :].rearrange("p (t c s) -> p t c s", t=2, c=C), ACT.Copy).then_inc(s["rt_Tcopy"], 1)
                    for k in range(2):
                        n = i * 2 + k + layer * RBLOCKS
                        act.wait_ge(s["rt_lg"], n + 1 + RT_CREDIT)
                        act.activation(lg[:, bass.ds((i * 2 + k) * RB, RB), :],
                                       ps[4 + k][:, 0:RB * NE].rearrange("p (a e) -> p a e", a=RB), ACT.Copy).then_inc(s["rt_lgcopy"], 1)

            for name in ("rt_Tcopy", "rt_lgcopy"):
                act.sem_inc(s[name], RT_CREDIT)
            batches(act, 0, prologue, iteration)
            route_evac(0)
            act.wait_ge(s["route_vec"], ROUTE0_DIFF)
            act.activation(wts[:, 1, :], wts[:, 0, :], ACT.Exp).then_inc(s["route_act"], 1)
            with act.Fori(0, NE * T // 4) as i:
                for f in range(C):
                    n = i * C + f
                    act.wait_ge(s["gu_psum"], n + 1)
                    act.wait_ge(s["h_done"], n + GU_CREDIT - 1)
                    act.activation(silu[:, f, :], ps[2 * f][:, :], ACT.Silu).then_inc(s["silu_done"], 1)
            batches(act, 1, prologue, iteration)
            route_evac(1)
            act.wait_ge(s["route_vec"], ROUTE1_DIFF)
            act.activation(gate[:, 0, :, :], gate[:, 1, :, :], ACT.Exp).then_inc(s["route_act"], 1)
            act.wait_ge(s["route_vec"], ROUTE1_SLOTS)
            def rows_evac(k, e):
                act.wait_ge(s["eT_psum"], e + 1)
                for c in range(C):
                    ins = act.activation(eT[:, k, c, :], ps[c][:, 0:CAP], ACT.Copy)
                ins.then_inc(s["eT_done"], 1)

            def expert(i, k, more):
                e = i * 2 + k
                for f in range(0, FF // P, 2):
                    act.wait_ge(s["hid_psum"], e * (FF // P) + f + 1)
                    act.activation(hT[:, f, :], ps[2][:, 0:CAP], ACT.Relu).then_inc(s["hid_act"], 1)
                if more:
                    rows_evac(1 - k, e + 1)
                act.wait_ge(eo_stored[k], i * 32 + HID_CREDIT)
                for a in range(3):
                    n = P if a < 2 else CAP - 2 * P
                    act.wait_ge(s["eo_psum"], e * 3 + a + 1)
                    act.activation(eo[0:n, k, a, :], ps[4 + a][0:n, 0:D], ACT.Copy).then_inc(s["eo_done"], 1)
                act.wait_ge(s["eo_done"], e * 3 + 3 + EO_CREDIT)
                rows = slots_out[bass.ds(e * CAP, CAP), :]
                act.dma_start(rows[0:2 * P, :].rearrange("(a p) d -> p a d", p=P), eo[:, k, 0:2, :]).then_inc(eo_stored[k], 16)
                act.dma_start(rows[2 * P:CAP, :], eo[0:CAP - 2 * P, k, 2, :]).then_inc(eo_stored[k], 16)

            rows_evac(0, 0)
            with act.Fori(0, NE // 2 - 1) as i:
                for k in range(2):
                    expert(i, k, True)
            expert(NE // 2 - 1, 0, True)
            expert(NE // 2 - 1, 1, False)

        @block.tensor
        def _(pe):
            def k_proj(b, at, layer):
                wait(pe, "v_ready", b.n - 1)
                for m in range(C):
                    for c in range(C):
                        ins = pe.matmul(misc[:, m * S:(m + 1) * S], wk[layer][:, c, m * P:(m + 1) * P],
                                        ctxT[:, c, bass.ds(at * S, S)], start=(c == 0), stop=(c == C - 1), skip_group_check=True)
                ins.then_inc(s["k_psum"], 1)

            def xn_transpose(b):
                pe.wait_ge(s["xn_ready"], b.n * 2 + 2)
                pe.wait_ge(s["kf_ready"], b.n * 2 + 2)
                for c in range(C):
                    for t in range(QC):
                        ins = pe.transpose(misc[:, c * S + t * P:c * S + (t + 1) * P], xn[:, b.p, t, c * P:(c + 1) * P], ident[:, :])
                ins.then_inc(s["xnT_psum"], 1)

            def q_proj(b, layer):
                pe.wait_ge(s["xnT_ready"], b.n + 1)
                for m in range(C):
                    for c in range(C):
                        ins = pe.matmul(misc[:, m * S:(m + 1) * S], wq[layer][:, c, m * P:(m + 1) * P],
                                        xnT[:, c, :], start=(c == 0), stop=(c == C - 1), skip_group_check=True)
                ins.then_inc(s["q_psum"], 1)

            def v_proj(b, layer):
                pe.wait_ge(s["ctxv_ready"], b.n + 1)
                pe.wait_ge(s["mT_ready"], b.n + 1)
                for t in range(QC):
                    for c in range(C):
                        ins = pe.matmul(misc[:, t * D:(t + 1) * D], ctxv[:, c, t * P:(t + 1) * P], wv[layer][:, c, :],
                                        start=(c == 0), stop=(c == C - 1), skip_group_check=True)
                ins.then_inc(s["v_psum"], 1)

            def max_unit(b, g, k, layer):
                if k == 0 and g % 2 == 0:
                    pe.wait_ge(qk_loaded[b.p][g // 2], qk_value(b, layer))
                if k == 0 and g == 0:
                    if layer == 0:
                        pe.wait_ge(s["mask_q_ready"], b.n + 1)
                    wait(pe, "resid", b.n - 1 + O_CREDIT)
                pair, c = k // 2, k % 2
                wait(pe, "mx_done", b.n * MAXU + 4 * g + k - 1)
                bank = mps[k % 2]
                for j in range(2):
                    h = g * HG + 2 * pair + j
                    ins = pe.matmul(bank[:, j * S:(j + 1) * S], qk[0:ROW_MASK + 1, b.p, 0, h, c * P:(c + 1) * P],
                                    qk[0:ROW_MASK + 1, b.p, 1, h, :], start=(j == 0), stop=(layer == 1), skip_group_check=True)
                if layer == 0:
                    ins = pe.matmul(bank[:, :].rearrange("p (h s) -> p h s", h=2), ident16[:, :],
                                    mask_q[:, b.p, c:c + 1, :].broadcast_to([P, 2, S]), start=False, stop=True, skip_group_check=True)
                ins.then_inc(s["max_psum"], 1)

            def max_transpose(b):
                pe.wait_ge(s["m_chain"], b.n * 4 + 4)
                wait(pe, "qf_ready", b.n * 2 + 2)
                settle(pe)
                for c in range(QC):
                    ins = pe.transpose(misc[0:TERM * H, :].bitcast(BF16)[:, c * P:(c + 1) * P],
                                       m_split[:, c, :, :].rearrange("p t h -> p (t h)"), ident16[:, :])
                ins.then_inc(s["mT_psum"], 1)

            def scores(b, u, half, layer):
                g, c = u // QC, u % QC
                if half == 0:
                    if u == 0:
                        pe.wait_ge(m_loaded[b.p], b.use * 16 + 16)
                        if layer == 0:
                            pe.wait_ge(s["mask_k_ready"], b.n + 1)
                    pe.wait_ge(s["exp_done"], b.n * UNITS + u - 1 + ST_CREDIT)
                bank = ps[2 * (u % 2) + half]
                for j in range(2):
                    h = g * HG + 2 * half + j
                    ins = pe.matmul(bank[:, j * S:(j + 1) * S], qk[0:ROWS, b.p, 1, h, c * P:(c + 1) * P],
                                    qk[0:ROWS, b.p, 0, h, :], start=(j == 0), stop=(layer == 1), skip_group_check=True)
                if layer == 0:
                    ins = pe.matmul(bank[:, :].rearrange("p (h s) -> p h s", h=2), ident16[:, :],
                                    mask_k[:, b.p, c:c + 1, :].broadcast_to([P, 2, S]), start=False, stop=True, skip_group_check=True)
                if half == 1:
                    ins.then_inc(s["st_ready"], 1)

            def values(b, u):
                g, c = u // QC, u % QC
                if u == 0:
                    pe.wait_ge(s["v_ready"], b.n + 1)
                pe.wait_ge(s["exp_done"], b.n * UNITS + u + 1 + ST_CREDIT)
                if c == 0:
                    pe.wait_ge(s["o_read"], b.n * G + g + O_CREDIT)
                for j in range(HG):
                    ins = pe.matmul(pv_bank[32 * j:32 * j + 32, 0:S], v[:, b.p, c, g * HG + j, :],
                                    prob[:, u % 4, j, :], start=(c == 0), stop=(c == QC - 1), tile_position=(0, 32 * j), skip_group_check=True)
                ins.then_inc(s["pv_done"], 1)

            def o_proj(b, layer):
                pe.wait_ge(s["o_ready"], b.n * G + G + O_CREDIT)
                for t in range(QC):
                    for g in range(G):
                        ins = pe.matmul(o_bank[:, t * D:(t + 1) * D], osb[:, g, t * P:(t + 1) * P], wo[layer][:, g, :],
                                        start=(g == 0), stop=(g == G - 1), skip_group_check=True)
                ins.then_inc(s["oproj"], 1)

            def prologue(layer):
                base = layer * B // 2
                if layer == 0:
                    pe.wait_ge(s["ident_done"], 4)
                    pe.wait_ge(s["ctx_in0"], 16)
                else:
                    pe.wait_ge(s["acc_done"], FFN0_ACC)
                pe.wait_ge(weights_in[layer][0], 16 * 6)
                for k in range(2):
                    b = Batch(base, k)
                    if k == 1:
                        pe.wait_ge(s["qf_ready"], b.n * 2)
                    k_proj(b, k, layer) if k == 0 else k_again(b, k, layer)
                    xn_transpose(b)
                    q_proj(b, layer)
                b = Batch(base, 0)
                for g in range(G):
                    for k in range(4):
                        max_unit(b, g, k, layer)
                pe.wait_ge(s["qf_ready"], b.n * 2 + 4)
                max_transpose(b)
                v_proj(b, layer)
                pe.wait_ge(weights_in[layer][1], 16 * 6)
                if layer == 0:
                    pe.wait_ge(s["ctx_in"], 16)

            def k_again(b, at, layer):
                for m in range(C):
                    for c in range(C):
                        ins = pe.matmul(misc[:, m * S:(m + 1) * S], wk[layer][:, c, m * P:(m + 1) * P],
                                        ctxT[:, c, at * S:(at + 1) * S], start=(c == 0), stop=(c == C - 1), skip_group_check=True)
                ins.then_inc(s["k_psum"], 1)

            def iteration(layer, b, at, more, prep):
                b1, b2 = b.plus(1), b.plus(2)
                for u in range(UNITS):
                    first = more and u < G
                    scores(b, u, 0, layer)
                    if first:
                        max_unit(b1, u, 0, layer)
                    scores(b, u, 1, layer)
                    if first:
                        max_unit(b1, u, 1, layer)
                    if u > 0:
                        values(b, u - 1)
                    if first:
                        max_unit(b1, u, 2, layer)
                    if prep and u == 0:
                        k_proj(b2, at + 2, layer)
                    if prep and u == 2:
                        xn_transpose(b2)
                    if prep and u == 3:
                        q_proj(b2, layer)
                    if first:
                        max_unit(b1, u, 3, layer)
                    if more and u == 5:
                        if prep:
                            pe.wait_ge(s["qf_ready"], b2.n * 2 + 2)
                        else:
                            pe.wait_ge(s["v_ready"], b.n + 1)
                        max_transpose(b1)
                values(b, UNITS - 1)
                if more:
                    v_proj(b1, layer)
                    pe.wait_ge(s["mx_done"], (b.n + 2) * MAXU)
                else:
                    pe.wait_ge(s["resid"], b.n + O_CREDIT)
                o_proj(b, layer)

            def route(layer):
                pe.wait_ge(s["resid"], (layer + 1) * B + O_CREDIT)
                with pe.Fori(0, RBLOCKS // 2) as i:
                    for k in range(2):
                        n = i * 2 + k + layer * RBLOCKS
                        pe.wait_ge(s["rt_Tcopy"], n * 2 - 2 + RT_CREDIT)
                        for t in range(RB):
                            pe.wait_ge(s["rt_xn"], n * RB + t + 1)
                            for c in range(C):
                                ins = pe.transpose(ps[2 * k + t // 2][:, (t % 2 * C + c) * P:(t % 2 * C + c + 1) * P],
                                                   rn[:, k, t, c * P:(c + 1) * P], ident[:, :])
                            if t % 2 == 1:
                                ins.then_inc(s["rt_T"], 1)
                    for k in range(2):
                        n = i * 2 + k + layer * RBLOCKS
                        pe.wait_ge(s["rt_Tcopy"], n * 2 + 2 + RT_CREDIT)
                        pe.wait_ge(s["rt_lgcopy"], n - 1 + RT_CREDIT)
                        for t in range(RB):
                            for c in range(C):
                                ins = pe.matmul(ps[4 + k][:, t * NE:(t + 1) * NE], rnT[:, k, t, c, :], wr[layer][:, c, :],
                                                start=(c == 0), stop=(c == C - 1), skip_group_check=True)
                        ins.then_inc(s["rt_lg"], 1)

            for name in ("rt_T", "rt_lg"):
                pe.sem_inc(s[name], RT_CREDIT)
            pe.sem_inc(s["pv_done"], PV_CREDIT)
            pe.sem_inc(s["oproj"], O_CREDIT)
            batches(pe, 0, prologue, iteration)
            route(0)
            pe.wait_ge(s["rt_copy"], RBLOCKS + RT_CREDIT)
            pe.wait_ge(s["rt_lgcopy"], RBLOCKS + RT_CREDIT)

            HALVES = ((0, 0), (0, 1), (1, 0))

            def gate_up(k, blk, f):
                for j in range(2):
                    for c in range(C):
                        base = (j * C + c) * D + f * P
                        for a, z in HALVES:
                            ins = pe.matmul(ps[2 * f + j][:, :], w0_part[k][a][:, base:base + P], xnT_part[z][:, c, blk * BLK:(blk + 1) * BLK],
                                            start=(c == 0 and (a, z) == HALVES[0]), stop=(c == C - 1 and (a, z) == HALVES[-1]), skip_group_check=True)
                ins.then_inc(s["gu_psum"], 1)

            def down(n, k, r):
                pe.wait_ge(s["h_low"], n * C + C + GU_CREDIT)
                for t in range(4):
                    pe.wait_ge(s["acc_done"], n * 4 + t - 3 + ACC_CREDIT)
                    for f in range(C):
                        base = (2 * C + f) * D
                        for a, z in HALVES:
                            ins = pe.matmul(ps[4 + t][:, 0:D], h0_part[z][:, r, f, t * P:(t + 1) * P], w0_part[k][a][:, base:base + D],
                                            start=(f == 0 and (a, z) == HALVES[0]), stop=(f == C - 1 and (a, z) == HALVES[-1]), skip_group_check=True)
                    ins.then_inc(s["down_psum"], 1)

            with pe.Fori(0, NE // 2) as i:
                for k in range(2):
                    pe.wait_ge(s["w0_low"], (i * 2 + k) * 3 + 3 + W0_CREDIT)
                    for blk in range(4):
                        n = (i * 2 + k) * 4 + blk
                        for f in range(C):
                            pe.wait_ge(s["h_done"], n * C + f - 1 + GU_CREDIT)
                            gate_up(k, blk, f)
                        if blk > 0:
                            down(n - 1, k, (blk - 1) % 2)
                    down((i * 2 + k) * 4 + 3, k, 1)

            batches(pe, 1, prologue, iteration)
            route(1)
            pe.wait_ge(s["route_vec"], ROUTE1_HOT)
            hot_v = hot16[:, :, :].rearrange("p t e -> p (t e)")
            pe.matmul(ps[4][:, 0:T * NE], below[:, :], hot_v, start=True, stop=True)
            pe.matmul(ps[5][:, 0:T * NE], ones16[:, :], hot_v, start=True, stop=True).then_inc(s["route_pe"], 1)
            pe.wait_ge(s["route_vec"], ROUTE1_SLOTS)
            pe.wait_ge(s["rt_lgcopy"], 2 * RBLOCKS + RT_CREDIT)
            def rows_transpose(i, k, e):
                pe.wait_ge(er_in[k], i * 32 + 32)
                pe.wait_ge(s["eT_done"], e + HID_CREDIT)
                for c in range(C):
                    for a in range(3):
                        n = P if a < 2 else CAP - 2 * P
                        ins = pe.transpose(ps[c][:, a * P:a * P + n], erow[0:n, k, a, c * P:(c + 1) * P], ident[0:n, 0:n])
                ins.then_inc(s["eT_psum"], 1)

            def expert(i, k, more):
                e = i * 2 + k
                pe.wait_ge(w1_in[k], i * 32 + 32)
                pe.wait_ge(s["eT_done"], e + 1 + HID_CREDIT)
                for f in range(FF // P):
                    if f % 2 == 0:
                        pe.wait_ge(s["hid_act"], e * (FF // P // 2) + f // 2 + HID_CREDIT)
                    else:
                        pe.wait_ge(s["hid_vec"], e * (FF // P // 2) + f // 2 + HID_CREDIT)
                    for c in range(C):
                        ins = pe.matmul(ps[2 + f % 2][:, 0:CAP], ring[:, k, c * FF + f * P:c * FF + (f + 1) * P],
                                        eT[:, k, c, :], start=(c == 0), stop=(c == C - 1))
                    ins.then_inc(s["hid_psum"], 1)
                if more:
                    rows_transpose(i + k, 1 - k, e + 1)
                pe.wait_ge(s["hid_act"], e * (FF // P // 2) + FF // P // 2 + HID_CREDIT)
                pe.wait_ge(s["hid_vec"], e * (FF // P // 2) + FF // P // 2 + HID_CREDIT)
                for a in range(3):
                    n = P if a < 2 else CAP - 2 * P
                    pe.wait_ge(s["eo_done"], e * 3 + a - 2 + EO_CREDIT)
                    for f in range(FF // P):
                        ins = pe.matmul(ps[4 + a][0:n, 0:D], hT[:, f, a * P:a * P + n],
                                        ring[:, k, C * FF + f * D:C * FF + (f + 1) * D],
                                        start=(f == 0), stop=(f == FF // P - 1))
                    ins.then_inc(s["eo_psum"], 1)

            rows_transpose(0, 0, 0)
            with pe.Fori(0, NE // 2 - 1) as i:
                for k in range(2):
                    expert(i, k, True)
            expert(NE // 2 - 1, 0, True)
            expert(NE // 2 - 1, 1, False)

        @block.vector
        def _(dve):
            for i in range(2):
                dve.memset(wo[i][:, :, :], 0.0).then_inc(s["wo_zero"], 1)
            dve.memset(xn_all[:, 0, :], 0.0).then_inc(s["wo_zero"], 1)
            dve.memset(v[:, :, :, :, HD:2 * HD], 1.0).then_inc(s["ones_set"], 1)
            dve.memset(all_ok[:, :], 1).then_inc(s["ones_set"], 1)

            def norm_stats(b, at):
                for t in range(QC):
                    dve.bn_stats(stats[:, t, :], xs[:, bass.ds(at * QC + t, 1), :].rearrange("p a d -> p (a d)")).then_inc(s["ln"], 1)
                dve.wait_ge(s["ln"], b.n * 4 + 2)
                settle(dve)
                for t in range(QC):
                    dve.bn_aggr(mean_var[:, t, :], stats[:, t, :]).then_inc(s["ln"], 1)

            def norm_apply(b, at):
                dve.wait_ge(s["rstd_ready"], (b.n + 1) * ROOT_STEPS)
                wait(dve, "xnT_psum", b.n - 1)
                for t in range(QC):
                    dve.tensor_scalar(xn[:, b.p, t, :], xs[:, bass.ds(at * QC + t, 1), :].rearrange("p a d -> p (a d)"),
                                      mean_var[:, t, 0:1], rstd[:, t:t + 1], ALU.subtract, ALU.mult).then_inc(s["xn_ready"], 1)

            def k_evac(b, at, layer):
                dve.wait_ge(s["k_psum"], b.n + 1)
                wait(dve, "ks_pool", b.n * 2)
                ok = all_ok[:, :] if layer == 0 else key_ok[:, bass.ds(at * S, S)]
                for c in range(C):
                    dve.scalar_tensor_tensor(out=kf[:, c, :], in0=misc[:, c * S:(c + 1) * S], scalar=bk[layer][:, c:c + 1], in1=ok,
                                             op0=ALU.add, op1=ALU.mult).then_inc(s["kf_ready"], 1)

            def v_evac(b, layer):
                dve.wait_ge(s["v_psum"], b.n + 1)
                dve.tensor_tensor(v[:, b.p, :, :, 0:HD], misc[:, :].rearrange("p (t h d) -> p t h d", t=QC, h=H),
                                  bv[layer][:, :].rearrange("p (o h d) -> p o h d", o=1, h=H).broadcast_to([P, QC, H, HD]), ALU.add).then_inc(s["v_ready"], 1)

            def reduce_max(b, g):
                for k in range(4):
                    pair, c = 2 * g + k // 2, k % 2
                    dve.wait_ge(s["max_psum"], b.n * MAXU + 4 * g + k + 1)
                    dve.tensor_reduce(mx[:, c, 2 * pair:2 * pair + 2], mps[k % 2][:, :].rearrange("p (h s) -> p h s", h=2),
                                      AX_X, ALU.max).then_inc(s["mx_done"], 1)

            def split_max(b):
                dve.wait_ge(s["mx_done"], b.n * MAXU + MAXU)
                wait(dve, "mT_psum", b.n)
                dve.tensor_scalar(m_split[:, :, 0, :], mx[:, :, :], -1.0, None, ALU.mult).then_inc(s["m_chain"], 1)
                dve.wait_ge(s["m_chain"], b.n * 4 + 1)
                dve.scalar_tensor_tensor(out=m_rest[:, :, :], in0=mx[:, :, :], scalar=-1.0, in1=m_split[:, :, 0, :],
                                         op0=ALU.mult, op1=ALU.subtract).then_inc(s["m_chain"], 1)
                dve.wait_ge(s["m_chain"], b.n * 4 + 2)
                dve.tensor_copy(m_split[:, :, 1, :], m_rest[:, :, :]).then_inc(s["m_chain"], 1)
                dve.wait_ge(s["m_chain"], b.n * 4 + 3)
                dve.tensor_tensor(m_split[:, :, 2, :], m_rest[:, :, :], m_split[:, :, 1, :], ALU.subtract).then_inc(s["m_chain"], 1)

            def max_evac(b):
                dve.wait_ge(s["mT_psum"], b.n + 1)
                wait(dve, "m_written", b.n * 16)
                dve.tensor_copy(m_T[:, :], misc[0:TERM * H, :].bitcast(BF16)[:, 0:S]).then_inc(s["mT_ready"], 1)

            def normalise(b, g):
                dve.wait_ge(s["pv_done"], b.n * UNITS + 2 * g + 2 + PV_CREDIT)
                dve.wait_ge(s["o_ready"], b.n * G + g + O_CREDIT)
                dve.transpose(oT[:, :, :].rearrange("p a r -> p (a r)"), pv_bank[:, 0:S]).then_inc(s["o_read"], 1)
                dve.wait_ge(s["o_read"], b.n * G + g + 1 + O_CREDIT)
                dve.reciprocal(o_inv[:, :], oT[:, :, HD]).then_inc(s["o_chain"], 1)
                dve.wait_ge(s["o_chain"], b.n * 2 * G + 2 * g + 1)
                dve.tensor_tensor(oT[:, :, :], oT[:, :, :], o_inv[:, :].rearrange("p (a o) -> p a o", o=1).broadcast_to([P, S // 32, 32]), ALU.mult).then_inc(s["o_chain"], 1)
                dve.wait_ge(s["o_chain"], b.n * 2 * G + 2 * g + 2)
                if g == 0:
                    dve.wait_ge(s["oproj"], b.n + O_CREDIT)
                dve.transpose(osb[:, g, :], oT[:, :, :].rearrange("p a r -> p (a r)")).then_inc(s["o_ready"], 1)

            def residual(b, at):
                dve.wait_ge(s["oproj"], b.n + 1 + O_CREDIT)
                xv = xs[:, bass.ds(at * QC, QC), :]
                dve.tensor_tensor(xv, o_bank[:, :].rearrange("p (t d) -> p t d", t=QC), xv, ALU.add).then_inc(s["resid"], 1)
                dve.wait_ge(s["resid"], b.n + 1 + O_CREDIT)
                settle(dve)
                for t in range(QC):
                    dve.bn_stats(stats_all[:, bass.ds(at * QC + t, 1), :].rearrange("p a k -> p (a k)"),
                                 xs[:, bass.ds(at * QC + t, 1), :].rearrange("p a d -> p (a d)")).then_inc(s["rt_stats"], 1)

            def prologue(layer):
                base = layer * B // 2
                if layer == 0:
                    dve.wait_ge(s["x_in0"], 32)
                    dve.wait_ge(s["ones_set"], 2)
                else:
                    dve.wait_ge(s["acc_done"], FFN0_ACC)
                    dve.wait_ge(s["valid_in"], 32)
                dve.wait_ge(weights_in[layer][0], 16 * 6)
                b0, b1 = Batch(base, 0), Batch(base, 1)
                norm_stats(b0, 0)
                k_evac(b0, 0, layer)
                norm_apply(b0, 0)
                norm_stats(b1, 1)
                k_evac(b1, 1, layer)
                norm_apply(b1, 1)
                b = Batch(base, 0)
                for g in range(G):
                    reduce_max(b, g)
                split_max(b)
                max_evac(b)
                v_evac(b, layer)
                if layer == 0:
                    dve.wait_ge(s["x_in"], 16)

            def iteration(layer, b, at, more, prep):
                b1, b2 = b.plus(1), b.plus(2)
                if prep:
                    norm_stats(b2, at + 2)
                if more:
                    reduce_max(b1, 0)
                if prep:
                    k_evac(b2, at + 2, layer)
                if more:
                    reduce_max(b1, 1)
                if prep:
                    norm_apply(b2, at + 2)
                if more:
                    reduce_max(b1, 2)
                normalise(b, 0)
                if more:
                    reduce_max(b1, 3)
                    split_max(b1)
                normalise(b, 1)
                if more:
                    max_evac(b1)
                normalise(b, 2)
                normalise(b, 3)
                residual(b, at)
                if more:
                    v_evac(b1, layer)

            def route(layer):
                dve.wait_ge(s["rt_stats"], (layer + 1) * T)
                for t in range(T):
                    dve.bn_aggr(mv_all[:, t, :], stats_all[:, t, :]).then_inc(s["rt_ln"], 1)
                dve.wait_ge(s["rt_rstd"], (layer + 1) * ROOT_STEPS)
                with dve.Fori(0, RBLOCKS // 2) as i:
                    for k in range(2):
                        n = i * 2 + k + layer * RBLOCKS
                        dve.wait_ge(s["rt_T"], n * 2 - 2 + RT_CREDIT)
                        dve.wait_ge(s["rt_copy"], n - 1 + RT_CREDIT)
                        settle(dve)
                        for t in range(RB):
                            tile = (i * 2 + k) * RB + t
                            dve.tensor_scalar(rn[:, k, t, :], xs[:, bass.ds(tile, 1), :].rearrange("p a d -> p (a d)"),
                                              mv_all[:, bass.ds(tile, 1), 0:1].rearrange("p a o -> p (a o)"), rstd_all[:, bass.ds(tile, 1)],
                                              ALU.subtract, ALU.mult).then_inc(s["rt_xn"], 1)
                    for k in range(2):
                        n = i * 2 + k + layer * RBLOCKS
                        if layer == 0:
                            dve.wait_ge(s["rt_Tcopy"], n * 2 + 2 + RT_CREDIT)
                            hi, lo = [a[:, :, bass.ds((i * 2 + k) * RB * P, RB * P)].rearrange("p c (t s) -> p t c s", t=RB) for a in xnT_part]
                            dve.tensor_copy(hi, rnT[:, k, :, :, :]).then_inc(s["rt_high"], 1)
                            dve.wait_ge(s["rt_high"], n + 1)
                            settle(dve)
                            dve.tensor_tensor(lo, rnT[:, k, :, :, :], hi, ALU.subtract).then_inc(s["rt_copy"], 1)
                        else:
                            dve.wait_ge(s["rt_xn"], n * RB + RB)
                            dve.tensor_copy(xn_all[:, bass.ds((i * 2 + k) * RB, RB), :], rn[:, k, :, :]).then_inc(s["rt_copy"], 1)
                dve.wait_ge(s["rt_lgcopy"], (layer + 1) * RBLOCKS + RT_CREDIT)
                dve.wait_ge(s["rt_copy"], (layer + 1) * RBLOCKS + RT_CREDIT)

            route_count = [0]

            def link(ins):
                ins.then_inc(s["route_vec"], 1)
                route_count[0] += 1
                dve.wait_ge(s["route_vec"], route_count[0])

            def bc(a):
                return a.rearrange("p (t o) -> p t o", o=1).broadcast_to([P, T, NE])

            def per_e(a):
                return a.rearrange("p (o e) -> p o e", o=1).broadcast_to([P, T, NE])

            for name in ("o_read", "o_ready", "resid"):
                dve.sem_inc(s[name], O_CREDIT)
            dve.sem_inc(s["rt_copy"], RT_CREDIT)
            dve.sem_inc(s["hid_vec"], HID_CREDIT)
            batches(dve, 0, prologue, iteration)
            route(0)
            dve.wait_ge(s["w0_in"], 48)
            for j in range(3):
                part = slice(j * C * D, (j + 1) * C * D)
                dve.tensor_copy(w0_part[0][0][:, part], w0_raw[:, part]).then_inc(s["w0_high"], 1)
            dve.wait_ge(s["router_bias_in"], 16)
            link(dve.tensor_tensor(lgb[:, :, :], lg[:, :, :], per_e(br[:, :]), ALU.add))
            for t in range(T):
                ins = dve.max(top[:, t, :], lgb[:, t, :])
            link(ins)
            for t in range(T):
                ins = dve.max_index(top_i[:, t, :], top[:, t, :], lgb[:, t, :])
            link(ins)
            for k in range(2):
                link(dve.tensor_copy(pick[:, k, :], top_i[:, :, k]))
                link(dve.tensor_tensor(hot[:, k, :, :], per_e(iota8[:, :]), bc(pick[:, k, :]), ALU.is_equal))
            link(dve.tensor_tensor(wts[:, 0, :], top[:, :, 1], top[:, :, 0], ALU.subtract))
            assert route_count[0] == ROUTE0_DIFF
            dve.wait_ge(s["route_act"], 1)
            link(dve.tensor_scalar(wts[:, 2, :], wts[:, 1, :], 1.0, None, ALU.add))
            link(dve.reciprocal(wts[:, 3, :], wts[:, 2, :]))
            link(dve.tensor_tensor(wts[:, 2, :], wts[:, 1, :], wts[:, 3, :], ALU.mult))
            link(dve.tensor_tensor(gate[:, 0, :, :], hot[:, 0, :, :], bc(wts[:, 3, :]), ALU.mult))
            link(dve.tensor_tensor(gate[:, 1, :, :], hot[:, 1, :, :], bc(wts[:, 2, :]), ALU.mult))
            link(dve.tensor_tensor(gate[:, 0, :, :], gate[:, 0, :, :], gate[:, 1, :, :], ALU.add))

            def add_down(n, e, blk):
                for t in range(4):
                    tile = blk * 4 + t
                    dve.wait_ge(s["down_psum"], n * 4 + t + 1)
                    dve.wait_ge(s["acc_done"], n * 4 + t - T + ACC_CREDIT + 1)
                    dve.scalar_tensor_tensor(out=xs[:, tile, :], in0=ps[4 + t][:, 0:D],
                                             scalar=gate[:, 0, tile, bass.ds(e, 1)], in1=xs[:, tile, :], op0=ALU.mult, op1=ALU.add).then_inc(s["acc_done"], 1)

            dve.sem_inc(s["acc_done"], ACC_CREDIT)
            dve.sem_inc(s["h_done"], GU_CREDIT)

            def w0_high(e, k, j):
                part = slice(j * C * D, (j + 1) * C * D)
                if j == 0:
                    dve.wait_ge(s["w0_in"], (e + 1) * 48)
                dve.tensor_copy(w0_part[k][0][:, part], w0_raw[:, part]).then_inc(s["w0_high"], 1)

            def expert0(i, k, more):
                e = i * 2 + k
                for blk in range(T // 4):
                    n = e * 4 + blk
                    for f in range(C):
                        dve.wait_ge(s["silu_done"], n * C + f + 1)
                        dve.wait_ge(s["h_low"], n * C + f - 1 + GU_CREDIT)
                        dve.tensor_tensor(h0[:, f, :], silu[:, f, :], ps[2 * f + 1][:, :], ALU.mult).then_inc(s["h_done"], 1)
                        dve.wait_ge(s["h_done"], n * C + f + 1 + GU_CREDIT)
                        dve.tensor_copy(h0_part[0][:, blk % 2, f, :], h0[:, f, :]).then_inc(s["h_high"], 1)
                    if blk > 0:
                        add_down(n - 1, e, blk - 1)
                        if more:
                            w0_high(e + 1, 1 - k, blk - 1)
                add_down(e * 4 + 3, e, 3)

            with dve.Fori(0, NE // 2 - 1) as i:
                for k in range(2):
                    expert0(i, k, True)
            expert0(NE // 2 - 1, 0, True)
            expert0(NE // 2 - 1, 1, False)

            batches(dve, 1, prologue, iteration)
            dve.wait_ge(s["slots_zero"], 16)
            route(1)
            for t in range(T):
                ins = dve.max(top[:, t, :], lg[:, t, :])
            link(ins)
            for t in range(T):
                ins = dve.max_index(top_i[:, t, :], top[:, t, :], lg[:, t, :])
            link(ins)
            link(dve.tensor_copy(pick[:, 0, :], top_i[:, :, 0]))
            link(dve.tensor_tensor(hot[:, 0, :, :], per_e(iota8[:, :]), bc(pick[:, 0, :]), ALU.is_equal))
            link(dve.tensor_copy(hot16[:, :, :], hot[:, 0, :, :]))
            assert route_count[0] == ROUTE1_HOT
            link(dve.tensor_tensor(gate[:, 1, :, :], lg[:, :, :], top[:, :, 0:1].broadcast_to([P, T, NE]), ALU.subtract))
            assert route_count[0] == ROUTE1_DIFF
            dve.wait_ge(s["route_act"], 2)
            link(dve.tensor_reduce(wts[:, 0, :], gate[:, 0, :, :], AX_X, ALU.add))
            link(dve.reciprocal(wts[:, 1, :], wts[:, 0, :]))
            dve.wait_ge(s["route_pe"], 1)
            link(dve.tensor_copy(cnt[:, 0, :, :], ps[5][:, 0:T * NE].rearrange("p (t e) -> p t e", t=T)))
            cur = 0
            step = 1
            while step < T:
                link(dve.tensor_tensor(cnt[:, 1 - cur, step:T, :], cnt[:, cur, step:T, :], cnt[:, cur, 0:T - step, :], ALU.add))
                link(dve.tensor_copy(cnt[:, 1 - cur, 0:step, :], cnt[:, cur, 0:step, :]))
                cur, step = 1 - cur, step * 2
            link(dve.tensor_tensor(rank[:, :, :], cnt[:, cur, :, :], ps[5][:, 0:T * NE].rearrange("p (t e) -> p t e", t=T), ALU.subtract))
            link(dve.tensor_tensor(rank[:, :, :], rank[:, :, :], ps[4][:, 0:T * NE].rearrange("p (t e) -> p t e", t=T), ALU.add))
            link(dve.tensor_tensor(rank[:, :, :], rank[:, :, :], hot[:, 0, :, :], ALU.mult))
            link(dve.tensor_reduce(pos[:, 0, :], rank[:, :, :], AX_X, ALU.add))
            link(dve.tensor_scalar(pos[:, 1, :], pos[:, 0, :], float(CAP), None, ALU.is_lt))
            link(dve.tensor_scalar(pos[:, 2, :], pos[:, 0, :], float(CAP - 1), None, ALU.min))
            link(dve.scalar_tensor_tensor(out=pos[:, 2, :], in0=pick[:, 0, :], scalar=float(CAP), in1=pos[:, 2, :], op0=ALU.mult, op1=ALU.add))
            link(dve.tensor_scalar(pos[:, 3, :], pos[:, 1, :], -float(SKIP), float(SKIP), ALU.mult, ALU.add))
            link(dve.tensor_tensor(pos[:, 3, :], pos[:, 3, :], pos[:, 2, :], ALU.add))
            link(dve.tensor_copy(slot[:, 1, :], pos[:, 2, :]))
            link(dve.tensor_copy(slot[:, 0, :], pos[:, 3, :]))
            assert route_count[0] == ROUTE1_SLOTS
            link(dve.tensor_tensor(wts[:, 2, :], wts[:, 1, :], pos[:, 1, :], ALU.mult))
            link(dve.tensor_scalar(wts[:, 3, :], pos[:, 1, :], -1.0, 1.0, ALU.mult, ALU.add))

            for t in range(T):
                dve.scalar_tensor_tensor(out=xs[:, t, :], in0=xn_all[:, t, :], scalar=wts[:, 3, t:t + 1], in1=xs[:, t, :],
                                         op0=ALU.mult, op1=ALU.add).then_inc(s["x_plus"], 1)

            with dve.Fori(0, NE // 2) as i:
                for k in range(2):
                    e = i * 2 + k
                    for f in range(1, FF // P, 2):
                        dve.wait_ge(s["hid_psum"], e * (FF // P) + f + 1)
                        dve.tensor_scalar(hT[:, f, :], ps[3][:, 0:CAP], 0.0, None, ALU.max).then_inc(s["hid_vec"], 1)
            dve.wait_ge(s["x_plus"], T)
            for t in range(T):
                dve.wait_ge(gathered[t % 8], 16 * (t // 8 + 1))
                if t >= 8:
                    dve.wait_ge(out_stored[t % 8], 16 * (t // 8))
                dve.scalar_tensor_tensor(out=fin[:, t % 8, :], in0=got[:, t % 8, :], scalar=wts[:, 2, t:t + 1], in1=xs[:, t, :],
                                         op0=ALU.mult, op1=ALU.add).then_inc(s["fin_done"], 1)


ROOT_NEWTON = 3
ROOT_STEPS = 2 + 4 * ROOT_NEWTON
GU_CREDIT, ACC_CREDIT, EO_CREDIT, HID_CREDIT = 2, T + 1, 4, 1
W0_CREDIT = 1
FFN0_ACC = ACC_CREDIT + NE * T
ROUTE0_DIFF = 8
ROUTE1_HOT = ROUTE0_DIFF + 6 + 5
ROUTE1_DIFF = ROUTE1_HOT + 1
ROUTE1_SLOTS = ROUTE1_DIFF + 3 + 8 + 4 + 7


def _by_channel(w):
    return w.reshape(w.shape[:-1] + (H, HD)).swapaxes(-1, -2).reshape(w.shape)


def kernel(**inputs):
    import concourse.bacc as _bacc
    from concourse.bass_utils import run_bass_kernel_spmd as _run

    nc = _bacc.Bacc("TRN2", target_bir_lowering=False, num_devices=1)
    a = {k: np.asarray(v) for k, v in inputs.items()}
    wkv, bkv = a["L1_xattn_Wkv"], a["L1_xattn_bkv"]
    lay = {
        "x": a["x"], "ctx_t": a["ctx_1024"].reshape(B * S, D).T,
        "mask": a["mask_Bx1xSxS2_ik1"][:, 0], "mask_t": a["mask_Bx1xSxS2_ik1"][:, 0].swapaxes(1, 2),
        "valid": a["mask_BxS2_bf1"],
        "wq0": _by_channel(a["L0_xattn_Wq"].T), "bq0": _by_channel(a["L0_xattn_bq"]),
        "wk0": _by_channel(a["L0_xattn_Wk"].T), "bk0": _by_channel(a["L0_xattn_bk"]),
        "wv0": a["L0_xattn_Wv"].T, "bv0": a["L0_xattn_bv"], "wo0": a["L0_xattn_Wo"].T, "bo0": a["L0_xattn_bo"],
        "wq1": _by_channel(a["L1_xattn_Wq"]), "bq1": _by_channel(a["L1_xattn_bq"]),
        "wk1": _by_channel(wkv[:, :D]), "bk1": _by_channel(bkv[:D]),
        "wv1": wkv[:, D:], "bv1": bkv[D:], "wo1": a["L1_xattn_Wp"], "bo1": a["L1_xattn_bp"],
        "wr0": a["L0_ffn_router_w"], "br0": a["L0_ffn_router_b"],
        "gate": a["L0_ffn_we_gate"], "up": a["L0_ffn_we_up"], "down": a["L0_ffn_we_down"],
        "wr1": a["L1_ffn_Wr"], "w1": a["L1_ffn_W1"], "w2": a["L1_ffn_W2"],
    }
    arrays, ap = {}, {}
    for name, arr in lay.items():
        arr = np.ascontiguousarray(arr)
        arrays[f"in_{name}"] = arr
        ap[name] = nc.dram_tensor(f"in_{name}", arr.shape, mybir.dt.from_np(arr.dtype), kind="ExternalInput").ap()
    out = nc.dram_tensor("out_0", (B, S, D), F32, kind="ExternalOutput").ap()
    attn = [{k: ap[f"{k}{i}"] for k in ("wq", "bq", "wk", "bk", "wv", "bv", "wo", "bo")} for i in range(2)]
    l0 = {"wr": ap["wr0"], "br": ap["br0"], "gate": ap["gate"], "up": ap["up"], "down": ap["down"]}
    l1 = {"wr": ap["wr1"], "w1": ap["w1"], "w2": ap["w2"]}
    build(nc, ap["x"], ap["ctx_t"], ap["mask"], ap["mask_t"], ap["valid"], attn, l0, l1, out)
    r = _run(nc, [arrays], core_ids=[0])
    return r.results[0]["out_0"]
```

```python
from contextlib import ExitStack

import numpy as np

import concourse.bass as bass
from concourse import mybir

ALU = mybir.AluOpType
ACT = mybir.ActivationFunctionType
AX_X = mybir.AxisListType.X
F32 = mybir.dt.float32
F32R = mybir.dt.float32r
BF16 = mybir.dt.bfloat16
I32 = mybir.dt.int32
U32 = mybir.dt.uint32
U8 = mybir.dt.uint8

P = 128
B, S, D = 8, 256, 256
H, HD = 16, 16
C = D // P
QC = S // P
T = B * S // P
RB = 4
RBLOCKS = T // RB
G = 4
HG = H // G
UNITS = G * QC
MAXU = H // 2 * QC
NE = 8
BLK = 512
CAP = int(1.25 * B * S / NE)
FF = 1024
TERM = 3
ROW_MASK = 6 * HD
ROW_MAX = ROW_MASK + 1
ROWS = ROW_MAX + TERM
NEG = -float((np.array([1e20], np.float32).view(np.uint32) & np.uint32(0xFFFF0000)).view(np.float32)[0])
EPS = 1e-5
TWO_ONES = float(np.array([0x3F803F80], np.uint32).view(np.float32)[0])
SCALE = (1.0 / D ** 0.5, 1.0 / HD ** 0.5)
SKIP = 1 << 20
ST_CREDIT, PV_CREDIT, O_CREDIT, RT_CREDIT = 2, 4, 1, 4
GU_CREDIT, ACC_CREDIT, EO_CREDIT, HID_CREDIT = 2, T + 1, 4, 2
W0_CREDIT = 1
PIECES = 4
PIECE = C * FF // PIECES
FFN0_ACC = ACC_CREDIT + NE * T
ROOT_NEWTON = 3
ROOT_STEPS = 2 + 4 * ROOT_NEWTON
ROUTE0_DIFF = 8
ROUTE1_HOT = ROUTE0_DIFF + 6 + 5
ROUTE1_DIFF = ROUTE1_HOT + 1
ROUTE1_SLOTS = ROUTE1_DIFF + 3 + 8 + 4 + 7


class Batch:

    def __init__(self, pair, offset):
        self.pair, self.offset = pair, offset
        self.p = offset % 2
        self.use = pair + offset // 2
        self.n = pair * 2 + offset

    def plus(self, k):
        return Batch(self.pair, self.offset + k)


def build(nc, x, ctx_t, mask, mask_t, valid, attn, l0, l1, out):
    stack = ExitStack()
    with stack:
        def sb(name, shape, dt=F32):
            return stack.enter_context(nc.sbuf_tensor(name, shape, dt))

        def sem(name):
            return stack.enter_context(nc.semaphore(name))

        def dram(name, shape, dt):
            return nc.dram_tensor(name, shape, dt, kind="Internal").ap()

        q_parts = dram("q_parts", (2 * B, TERM, D, S), BF16)
        k_parts = dram("k_parts", (2 * B, TERM, D, S), BF16)
        m_parts = dram("m_parts", (2 * B, TERM, H, S), BF16)
        slots_in = dram("slots_in", (NE * CAP, D), F32)
        slots_out = dram("slots_out", (NE * CAP, D), F32)

        xs = sb("xs", [P, T, D])
        ctxT = sb("ctxT", [P, C, B * S])
        wq = [sb(f"wq{i}", [P, C, D]) for i in range(2)]
        wk = [sb(f"wk{i}", [P, C, D]) for i in range(2)]
        wv = [sb(f"wv{i}", [P, C, D]) for i in range(2)]
        wo = [sb(f"wo{i}", [P, G // 2, D]) for i in range(2)]
        bo = [sb(f"bo{i}", [P, D]) for i in range(2)]
        bq = [sb(f"bq{i}", [P, C]) for i in range(2)]
        bk = [sb(f"bk{i}", [P, C]) for i in range(2)]
        bv = [sb(f"bv{i}", [P, D]) for i in range(2)]
        wr = [sb(f"wr{i}", [P, C, NE]) for i in range(2)]
        br = sb("br", [P, NE])
        key_ok = sb("key_ok", [P, B * S], U8)
        all_ok = sb("all_ok", [P, S], U8)
        ok_row = sb("ok_row", [1, B * S], U8)
        ident = sb("ident", [P, P])
        ident16 = sb("ident16", [P, P], BF16)
        below = sb("below", [P, P], BF16)
        ones16 = sb("ones16", [P, P], BF16)
        iota8 = sb("iota8", [P, NE])

        w0_size = 3 * C * D
        with ExitStack() as first:
            def fsb(name, shape, dt=F32):
                return first.enter_context(nc.sbuf_tensor(name, shape, dt))

            w0_part = [[fsb(f"w0_{k}{n}", [P, w0_size], F32R) for n in range(2)] for k in range(2)]
            w0_raw = fsb("w0_raw", [P, w0_size])
            fsb("w0_rest", [P, 2 * 2 * C * FF - 5 * w0_size])
            xnT_part = [fsb(f"xnT_{n}", [P, C, B * S], F32R) for n in range(2)]
            silu = fsb("silu", [P, 2, BLK])
            h0 = fsb("h0", [P, C, BLK])
            h0_high = fsb("h0_high", [P, 2, C, BLK], F32R)
            fsb("h0_rest", [P, 2 * C * BLK])
            h0_part = [h0_high, fsb("h0_low", [P, 2, C, BLK], F32R)]
        with ExitStack() as second:
            def ssb(name, shape, dt=F32):
                return second.enter_context(nc.sbuf_tensor(name, shape, dt))

            w_raw = ssb("w_raw", [P, 2, C * FF])
            w_part = [[ssb(f"w{w + 1}_{n}", [P, C * FF], F32R) for n in range(2)] for w in range(2)]
            erow = ssb("erow", [P, 2, 3, D])
            eT_part = [ssb(f"eT_{n}", [P, 2, C, CAP], F32R) for n in range(2)]
            hT_high = ssb("hT_high", [P, FF // P, CAP], F32R)
            ssb("hT_rest", [P, 4 * HG * S - FF // P * CAP])
            hT_part = [hT_high, ssb("hT_low", [P, FF // P, CAP], F32R)]
            eo = ssb("eo", [P, 2, 3, D])
        sb("w_place", [P, 4 * C * FF])
        qk = sb("qk", [P, 2, 2, H, S], BF16)
        prob = sb("prob", [P, 4, HG, S])
        xn_all = sb("xn_all", [P, T, D])

        ctxv = sb("ctxv", [P, C, S])
        mean_var = sb("mean_var", [P, T, 2])
        rstd = sb("rstd", [P, T])
        root = sb("root", [P, 3, T])
        xn = sb("xn", [P, 2, QC, D])
        xnT = sb("xnT", [P, C, S])
        kf = sb("kf", [P, C, S])
        kr = sb("kr", [P, C, S])
        ks = sb("ks", [P, TERM, C, S], BF16)
        qf = sb("qf", [P, C, S])
        qr = sb("qr", [P, C, S])
        qs = sb("qs", [P, TERM, C, S], BF16)
        mask_i = sb("mask_i", [P, 2, QC, S], I32)
        neg_row = mask_i[0:1, :, :, :].rearrange("p a c s -> p (a c s)").bitcast(BF16)
        mask_q = sb("mask_q", [P, 2, QC, S], BF16)
        mask_k = sb("mask_k", [P, 2, QC, S], BF16)
        mx = sb("mx", [P, QC, H])
        m_rest = sb("m_rest", [P, QC, H])
        m_split = sb("m_split", [P, QC, TERM, H], BF16)
        m_T = sb("m_T", [TERM * H, S], BF16)
        v = sb("v", [P, 2, QC, H, 2 * HD])
        oT = sb("oT", [P, S // 32, 32])
        o_inv = sb("o_inv", [P, S // 32])
        o_norm = sb("o_norm", [P, S // 32, 32])
        osb = sb("osb", [P, G // 2, S])

        big = qk[:, :, :, :, :].rearrange("p a b h s -> p (a b h s)").bitcast(F32)
        big_k = big.rearrange("p (a b n) -> p a b n", a=2, b=2)[:, :, 1, :]
        pr = prob[:, :, :, :].rearrange("p a h s -> p (a h s)")
        rn = pr[:, 0:2 * RB * D].rearrange("p (r t d) -> p r t d", r=2, t=RB)
        rnT = pr[:, 2 * RB * D:4 * RB * D].rearrange("p (r t c s) -> p r t c s", r=2, t=RB, c=C)
        lg = qr[:, :, :].rearrange("p c s -> p (c s)")[:, 0:T * NE].rearrange("p (t e) -> p t e", t=T)
        old_ctx = ctxT[:, :, :].rearrange("p c s -> p (c s)")
        got = old_ctx[:, 0:8 * D].rearrange("p (r d) -> p r d", r=8)
        fin = old_ctx[:, 8 * D:16 * D].rearrange("p (r d) -> p r d", r=8)
        small = [a[:, :, :].rearrange("p c s -> p (c s)") for a in (kf, kr)]
        table = T * NE
        lgb = small[0][:, 0:table].rearrange("p (t e) -> p t e", t=T)
        top = small[0][:, table:2 * table].rearrange("p (t e) -> p t e", t=T)
        top_i = small[0][:, 2 * table:3 * table].bitcast(U32).rearrange("p (t e) -> p t e", t=T)
        mv_all = small[1][:, 3 * table:3 * table + 2 * T].rearrange("p (t k) -> p t k", t=T)
        rstd_all = small[1][:, 3 * table + 2 * T:3 * table + 3 * T]
        root_all = small[1][:, 3 * table + 3 * T:3 * table + 6 * T].rearrange("p (k t) -> p k t", k=3)
        stats_all = sb("stats_all", [P, T, 6])
        pick = sb("pick", [P, 2, T])
        hot = qf[:, :, :].rearrange("p c s -> p (c s)")[:, 0:2 * table].rearrange("p (r t e) -> p r t e", r=2, t=T)
        hot16 = sb("hot16", [P, T, NE], BF16)
        wts = sb("wts", [P, 4, T])
        gate = sb("gate", [P, 2, T, NE])
        cnt = small[1][:, 0:2 * table].rearrange("p (r t e) -> p r t e", r=2, t=T)
        rank = small[1][:, 2 * table:3 * table].rearrange("p (t e) -> p t e", t=T)
        pos = sb("pos", [P, 4, T])
        slot = sb("slot", [P, 2, T], U32)

        ps = [stack.enter_context(nc.psum_tensor(f"ps{i}", [P, 512], F32)) for i in range(8)]
        misc, pv_bank = ps[7], ps[6]
        hid_bank = [ps[n] for n in (0, 1, 2, 3, 7, 2, 3, 7)]
        mps = [ps[4], ps[5]]
        o_bank = ps[4]

        names = """ones_again settled const_pool ident_done zeros_set bias_added router_bias_in ctx_in0 ctx_in x_in0 x_in valid_in
 qk_ones
            ones_set neg_done slots_zero
            ln rstd_ready xn_centred xn_ready xnT_psum xnT_ready k_psum kf_ready ks_act ks_pool k_written
            q_psum qf_ready qs_act qs_pool q_written
            mask_in mask_t_in mask_q_ready mask_k_ready
            ctxv_ready v_psum v_ready
            max_psum mx_done m_chain mT_psum mT_ready m_written
            st_ready exp_done pv_done o_read o_chain o_ready oproj resid
            rt_stats rt_high rt_ln rt_rstd rt_xn rt_T rt_Tcopy rt_copy rt_lg rt_lgcopy
            route_vec route_act route_pe
            w0_in w0_high w0_low gu_psum silu_done h_done h_high h_low down_psum acc_done
            scattered w1_in w2_in w_high w_low er_in0 er_in1 eT_psum eT_high eT_low hid_psum hid_high hid_low
            eo_psum eo_done eo_stored0 eo_stored1 x_plus fin_done""".split()
        s = {n: sem(n) for n in names}
        qk_loaded = [[sem(f"qk_loaded{p}{g}") for g in range(2)] for p in range(2)]
        m_loaded = [sem(f"m_loaded{p}") for p in range(2)]
        gathered = [sem(f"gathered{r}") for r in range(8)]
        out_stored = [sem(f"out_stored{r}") for r in range(8)]
        weights_in = [[sem(f"weights{i}{k}_in") for k in range(2)] for i in range(2)]
        w_in = [s["w1_in"], s["w2_in"]]
        er_in = [s["er_in0"], s["er_in1"]]
        eo_stored = [s["eo_stored0"], s["eo_stored1"]]
        block = stack.enter_context(nc.Block())

        def wait(eng, name, value):
            if not isinstance(value, int) or value > 0:
                eng.wait_ge(s[name] if isinstance(name, str) else name, value)

        def settle(eng):
            eng.sem_inc(s["settled"], 1)

        def qk_value(b, layer):
            return b.use * 96 + 96 if layer == 0 else (b.use - B // 2) * 112 + 96 * (B // 2) + 112

        def load_weights(eng, i, stage):
            done = weights_in[i][stage]
            if stage == 0:
                for w, name in ((wk, "wk"), (wq, "wq"), (wv, "wv")):
                    eng.dma_start(w[i][:, :, :], attn[i][name].rearrange("(c p) n -> p c n", p=P)).then_inc(done, 16)
                for w, name in ((bk, "bk"), (bq, "bq")):
                    eng.dma_start(w[i][:, :], attn[i][name].rearrange("(c p) -> p c", p=P),
                                  allow_slow_non_contiguous=True).then_inc(done, 16)
                eng.dma_start(bv[i][:, :], attn[i]["bv"].rearrange("(o n) -> o n", o=1).broadcast_to([P, D])).then_inc(done, 16)
            else:
                eng.dma_start(wo[i][:, :, :], attn[i]["wo"].rearrange("(g p) n -> p g n", p=P)).then_inc(done, 16)
                eng.dma_start(bo[i][:, :], attn[i]["bo"].rearrange("(o n) -> o n", o=1).broadcast_to([P, D])).then_inc(done, 16)
                eng.dma_start(wr[i][:, :, :], (l0, l1)[i]["wr"].rearrange("(c p) n -> p c n", p=P)).then_inc(done, 16)

        def batches(eng, layer, prologue, iteration):
            prologue(layer)
            base = layer * B // 2
            with eng.Fori(0, (B - 2) // 2) as i:
                for k in range(2):
                    iteration(layer, Batch(i + base, k), i * 2 + k, True, True)
            iteration(layer, Batch(base, B - 2), B - 2, True, False)
            iteration(layer, Batch(base, B - 1), B - 1, False, False)

        @block.sync
        def _(sp):
            sp.dma_start(ctxT[:, :, 0:2 * S], ctx_t.rearrange("(c p) s -> p c s", p=P)[:, :, 0:2 * S]).then_inc(s["ctx_in0"], 16)
            for t in range(2):
                sp.dma_start(xs[:, t * QC:(t + 1) * QC, :],
                             x[t].rearrange("(t p) d -> p t d", p=P)).then_inc(s["x_in0"], 16)
            sp.dma_start(ctxT[:, :, 2 * S:], ctx_t.rearrange("(c p) s -> p c s", p=P)[:, :, 2 * S:]).then_inc(s["ctx_in"], 16)
            sp.dma_start(xs[:, 2 * QC:, :],
                         x[2:B].rearrange("b (t p) d -> p (b t) d", p=P)).then_inc(s["x_in"], 16)

            def load_mask_q(b, at):
                wait(sp, "mask_q_ready", b.n)
                sp.dma_start(mask_i[:, 0, :, :], mask[at].rearrange("(c p) k -> p c k", p=P)).then_inc(s["mask_in"], 16)

            def load_mask_k(b, at):
                wait(sp, "mask_k_ready", b.n)
                sp.dma_start(mask_i[:, 1, :, :], mask_t[at].rearrange("(c p) q -> p c q", p=P)).then_inc(s["mask_t_in"], 16)

            def write_parts(b):
                sp.wait_ge(s["ks_pool"], b.n * 2 + 2)
                sp.dma_start(k_parts[b.n].rearrange("t (c p) s -> p t c s", p=P), ks[:, :, :, :]).then_inc(s["k_written"], 16)
                sp.wait_ge(s["qs_pool"], b.n * 2 + 2)
                sp.dma_start(q_parts[b.n].rearrange("t (c p) s -> p t c s", p=P), qs[:, :, :, :]).then_inc(s["q_written"], 16)

            def load_half(b, at, layer, half):
                sp.wait_ge(s["k_written"], b.n * 16 + 16)
                sp.wait_ge(s["q_written"], b.n * 16 + 16)
                settle(sp)
                wait(sp, "st_ready", b.n * UNITS - 2 * UNITS + (half + 1) * UNITS // 2)
                heads = slice(half * H // 2, (half + 1) * H // 2)
                for side, parts in ((0, q_parts), (1, k_parts)):
                    src = parts[b.n].rearrange("t (d h) s -> (t d) h s", h=H)
                    for to, n, frm in ((0, 3, 0), (3, 2, side), (5, 1, 2 * side)):
                        sp.dma_start(qk[to * HD:(to + n) * HD, b.p, side, heads, :],
                                     src[frm * HD:(frm + n) * HD, heads, :]).then_inc(qk_loaded[b.p][half], 16)
                if layer == 1:
                    row = neg_row[0:1, bass.ds(at * S, S)]
                    sp.dma_start(qk[ROW_MASK:ROW_MASK + 1, b.p, 1, heads, :],
                                 row.rearrange("o (a s) -> o a s", a=1).broadcast_to([1, H // 2, S])).then_inc(qk_loaded[b.p][half], 16)

            def prologue(layer):
                base = layer * B // 2
                b0, b1 = Batch(base, 0), Batch(base, 1)
                if layer == 0:
                    load_mask_q(b0, 0)
                    load_mask_k(b0, 0)
                    sp.wait_ge(s["qk_ones"], 2)
                else:
                    sp.wait_ge(s["acc_done"], FFN0_ACC)
                    sp.wait_ge(s["neg_done"], 1)
                    sp.wait_ge(s["ones_again"], 1)
                write_parts(b0)
                for half in range(2):
                    load_half(b0, 0, layer, half)
                if layer == 0:
                    load_mask_q(b1, 1)
                write_parts(b1)
                for half in range(2):
                    load_half(b1, 1, layer, half)

            def iteration(layer, b, at, more, prep):
                if layer == 0 and prep:
                    load_mask_q(b.plus(2), at + 2)
                if layer == 0 and more:
                    load_mask_k(b.plus(1), at + 1)
                if prep:
                    write_parts(b.plus(2))
                if prep:
                    for half in range(2):
                        load_half(b.plus(2), at + 2, layer, half)

            batches(sp, 0, prologue, iteration)

            sp.dma_start(key_ok[:, :], valid.rearrange("(o b) s -> o (b s)", o=1).broadcast_to([P, B * S])).then_inc(s["valid_in"], 16)
            sp.dma_start(ok_row[:, :], valid.rearrange("(o b) s -> o (b s)", o=1)).then_inc(s["valid_in"], 16)
            sp.dma_start(br[:, :], l0["br"].rearrange("(o n) -> o n", o=1).broadcast_to([P, NE])).then_inc(s["router_bias_in"], 16)
            gate_v = l0["gate"].rearrange("e (c p) f -> e p c f", p=P)
            up_v = l0["up"].rearrange("e (c p) f -> e p c f", p=P)
            down_v = l0["down"].rearrange("e (c p) f -> e p c f", p=P)
            with sp.Fori(0, NE) as e:
                sp.wait_ge(s["w0_low"], e * 3 + W0_CREDIT)
                for j, w in enumerate((gate_v, up_v, down_v)):
                    sp.dma_start(w0_raw[:, j * C * D:(j + 1) * C * D].rearrange("p (c f) -> p c f", c=C), w[e]).then_inc(s["w0_in"], 16)
            for stage in range(2):
                load_weights(sp, 1, stage)
            sp.wait_ge(s["zeros_set"], 1)
            sp.dma_start(slots_in.rearrange("(a p) d -> p a d", p=P), xn_all[:, 0:1, :].broadcast_to([P, NE * CAP // P, D])).then_inc(s["slots_zero"], 16)

            batches(sp, 1, prologue, iteration)

            w1_v = l1["w1"].rearrange("e (c p) f -> e p c f", p=P)
            w2_v = l1["w2"].rearrange("e (c p) d -> e p c d", p=P)

            def load_weights1(e):
                for w, view in enumerate((w1_v, w2_v)):
                    if not (isinstance(e, int) and e == 0):
                        sp.wait_ge(s["w_low"], e * 2 * PIECES - PIECES + w * PIECES)
                    sp.dma_start(w_raw[:, w, :].rearrange("p (c f) -> p c f", c=(C, FF // P)[w]), view[e]).then_inc(w_in[w], 16)

            def load_rows(k, e):
                sp.wait_ge(s["eT_psum"], e - 1 + HID_CREDIT)
                rows = slots_in[bass.ds(e * CAP, CAP), :]
                sp.dma_start(erow[:, k, 0:2, :], rows[0:2 * P, :].rearrange("(a p) d -> p a d", p=P)).then_inc(er_in[k], 16)
                sp.dma_start(erow[0:CAP - 2 * P, k, 2, :], rows[2 * P:CAP, :]).then_inc(er_in[k], 16)

            load_weights1(0)
            sp.wait_ge(s["scattered"], 16 * T)
            load_rows(0, 0)
            with sp.Fori(0, NE // 2 - 1) as i:
                for k in range(2):
                    load_rows(1 - k, i * 2 + k + 1)
                    load_weights1(i * 2 + k + 1)
            load_rows(1, NE - 1)
            load_weights1(NE - 1)
            for t in range(T):
                sp.wait_ge(s["fin_done"], t + 1)
                sp.dma_start(out[t // QC, (t % QC) * P:(t % QC + 1) * P, :], fin[:, t % 8, :]).then_inc(out_stored[t % 8], 16)
            for r in range(8):
                sp.wait_ge(out_stored[r], 16 * T // 8)

        @block.gpsimd
        def _(pool):
            for m in (ident, ident16):
                pool.memset(m[:, :], 0.0).then_inc(s["const_pool"], 1)
            pool.memset(below[:, :], 1.0).then_inc(s["const_pool"], 1)
            pool.memset(ones16[:, :], 1.0).then_inc(s["const_pool"], 1)
            pool.wait_ge(s["const_pool"], 4)
            for m in (ident, ident16):
                pool.affine_select(out=m[:, :], in_=m[:, :], compare_op=ALU.not_equal, fill=1.0, base=0,
                                   pattern=[[-1, P]], channel_multiplier=1).then_inc(s["ident_done"], 1)
            pool.affine_select(out=below[:, :], in_=below[:, :], compare_op=ALU.is_gt, fill=0.0, base=0,
                               pattern=[[1, P]], channel_multiplier=-1).then_inc(s["ident_done"], 1)
            pool.wait_ge(s["ident_done"], 3)
            pool.memset(big[ROW_MASK:P, :], TWO_ONES).then_inc(s["qk_ones"], 1)
            pool.wait_ge(s["qk_ones"], 1)
            pool.memset(big_k[ROW_MASK:ROW_MASK + 1, :, :], 0.0).then_inc(s["qk_ones"], 1)
            pool.wait_ge(s["qk_ones"], 2)
            pool.iota(iota8[:, :], pattern=[[1, NE]], base=0, channel_multiplier=0,
                      allow_small_or_imprecise_dtypes=True).then_inc(s["ident_done"], 1)

            def inverse_root(chain, start, root, mean_var, rstd):
                var, y, t = root[:, 0, :], root[:, 1, :], root[:, 2, :]
                settle(pool)
                pool.tensor_scalar(var, mean_var[:, :, 1], EPS, None, ALU.add).then_inc(chain, 1)
                pool.wait_ge(chain, start + 1)
                settle(pool)
                pool.tensor_scalar(y.bitcast(I32), var.bitcast(I32), -0.5, float(0x5F3759DF), ALU.mult, ALU.add).then_inc(chain, 1)
                for k in range(ROOT_NEWTON):
                    pool.wait_ge(chain, start + 2 + 4 * k)
                    pool.tensor_tensor(t, y, y, ALU.mult).then_inc(chain, 1)
                    pool.wait_ge(chain, start + 3 + 4 * k)
                    pool.tensor_tensor(t, t, var, ALU.mult).then_inc(chain, 1)
                    pool.wait_ge(chain, start + 4 + 4 * k)
                    settle(pool)
                    pool.tensor_scalar(t, t, -0.5, 1.5, ALU.mult, ALU.add).then_inc(chain, 1)
                    pool.wait_ge(chain, start + 5 + 4 * k)
                    to = rstd[:, :] if k == ROOT_NEWTON - 1 else y
                    pool.tensor_tensor(to, y, t, ALU.mult).then_inc(chain, 1)

            def inv_std(layer, a, z):
                pool.wait_ge(s["ln"], (layer * T + z) * 2)
                inverse_root(s["rstd_ready"], (layer * 2 + (a > 0)) * ROOT_STEPS, root[:, :, a:z], mean_var[:, a:z, :], rstd[:, a:z])

            def norm_apply(b, at):
                wait(pool, "xnT_psum", b.n - 1)
                settle(pool)
                mean = mean_var[:, bass.ds(at * QC, QC), 0:1].broadcast_to([P, QC, D])
                scale = rstd[:, bass.ds(at * QC, QC)].rearrange("p (t o) -> p t o", o=1).broadcast_to([P, QC, D])
                pool.tensor_tensor(xn[:, b.p, :, :], xs[:, bass.ds(at * QC, QC), :], mean, ALU.subtract).then_inc(s["xn_centred"], 1)
                pool.wait_ge(s["xn_centred"], b.n + 1)
                settle(pool)
                pool.tensor_tensor(xn[:, b.p, :, :], xn[:, b.p, :, :], scale, ALU.mult).then_inc(s["xn_ready"], 1)

            def k_rest(b):
                pool.wait_ge(s["ks_act"], b.n * 2 + 1)
                pool.tensor_tensor(kr[:, :, :], kf[:, :, :], ks[:, 2, :, :], ALU.subtract).then_inc(s["ks_pool"], 1)
                pool.wait_ge(s["ks_act"], b.n * 2 + 2)
                pool.tensor_tensor(ks[:, 0, :, :], kr[:, :, :], ks[:, 1, :, :], ALU.subtract).then_inc(s["ks_pool"], 1)

            def q_rest(b):
                pool.wait_ge(s["qs_act"], b.n * 2 + 1)
                pool.tensor_tensor(qr[:, :, :], qf[:, :, :], qs[:, 0, :, :], ALU.subtract).then_inc(s["qs_pool"], 1)
                pool.wait_ge(s["qs_act"], b.n * 2 + 2)
                pool.tensor_tensor(qs[:, 2, :, :], qr[:, :, :], qs[:, 1, :, :], ALU.subtract).then_inc(s["qs_pool"], 1)

            def copy_ctx(b, at):
                wait(pool, "v_psum", b.n)
                pool.tensor_copy(ctxv[:, :, :], ctxT[:, :, bass.ds(at * S, S)]).then_inc(s["ctxv_ready"], 1)

            def add_bias(b, at, layer):
                pool.wait_ge(s["xn_ready"], b.n + 1)
                settle(pool)
                xv = xs[:, bass.ds(at * QC, QC), :]
                pool.tensor_tensor(xv, xv, bo[layer][:, :].rearrange("p (o d) -> p o d", o=1).broadcast_to([P, QC, D]), ALU.add).then_inc(s["bias_added"], 1)

            def mask_for_q(b):
                pool.wait_ge(s["mask_in"], b.n * 16 + 16)
                wait(pool, "mx_done", b.n * MAXU - MAXU)
                settle(pool)
                pool.tensor_scalar(mask_q[:, b.p, :, :], mask_i[:, 0, :, :], 0.0, NEG, ALU.is_equal, ALU.mult).then_inc(s["mask_q_ready"], 1)

            def mask_for_k(b):
                pool.wait_ge(s["mask_t_in"], b.n * 16 + 16)
                wait(pool, "st_ready", b.n * UNITS - UNITS + 1)
                settle(pool)
                pool.tensor_scalar(mask_k[:, b.p, :, :], mask_i[:, 1, :, :], 0.0, NEG, ALU.is_equal, ALU.mult).then_inc(s["mask_k_ready"], 1)

            def prologue(layer):
                base = layer * B // 2
                b0, b1 = Batch(base, 0), Batch(base, 1)
                inv_std(layer, 0, 2 * QC)
                pool.wait_ge(s["rstd_ready"], (layer * 2 + 1) * ROOT_STEPS)
                norm_apply(b0, 0)
                norm_apply(b1, 1)
                if layer == 0:
                    mask_for_q(b0)
                k_rest(b0)
                q_rest(b0)
                k_rest(b1)
                inv_std(layer, 2 * QC, T)
                pool.wait_ge(s["rstd_ready"], (layer * 2 + 2) * ROOT_STEPS)
                if layer == 0:
                    pool.wait_ge(s["ctx_in0"], 16)
                q_rest(b1)
                copy_ctx(b0, 0)
                if layer == 0:
                    mask_for_k(b0)
                    mask_for_q(b1)
                pool.wait_ge(weights_in[layer][1], 16 * 3)
                if layer == 0:
                    pool.wait_ge(s["ctx_in"], 16)

            def iteration(layer, b, at, more, prep):
                if prep:
                    norm_apply(b.plus(2), at + 2)
                    k_rest(b.plus(2))
                if more:
                    copy_ctx(b.plus(1), at + 1)
                if prep:
                    q_rest(b.plus(2))
                add_bias(b, at, layer)
                if layer == 0 and more:
                    mask_for_k(b.plus(1))
                if layer == 0 and prep:
                    mask_for_q(b.plus(2))

            def route_std(layer):
                pool.wait_ge(s["rt_ln"], (layer + 1) * T)
                inverse_root(s["rt_rstd"], layer * ROOT_STEPS, root_all, mv_all, rstd_all)

            pool.sem_inc(s["w0_low"], W0_CREDIT)
            pool.sem_inc(s["h_low"], GU_CREDIT)
            batches(pool, 0, prologue, iteration)
            route_std(0)
            pool.wait_ge(s["valid_in"], 32)
            pool.tensor_scalar(neg_row[:, :], ok_row[:, :], 0.0, NEG, ALU.is_equal, ALU.mult).then_inc(s["neg_done"], 1)
            def w0_low(e, k, j):
                part = slice(j * C * D, (j + 1) * C * D)
                pool.wait_ge(s["w0_high"], e * 3 + j + 1)
                pool.tensor_tensor(w0_part[k][1][:, part], w0_raw[:, part], w0_part[k][0][:, part], ALU.subtract).then_inc(s["w0_low"], 1)

            def expert0(i, k, more):
                e = i * 2 + k
                for blk in range(T // 4):
                    for f in range(C):
                        pool.wait_ge(s["h_high"], (e * 4 + blk) * C + f + 1)
                        pool.tensor_tensor(h0_part[1][:, blk % 2, f, :], h0[:, f, :], h0_part[0][:, blk % 2, f, :], ALU.subtract).then_inc(s["h_low"], 1)
                    if more and blk > 0:
                        w0_low(e + 1, 1 - k, blk - 1)

            for j in range(3):
                w0_low(0, 0, j)
            with pool.Fori(0, NE // 2 - 1) as i:
                for k in range(2):
                    expert0(i, k, True)
            expert0(NE // 2 - 1, 0, True)
            expert0(NE // 2 - 1, 1, False)
            batches(pool, 1, prologue, iteration)
            route_std(1)
            pool.wait_ge(s["route_vec"], ROUTE1_SLOTS)
            pool.wait_ge(s["rt_copy"], 2 * RBLOCKS + RT_CREDIT)
            for t in range(T):
                pool.indirect_dma_start(slots_in[:, :], bass.IndirectOffsetOnAxis(ap=slot[:, 0, t:t + 1], axis=0),
                                        xn_all[:, t, :], None, bounds_check=NE * CAP - 1, oob_is_err=False).then_inc(s["scattered"], 16)
            for k in range(2):
                pool.wait_ge(eo_stored[k], 32 * (NE // 2) + HID_CREDIT)
            for t in range(T):
                if t >= 8:
                    pool.wait_ge(s["fin_done"], t - 7)
                pool.indirect_dma_start(got[:, t % 8, :], None, slots_out[:, :],
                                        bass.IndirectOffsetOnAxis(ap=slot[:, 1, t:t + 1], axis=0)).then_inc(gathered[t % 8], 16)

        @block.scalar
        def _(act):
            load_weights(act, 0, 0)
            load_weights(act, 0, 1)
            act.sem_inc(s["exp_done"], ST_CREDIT)
            act.sem_inc(s["eo_done"], EO_CREDIT)
            for k in range(2):
                act.sem_inc(eo_stored[k], HID_CREDIT)
            def write_max(b):
                act.wait_ge(s["mT_ready"], b.n + 1)
                settle(act)
                act.dma_start(m_parts[b.n].rearrange("t h s -> (t h) s"), m_T[:, :]).then_inc(s["m_written"], 16)

            def load_max(b):
                act.wait_ge(s["m_written"], b.n * 16 + 16)
                settle(act)
                wait(act, "st_ready", b.n * UNITS - UNITS + 1)
                settle(act)
                act.dma_start(qk[ROW_MAX:ROWS, b.p, 0, :, :],
                             m_parts[b.n]).then_inc(m_loaded[b.p], 16)

            def k_high(b):
                act.wait_ge(s["kf_ready"], b.n * 2 + 2)
                wait(act, "k_written", b.n * 16)
                act.activation(ks[:, 2, :, :], kf[:, :, :], ACT.Copy).then_inc(s["ks_act"], 1)

            def k_mid(b):
                act.wait_ge(s["ks_pool"], b.n * 2 + 1)
                act.activation(ks[:, 1, :, :], kr[:, :, :], ACT.Copy).then_inc(s["ks_act"], 1)

            def q_evac(b, layer):
                act.wait_ge(s["q_psum"], b.n + 1)
                wait(act, "qs_pool", b.n * 2)
                for c in range(C):
                    act.activation(qf[:, c, :], misc[:, c * S:(c + 1) * S], ACT.Identity, bias=bq[layer][:, c:c + 1]).then_inc(s["qf_ready"], 1)

            def q_high(b):
                act.wait_ge(s["qf_ready"], b.n * 2 + 2)
                wait(act, "q_written", b.n * 16)
                act.activation(qs[:, 0, :, :], qf[:, :, :], ACT.Copy).then_inc(s["qs_act"], 1)

            def q_mid(b):
                act.wait_ge(s["qs_pool"], b.n * 2 + 1)
                act.activation(qs[:, 1, :, :], qr[:, :, :], ACT.Copy).then_inc(s["qs_act"], 1)

            def xnT_evac(b):
                act.wait_ge(s["xnT_psum"], b.n + 1)
                wait(act, "q_psum", b.n)
                act.activation(xnT[:, :, :], misc[:, :].rearrange("p (c s) -> p c s", c=C), ACT.Copy).then_inc(s["xnT_ready"], 1)

            def exp(b, u, layer):
                unit = b.n * UNITS + u
                act.wait_ge(s["st_ready"], unit + 1)
                act.wait_ge(s["pv_done"], unit - 3 + PV_CREDIT)
                for half in range(2):
                    ins = act.activation(prob[:, u % 4, 2 * half:2 * half + 2, :],
                                         ps[2 * (u % 2) + half][:, :].rearrange("p (h s) -> p h s", h=2), ACT.Exp, scale=SCALE[layer])
                ins.then_inc(s["exp_done"], 1)

            def prologue(layer):
                for k in range(2):
                    b = Batch(layer * B // 2, k)
                    if k == 0:
                        act.wait_ge(weights_in[layer][0], 16 * 6)
                    k_high(b)
                    xnT_evac(b)
                    k_mid(b)
                    q_evac(b, layer)
                    q_high(b)
                    q_mid(b)
                write_max(Batch(layer * B // 2, 0))
                load_max(Batch(layer * B // 2, 0))

            def iteration(layer, b, at, more, prep):
                b2 = b.plus(2)
                exp(b, 0, layer)
                exp(b, 1, layer)
                if prep:
                    k_high(b2)
                    xnT_evac(b2)
                exp(b, 2, layer)
                if prep:
                    k_mid(b2)
                    q_evac(b2, layer)
                    q_high(b2)
                exp(b, 3, layer)
                if prep:
                    q_mid(b2)
                exp(b, 4, layer)
                for u in range(5, UNITS):
                    if more and u == UNITS - 1:
                        write_max(b.plus(1))
                    exp(b, u, layer)
                if more:
                    load_max(b.plus(1))

            def route_evac(layer):
                with act.Fori(0, RBLOCKS // 2) as i:
                    for k in range(2):
                        n = i * 2 + k + layer * RBLOCKS
                        act.wait_ge(s["rt_lg"], n - 1 + RT_CREDIT)
                        act.wait_ge(s["rt_copy"], n - 1 + RT_CREDIT)
                        for half in range(2):
                            act.wait_ge(s["rt_T"], n * 2 + half + 1 + RT_CREDIT)
                            act.activation(rnT[:, k, 2 * half:2 * half + 2, :, :],
                                           ps[2 * k + half][:, :].rearrange("p (t c s) -> p t c s", t=2, c=C), ACT.Copy).then_inc(s["rt_Tcopy"], 1)
                    for k in range(2):
                        n = i * 2 + k + layer * RBLOCKS
                        act.wait_ge(s["rt_lg"], n + 1 + RT_CREDIT)
                        act.activation(lg[:, bass.ds((i * 2 + k) * RB, RB), :],
                                       ps[4 + k][:, 0:RB * NE].rearrange("p (a e) -> p a e", a=RB), ACT.Copy).then_inc(s["rt_lgcopy"], 1)

            for name in ("rt_Tcopy", "rt_lgcopy"):
                act.sem_inc(s[name], RT_CREDIT)
            batches(act, 0, prologue, iteration)
            route_evac(0)
            act.wait_ge(s["route_vec"], ROUTE0_DIFF)
            act.activation(wts[:, 1, :], wts[:, 0, :], ACT.Exp).then_inc(s["route_act"], 1)
            with act.Fori(0, NE * T // 4) as i:
                for f in range(C):
                    n = i * C + f
                    act.wait_ge(s["gu_psum"], n + 1)
                    act.wait_ge(s["h_done"], n + GU_CREDIT - 1)
                    act.activation(silu[:, f, :], ps[2 * f][:, :], ACT.Silu).then_inc(s["silu_done"], 1)
            batches(act, 1, prologue, iteration)
            route_evac(1)
            act.wait_ge(s["route_vec"], ROUTE1_DIFF)
            act.activation(gate[:, 0, :, :], gate[:, 1, :, :], ACT.Exp).then_inc(s["route_act"], 1)
            act.wait_ge(s["route_vec"], ROUTE1_SLOTS)
            def w_high(e, w, piece):
                if piece == 0:
                    act.wait_ge(w_in[w], (e + 1) * 16)
                    if not (isinstance(e, int) and e == 0):
                        act.wait_ge(*((s["hid_psum"], e * (FF // P)) if w == 0 else (s["eo_psum"], e * 3)))
                part = slice(piece * PIECE, (piece + 1) * PIECE)
                act.activation(w_part[w][0][:, part], w_raw[:, w, part], ACT.Copy).then_inc(s["w_high"], 1)

            def rows_evac(k, e):
                act.wait_ge(s["eT_psum"], e + 1 + HID_CREDIT)
                for c in range(C):
                    ins = act.activation(eT_part[0][:, k, c, :], ps[c][:, 0:CAP], ACT.Copy)
                ins.then_inc(s["eT_high"], 1)

            def expert(i, k, more):
                e = i * 2 + k
                for f in range(FF // P):
                    act.wait_ge(s["hid_psum"], e * (FF // P) + f + 1)
                    act.activation(hT_part[0][:, f, :], hid_bank[f][:, 0:CAP], ACT.Relu).then_inc(s["hid_high"], 1)
                    if f % 2 == 0:
                        w_high(e, 1, f // 2)
                if more:
                    rows_evac(1 - k, e + 1)
                    for piece in range(PIECES):
                        w_high(e + 1, 0, piece)
                act.wait_ge(eo_stored[k], i * 32 + HID_CREDIT)
                for a in range(3):
                    n = P if a < 2 else CAP - 2 * P
                    act.wait_ge(s["eo_psum"], e * 3 + a + 1)
                    act.activation(eo[0:n, k, a, :], ps[4 + a][0:n, 0:D], ACT.Copy).then_inc(s["eo_done"], 1)
                act.wait_ge(s["eo_done"], e * 3 + 3 + EO_CREDIT)
                rows = slots_out[bass.ds(e * CAP, CAP), :]
                act.dma_start(rows[0:2 * P, :].rearrange("(a p) d -> p a d", p=P), eo[:, k, 0:2, :]).then_inc(eo_stored[k], 16)
                act.dma_start(rows[2 * P:CAP, :], eo[0:CAP - 2 * P, k, 2, :]).then_inc(eo_stored[k], 16)

            for piece in range(PIECES):
                w_high(0, 0, piece)
            rows_evac(0, 0)
            with act.Fori(0, NE // 2 - 1) as i:
                for k in range(2):
                    expert(i, k, True)
            expert(NE // 2 - 1, 0, True)
            expert(NE // 2 - 1, 1, False)

        @block.tensor
        def _(pe):
            def k_matmul(at, layer):
                for m in range(C):
                    for c in range(C):
                        ins = pe.matmul(misc[:, m * S:(m + 1) * S], wk[layer][:, c, m * P:(m + 1) * P],
                                        ctxT[:, c, bass.ds(at * S, S)], start=(c == 0), stop=(c == C - 1), skip_group_check=True)
                ins.then_inc(s["k_psum"], 1)

            def k_proj(b, at, layer):
                wait(pe, "v_ready", b.n - 1)
                k_matmul(at, layer)

            def xn_transpose(b):
                pe.wait_ge(s["xn_ready"], b.n + 1)
                pe.wait_ge(s["kf_ready"], b.n * 2 + 2)
                for c in range(C):
                    for t in range(QC):
                        ins = pe.transpose(misc[:, c * S + t * P:c * S + (t + 1) * P], xn[:, b.p, t, c * P:(c + 1) * P], ident[:, :])
                ins.then_inc(s["xnT_psum"], 1)

            def q_proj(b, layer):
                pe.wait_ge(s["xnT_ready"], b.n + 1)
                for m in range(C):
                    for c in range(C):
                        ins = pe.matmul(misc[:, m * S:(m + 1) * S], wq[layer][:, c, m * P:(m + 1) * P],
                                        xnT[:, c, :], start=(c == 0), stop=(c == C - 1), skip_group_check=True)
                ins.then_inc(s["q_psum"], 1)

            def v_proj(b, layer):
                pe.wait_ge(s["ctxv_ready"], b.n + 1)
                pe.wait_ge(s["mT_ready"], b.n + 1)
                for t in range(QC):
                    for c in range(C):
                        ins = pe.matmul(misc[:, t * D:(t + 1) * D], ctxv[:, c, t * P:(t + 1) * P], wv[layer][:, c, :],
                                        start=(c == 0), stop=(c == C - 1), skip_group_check=True)
                ins.then_inc(s["v_psum"], 1)

            def max_unit(b, g, k, layer):
                if k == 0 and g % 2 == 0:
                    pe.wait_ge(qk_loaded[b.p][g // 2], qk_value(b, layer))
                if k == 0 and g == 0:
                    if layer == 0:
                        pe.wait_ge(s["mask_q_ready"], b.n + 1)
                    wait(pe, "resid", b.n - 1 + O_CREDIT)
                pair, c = k // 2, k % 2
                wait(pe, "mx_done", b.n * MAXU + 4 * g + k - 1)
                bank = mps[k % 2]
                for j in range(2):
                    h = g * HG + 2 * pair + j
                    ins = pe.matmul(bank[:, j * S:(j + 1) * S], qk[0:ROW_MASK + 1, b.p, 0, h, c * P:(c + 1) * P],
                                    qk[0:ROW_MASK + 1, b.p, 1, h, :], start=(j == 0), stop=(layer == 1), skip_group_check=True)
                if layer == 0:
                    ins = pe.matmul(bank[:, :].rearrange("p (h s) -> p h s", h=2), ident16[:, :],
                                    mask_q[:, b.p, c:c + 1, :].broadcast_to([P, 2, S]), start=False, stop=True, skip_group_check=True)
                ins.then_inc(s["max_psum"], 1)

            def max_transpose(b):
                pe.wait_ge(s["m_chain"], b.n * 4 + 4)
                wait(pe, "qf_ready", b.n * 2 + 2)
                settle(pe)
                for c in range(QC):
                    ins = pe.transpose(misc[0:TERM * H, :].bitcast(BF16)[:, c * P:(c + 1) * P],
                                       m_split[:, c, :, :].rearrange("p t h -> p (t h)"), ident16[:, :])
                ins.then_inc(s["mT_psum"], 1)

            def scores(b, u, half, layer):
                g, c = u // QC, u % QC
                if half == 0:
                    if u == 0:
                        pe.wait_ge(m_loaded[b.p], b.use * 16 + 16)
                        if layer == 0:
                            pe.wait_ge(s["mask_k_ready"], b.n + 1)
                    pe.wait_ge(s["exp_done"], b.n * UNITS + u - 1 + ST_CREDIT)
                bank = ps[2 * (u % 2) + half]
                for j in range(2):
                    h = g * HG + 2 * half + j
                    ins = pe.matmul(bank[:, j * S:(j + 1) * S], qk[0:ROWS, b.p, 1, h, c * P:(c + 1) * P],
                                    qk[0:ROWS, b.p, 0, h, :], start=(j == 0), stop=(layer == 1), skip_group_check=True)
                if layer == 0:
                    ins = pe.matmul(bank[:, :].rearrange("p (h s) -> p h s", h=2), ident16[:, :],
                                    mask_k[:, b.p, c:c + 1, :].broadcast_to([P, 2, S]), start=False, stop=True, skip_group_check=True)
                if half == 1:
                    ins.then_inc(s["st_ready"], 1)

            def values(b, u):
                g, c = u // QC, u % QC
                if u == 0:
                    pe.wait_ge(s["v_ready"], b.n + 1)
                pe.wait_ge(s["exp_done"], b.n * UNITS + u + 1 + ST_CREDIT)
                if c == 0:
                    pe.wait_ge(s["o_read"], b.n * G + g + O_CREDIT)
                for j in range(HG):
                    ins = pe.matmul(pv_bank[32 * j:32 * j + 32, 0:S], v[:, b.p, c, g * HG + j, :],
                                    prob[:, u % 4, j, :], start=(c == 0), stop=(c == QC - 1), tile_position=(0, 32 * j), skip_group_check=True)
                ins.then_inc(s["pv_done"], 1)

            def o_proj(b, layer):
                pe.wait_ge(s["o_ready"], b.n * G // 2 + G // 2 + O_CREDIT)
                for t in range(QC):
                    for g in range(G // 2):
                        ins = pe.matmul(o_bank[:, t * D:(t + 1) * D], osb[:, g, t * P:(t + 1) * P], wo[layer][:, g, :],
                                        start=(g == 0), stop=(g == G // 2 - 1), skip_group_check=True)
                ins.then_inc(s["oproj"], 1)

            def prologue(layer):
                base = layer * B // 2
                if layer == 0:
                    pe.wait_ge(s["ident_done"], 4)
                    pe.wait_ge(s["ctx_in0"], 16)
                else:
                    pe.wait_ge(s["acc_done"], FFN0_ACC)
                pe.wait_ge(weights_in[layer][0], 16 * 6)
                for k in range(2):
                    b = Batch(base, k)
                    if k == 1:
                        pe.wait_ge(s["qf_ready"], b.n * 2)
                    if k == 0:
                        k_proj(b, k, layer)
                    else:
                        k_matmul(k, layer)
                    xn_transpose(b)
                    q_proj(b, layer)
                b = Batch(base, 0)
                for g in range(G):
                    for k in range(4):
                        max_unit(b, g, k, layer)
                pe.wait_ge(s["qf_ready"], b.n * 2 + 4)
                max_transpose(b)
                v_proj(b, layer)
                pe.wait_ge(weights_in[layer][1], 16 * 3)
                if layer == 0:
                    pe.wait_ge(s["ctx_in"], 16)

            def iteration(layer, b, at, more, prep):
                b1, b2 = b.plus(1), b.plus(2)
                for u in range(UNITS):
                    first = more and u < G
                    if prep and u == 0:
                        k_proj(b2, at + 2, layer)
                    scores(b, u, 0, layer)
                    if first:
                        max_unit(b1, u, 0, layer)
                    scores(b, u, 1, layer)
                    if first:
                        max_unit(b1, u, 1, layer)
                    if u > 0:
                        values(b, u - 1)
                    if first:
                        max_unit(b1, u, 2, layer)
                    if prep and u == 1:
                        xn_transpose(b2)
                    if prep and u == 2:
                        q_proj(b2, layer)
                    if first:
                        max_unit(b1, u, 3, layer)
                    if more and u == 6:
                        if prep:
                            pe.wait_ge(s["qf_ready"], b2.n * 2 + 2)
                        else:
                            pe.wait_ge(s["v_ready"], b.n + 1)
                        max_transpose(b1)
                values(b, UNITS - 1)
                if more:
                    v_proj(b1, layer)
                    pe.wait_ge(s["mx_done"], (b.n + 2) * MAXU)
                else:
                    pe.wait_ge(s["resid"], b.n + O_CREDIT)
                o_proj(b, layer)

            def route(layer):
                pe.wait_ge(s["resid"], (layer + 1) * B + O_CREDIT)
                with pe.Fori(0, RBLOCKS // 2) as i:
                    for k in range(2):
                        n = i * 2 + k + layer * RBLOCKS
                        pe.wait_ge(s["rt_Tcopy"], n * 2 - 2 + RT_CREDIT)
                        for t in range(RB):
                            pe.wait_ge(s["rt_xn"], n * RB + t + 1)
                            for c in range(C):
                                ins = pe.transpose(ps[2 * k + t // 2][:, (t % 2 * C + c) * P:(t % 2 * C + c + 1) * P],
                                                   rn[:, k, t, c * P:(c + 1) * P], ident[:, :])
                            if t % 2 == 1:
                                ins.then_inc(s["rt_T"], 1)
                    for k in range(2):
                        n = i * 2 + k + layer * RBLOCKS
                        pe.wait_ge(s["rt_Tcopy"], n * 2 + 2 + RT_CREDIT)
                        pe.wait_ge(s["rt_lgcopy"], n - 1 + RT_CREDIT)
                        for t in range(RB):
                            for c in range(C):
                                ins = pe.matmul(ps[4 + k][:, t * NE:(t + 1) * NE], rnT[:, k, t, c, :], wr[layer][:, c, :],
                                                start=(c == 0), stop=(c == C - 1), skip_group_check=True)
                        ins.then_inc(s["rt_lg"], 1)

            for name in ("rt_T", "rt_lg"):
                pe.sem_inc(s[name], RT_CREDIT)
            pe.sem_inc(s["eT_psum"], HID_CREDIT)
            pe.sem_inc(s["pv_done"], PV_CREDIT)
            pe.sem_inc(s["oproj"], O_CREDIT)
            batches(pe, 0, prologue, iteration)
            route(0)
            pe.wait_ge(s["rt_copy"], RBLOCKS + RT_CREDIT)
            pe.wait_ge(s["rt_lgcopy"], RBLOCKS + RT_CREDIT)

            HALVES = ((0, 0), (0, 1), (1, 0))

            def gate_up(k, blk, f):
                for j in range(2):
                    for c in range(C):
                        base = (j * C + c) * D + f * P
                        for a, z in HALVES:
                            ins = pe.matmul(ps[2 * f + j][:, :], w0_part[k][a][:, base:base + P], xnT_part[z][:, c, blk * BLK:(blk + 1) * BLK],
                                            start=(c == 0 and (a, z) == HALVES[0]), stop=(c == C - 1 and (a, z) == HALVES[-1]), skip_group_check=True)
                ins.then_inc(s["gu_psum"], 1)

            def down(n, k, r):
                pe.wait_ge(s["h_low"], n * C + C + GU_CREDIT)
                for t in range(4):
                    pe.wait_ge(s["acc_done"], n * 4 + t - 3 + ACC_CREDIT)
                    for f in range(C):
                        base = (2 * C + f) * D
                        for a, z in HALVES:
                            ins = pe.matmul(ps[4 + t][:, 0:D], h0_part[z][:, r, f, t * P:(t + 1) * P], w0_part[k][a][:, base:base + D],
                                            start=(f == 0 and (a, z) == HALVES[0]), stop=(f == C - 1 and (a, z) == HALVES[-1]), skip_group_check=True)
                    ins.then_inc(s["down_psum"], 1)

            with pe.Fori(0, NE // 2) as i:
                for k in range(2):
                    pe.wait_ge(s["w0_low"], (i * 2 + k) * 3 + 3 + W0_CREDIT)
                    for blk in range(4):
                        n = (i * 2 + k) * 4 + blk
                        for f in range(C):
                            pe.wait_ge(s["h_done"], n * C + f - 1 + GU_CREDIT)
                            gate_up(k, blk, f)
                        if blk > 0:
                            down(n - 1, k, (blk - 1) % 2)
                    down((i * 2 + k) * 4 + 3, k, 1)

            batches(pe, 1, prologue, iteration)
            route(1)
            pe.wait_ge(s["route_vec"], ROUTE1_HOT)
            hot_v = hot16[:, :, :].rearrange("p t e -> p (t e)")
            pe.matmul(ps[4][:, 0:T * NE], below[:, :], hot_v, start=True, stop=True)
            pe.matmul(ps[5][:, 0:T * NE], ones16[:, :], hot_v, start=True, stop=True).then_inc(s["route_pe"], 1)
            pe.wait_ge(s["route_vec"], ROUTE1_SLOTS)
            pe.wait_ge(s["rt_lgcopy"], 2 * RBLOCKS + RT_CREDIT)
            def rows_transpose(i, k, e):
                pe.wait_ge(er_in[k], i * 32 + 32)
                if not (isinstance(e, int) and e == 0):
                    pe.wait_ge(s["eT_low"], e)
                for c in range(C):
                    for a in range(3):
                        n = P if a < 2 else CAP - 2 * P
                        ins = pe.transpose(ps[c][:, a * P:a * P + n], erow[0:n, k, a, c * P:(c + 1) * P], ident[0:n, 0:n])
                ins.then_inc(s["eT_psum"], 1)

            def expert(i, k, more):
                e = i * 2 + k
                pe.wait_ge(s["w_low"], e * 2 * PIECES + PIECES)
                pe.wait_ge(s["eT_low"], e + 1)
                for f in range(FF // P):
                    if f >= 5:
                        pe.wait_ge(s["hid_low"], e * (FF // P) + f - 2)
                    for c in range(C):
                        for a, z in HALVES:
                            ins = pe.matmul(hid_bank[f][:, 0:CAP], w_part[0][a][:, c * FF + f * P:c * FF + (f + 1) * P],
                                            eT_part[z][:, k, c, :], start=(c == 0 and (a, z) == HALVES[0]), stop=(c == C - 1 and (a, z) == HALVES[-1]))
                    ins.then_inc(s["hid_psum"], 1)
                if more:
                    rows_transpose(i + k, 1 - k, e + 1)
                for t in range(3):
                    n = P if t < 2 else CAP - 2 * P
                    pe.wait_ge(s["eo_done"], e * 3 + t - 2 + EO_CREDIT)
                    for f in range(FF // P):
                        if t == 0:
                            pe.wait_ge(s["hid_low"], e * (FF // P) + f + 1)
                            pe.wait_ge(s["w_low"], (e * 2 + 1) * PIECES + f * PIECES // (FF // P) + 1)
                        for a, z in HALVES:
                            ins = pe.matmul(ps[4 + t][0:n, 0:D], hT_part[z][:, f, t * P:t * P + n], w_part[1][a][:, f * D:(f + 1) * D],
                                            start=(f == 0 and (a, z) == HALVES[0]), stop=(f == FF // P - 1 and (a, z) == HALVES[-1]))
                    ins.then_inc(s["eo_psum"], 1)

            rows_transpose(0, 0, 0)
            with pe.Fori(0, NE // 2 - 1) as i:
                for k in range(2):
                    expert(i, k, True)
            expert(NE // 2 - 1, 0, True)
            expert(NE // 2 - 1, 1, False)

        @block.vector
        def _(dve):
            dve.memset(xn_all[:, 0, :], 0.0).then_inc(s["zeros_set"], 1)
            dve.memset(v[:, :, :, :, HD:2 * HD], 1.0).then_inc(s["ones_set"], 1)
            dve.memset(all_ok[:, :], 1).then_inc(s["ones_set"], 1)

            def norm_stats(layer, a, z):
                for t in range(a, z):
                    dve.bn_stats(stats_all[:, t, :], xs[:, t, :]).then_inc(s["ln"], 1)
                dve.wait_ge(s["ln"], (layer * T + a) * 2 + z - a)
                for t in range(a, z):
                    dve.bn_aggr(mean_var[:, t, :], stats_all[:, t, :]).then_inc(s["ln"], 1)

            def k_evac(b, at, layer):
                dve.wait_ge(s["k_psum"], b.n + 1)
                wait(dve, "ks_pool", b.n * 2)
                ok = all_ok[:, :] if layer == 0 else key_ok[:, bass.ds(at * S, S)]
                for c in range(C):
                    dve.scalar_tensor_tensor(out=kf[:, c, :], in0=misc[:, c * S:(c + 1) * S], scalar=bk[layer][:, c:c + 1], in1=ok,
                                             op0=ALU.add, op1=ALU.mult).then_inc(s["kf_ready"], 1)

            def v_evac(b, layer):
                dve.wait_ge(s["v_psum"], b.n + 1)
                dve.tensor_tensor(v[:, b.p, :, :, 0:HD], misc[:, :].rearrange("p (t h d) -> p t h d", t=QC, h=H),
                                  bv[layer][:, :].rearrange("p (o h d) -> p o h d", o=1, h=H).broadcast_to([P, QC, H, HD]), ALU.add).then_inc(s["v_ready"], 1)

            def reduce_max(b, g):
                for k in range(4):
                    pair, c = 2 * g + k // 2, k % 2
                    dve.wait_ge(s["max_psum"], b.n * MAXU + 4 * g + k + 1)
                    dve.tensor_reduce(mx[:, c, 2 * pair:2 * pair + 2], mps[k % 2][:, :].rearrange("p (h s) -> p h s", h=2),
                                      AX_X, ALU.max).then_inc(s["mx_done"], 1)

            def split_max(b):
                dve.wait_ge(s["mx_done"], b.n * MAXU + MAXU)
                wait(dve, "mT_psum", b.n)
                dve.tensor_scalar(m_split[:, :, 0, :], mx[:, :, :], -1.0, None, ALU.mult).then_inc(s["m_chain"], 1)
                dve.wait_ge(s["m_chain"], b.n * 4 + 1)
                dve.scalar_tensor_tensor(out=m_rest[:, :, :], in0=mx[:, :, :], scalar=-1.0, in1=m_split[:, :, 0, :],
                                         op0=ALU.mult, op1=ALU.subtract).then_inc(s["m_chain"], 1)
                dve.wait_ge(s["m_chain"], b.n * 4 + 2)
                dve.tensor_copy(m_split[:, :, 1, :], m_rest[:, :, :]).then_inc(s["m_chain"], 1)
                dve.wait_ge(s["m_chain"], b.n * 4 + 3)
                dve.tensor_tensor(m_split[:, :, 2, :], m_rest[:, :, :], m_split[:, :, 1, :], ALU.subtract).then_inc(s["m_chain"], 1)

            def max_evac(b):
                dve.wait_ge(s["mT_psum"], b.n + 1)
                wait(dve, "m_written", b.n * 16)
                dve.tensor_copy(m_T[:, :], misc[0:TERM * H, :].bitcast(BF16)[:, 0:S]).then_inc(s["mT_ready"], 1)

            def normalise(b, g):
                n = b.n * G + g
                dve.wait_ge(s["pv_done"], b.n * UNITS + 2 * g + 2 + PV_CREDIT)
                dve.wait_ge(s["o_chain"], n * 2 + O_CREDIT)
                dve.transpose(oT[:, :, :].rearrange("p a r -> p (a r)"), pv_bank[:, 0:S]).then_inc(s["o_read"], 1)
                dve.wait_ge(s["o_read"], n + 1 + O_CREDIT)
                dve.reciprocal(o_inv[:, :], oT[:, :, HD]).then_inc(s["o_chain"], 1)
                dve.wait_ge(s["o_chain"], n * 2 + 1 + O_CREDIT)
                if g % 2 == 0:
                    dve.wait_ge(s["o_ready"], b.n * G // 2 + g // 2 + O_CREDIT)
                rows = slice(g % 2 * HD, (g % 2 + 1) * HD)
                dve.tensor_tensor(o_norm[:, :, rows], oT[:, :, 0:HD], o_inv[:, :].rearrange("p (a o) -> p a o", o=1).broadcast_to([P, S // 32, HD]), ALU.mult).then_inc(s["o_chain"], 1)
                if g % 2 == 1:
                    dve.wait_ge(s["o_chain"], n * 2 + 2 + O_CREDIT)
                    if g == 1:
                        dve.wait_ge(s["oproj"], b.n + O_CREDIT)
                    dve.transpose(osb[:, g // 2, :], o_norm[:, :, :].rearrange("p a r -> p (a r)")).then_inc(s["o_ready"], 1)

            def residual(b, at):
                dve.wait_ge(s["oproj"], b.n + 1 + O_CREDIT)
                dve.wait_ge(s["bias_added"], b.n + 1)
                xv = xs[:, bass.ds(at * QC, QC), :]
                dve.tensor_tensor(xv, o_bank[:, :].rearrange("p (t d) -> p t d", t=QC), xv, ALU.add).then_inc(s["resid"], 1)
                dve.wait_ge(s["resid"], b.n + 1 + O_CREDIT)
                settle(dve)
                for t in range(QC):
                    dve.bn_stats(stats_all[:, bass.ds(at * QC + t, 1), :].rearrange("p a k -> p (a k)"),
                                 xs[:, bass.ds(at * QC + t, 1), :].rearrange("p a d -> p (a d)")).then_inc(s["rt_stats"], 1)

            def prologue(layer):
                base = layer * B // 2
                if layer == 0:
                    dve.wait_ge(s["x_in0"], 32)
                    dve.wait_ge(s["ones_set"], 2)
                else:
                    dve.wait_ge(s["acc_done"], FFN0_ACC)
                    dve.wait_ge(s["valid_in"], 32)
                dve.wait_ge(weights_in[layer][0], 16 * 6)
                b0, b1 = Batch(base, 0), Batch(base, 1)
                norm_stats(layer, 0, 2 * QC)
                k_evac(b0, 0, layer)
                if layer == 1:
                    dve.memset(big[ROW_MASK:P, :], TWO_ONES).then_inc(s["ones_again"], 1)
                k_evac(b1, 1, layer)
                if layer == 0:
                    dve.wait_ge(s["x_in"], 16)
                norm_stats(layer, 2 * QC, T)
                b = Batch(base, 0)
                for g in range(G):
                    reduce_max(b, g)
                split_max(b)
                max_evac(b)
                v_evac(b, layer)

            def iteration(layer, b, at, more, prep):
                b1, b2 = b.plus(1), b.plus(2)
                if more:
                    reduce_max(b1, 0)
                if prep:
                    k_evac(b2, at + 2, layer)
                if more:
                    reduce_max(b1, 1)
                if more:
                    reduce_max(b1, 2)
                normalise(b, 0)
                if more:
                    reduce_max(b1, 3)
                normalise(b, 1)
                if more:
                    split_max(b1)
                    max_evac(b1)
                normalise(b, 2)
                normalise(b, 3)
                if more:
                    v_evac(b1, layer)
                residual(b, at)

            def route(layer):
                dve.wait_ge(s["rt_stats"], (layer + 1) * T)
                for t in range(T):
                    dve.bn_aggr(mv_all[:, t, :], stats_all[:, t, :]).then_inc(s["rt_ln"], 1)
                dve.wait_ge(s["rt_rstd"], (layer + 1) * ROOT_STEPS)
                with dve.Fori(0, RBLOCKS // 2) as i:
                    for k in range(2):
                        n = i * 2 + k + layer * RBLOCKS
                        dve.wait_ge(s["rt_T"], n * 2 - 2 + RT_CREDIT)
                        dve.wait_ge(s["rt_copy"], n - 1 + RT_CREDIT)
                        settle(dve)
                        for t in range(RB):
                            tile = (i * 2 + k) * RB + t
                            dve.tensor_scalar(rn[:, k, t, :], xs[:, bass.ds(tile, 1), :].rearrange("p a d -> p (a d)"),
                                              mv_all[:, bass.ds(tile, 1), 0:1].rearrange("p a o -> p (a o)"), rstd_all[:, bass.ds(tile, 1)],
                                              ALU.subtract, ALU.mult).then_inc(s["rt_xn"], 1)
                    for k in range(2):
                        n = i * 2 + k + layer * RBLOCKS
                        if layer == 0:
                            dve.wait_ge(s["rt_Tcopy"], n * 2 + 2 + RT_CREDIT)
                            hi, lo = [a[:, :, bass.ds((i * 2 + k) * RB * P, RB * P)].rearrange("p c (t s) -> p t c s", t=RB) for a in xnT_part]
                            dve.tensor_copy(hi, rnT[:, k, :, :, :]).then_inc(s["rt_high"], 1)
                            dve.wait_ge(s["rt_high"], n + 1)
                            settle(dve)
                            dve.tensor_tensor(lo, rnT[:, k, :, :, :], hi, ALU.subtract).then_inc(s["rt_copy"], 1)
                        else:
                            dve.wait_ge(s["rt_xn"], n * RB + RB)
                            dve.tensor_copy(xn_all[:, bass.ds((i * 2 + k) * RB, RB), :], rn[:, k, :, :]).then_inc(s["rt_copy"], 1)
                dve.wait_ge(s["rt_lgcopy"], (layer + 1) * RBLOCKS + RT_CREDIT)
                dve.wait_ge(s["rt_copy"], (layer + 1) * RBLOCKS + RT_CREDIT)

            route_count = [0]

            def link(ins):
                ins.then_inc(s["route_vec"], 1)
                route_count[0] += 1
                dve.wait_ge(s["route_vec"], route_count[0])

            def bc(a):
                return a.rearrange("p (t o) -> p t o", o=1).broadcast_to([P, T, NE])

            def per_e(a):
                return a.rearrange("p (o e) -> p o e", o=1).broadcast_to([P, T, NE])

            for name in ("o_read", "o_chain", "o_ready", "resid"):
                dve.sem_inc(s[name], O_CREDIT)
            dve.sem_inc(s["rt_copy"], RT_CREDIT)
            batches(dve, 0, prologue, iteration)
            route(0)
            dve.wait_ge(s["w0_in"], 48)
            for j in range(3):
                part = slice(j * C * D, (j + 1) * C * D)
                dve.tensor_copy(w0_part[0][0][:, part], w0_raw[:, part]).then_inc(s["w0_high"], 1)
            dve.wait_ge(s["router_bias_in"], 16)
            link(dve.tensor_tensor(lgb[:, :, :], lg[:, :, :], per_e(br[:, :]), ALU.add))
            for t in range(T):
                ins = dve.max(top[:, t, :], lgb[:, t, :])
            link(ins)
            for t in range(T):
                ins = dve.max_index(top_i[:, t, :], top[:, t, :], lgb[:, t, :])
            link(ins)
            for k in range(2):
                link(dve.tensor_copy(pick[:, k, :], top_i[:, :, k]))
                link(dve.tensor_tensor(hot[:, k, :, :], per_e(iota8[:, :]), bc(pick[:, k, :]), ALU.is_equal))
            link(dve.tensor_tensor(wts[:, 0, :], top[:, :, 1], top[:, :, 0], ALU.subtract))
            assert route_count[0] == ROUTE0_DIFF
            dve.wait_ge(s["route_act"], 1)
            link(dve.tensor_scalar(wts[:, 2, :], wts[:, 1, :], 1.0, None, ALU.add))
            link(dve.reciprocal(wts[:, 3, :], wts[:, 2, :]))
            link(dve.tensor_tensor(wts[:, 2, :], wts[:, 1, :], wts[:, 3, :], ALU.mult))
            link(dve.tensor_tensor(gate[:, 0, :, :], hot[:, 0, :, :], bc(wts[:, 3, :]), ALU.mult))
            link(dve.tensor_tensor(gate[:, 1, :, :], hot[:, 1, :, :], bc(wts[:, 2, :]), ALU.mult))
            link(dve.tensor_tensor(gate[:, 0, :, :], gate[:, 0, :, :], gate[:, 1, :, :], ALU.add))

            def add_down(n, e, blk):
                for t in range(4):
                    tile = blk * 4 + t
                    dve.wait_ge(s["down_psum"], n * 4 + t + 1)
                    dve.wait_ge(s["acc_done"], n * 4 + t - T + ACC_CREDIT + 1)
                    dve.scalar_tensor_tensor(out=xs[:, tile, :], in0=ps[4 + t][:, 0:D],
                                             scalar=gate[:, 0, tile, bass.ds(e, 1)], in1=xs[:, tile, :], op0=ALU.mult, op1=ALU.add).then_inc(s["acc_done"], 1)

            dve.sem_inc(s["acc_done"], ACC_CREDIT)
            dve.sem_inc(s["h_done"], GU_CREDIT)

            def w0_high(e, k, j):
                part = slice(j * C * D, (j + 1) * C * D)
                if j == 0:
                    dve.wait_ge(s["w0_in"], (e + 1) * 48)
                dve.tensor_copy(w0_part[k][0][:, part], w0_raw[:, part]).then_inc(s["w0_high"], 1)

            def expert0(i, k, more):
                e = i * 2 + k
                for blk in range(T // 4):
                    n = e * 4 + blk
                    for f in range(C):
                        dve.wait_ge(s["silu_done"], n * C + f + 1)
                        dve.wait_ge(s["h_low"], n * C + f - 1 + GU_CREDIT)
                        dve.tensor_tensor(h0[:, f, :], silu[:, f, :], ps[2 * f + 1][:, :], ALU.mult).then_inc(s["h_done"], 1)
                        dve.wait_ge(s["h_done"], n * C + f + 1 + GU_CREDIT)
                        dve.tensor_copy(h0_part[0][:, blk % 2, f, :], h0[:, f, :]).then_inc(s["h_high"], 1)
                    if blk > 0:
                        add_down(n - 1, e, blk - 1)
                        if more:
                            w0_high(e + 1, 1 - k, blk - 1)
                add_down(e * 4 + 3, e, 3)

            with dve.Fori(0, NE // 2 - 1) as i:
                for k in range(2):
                    expert0(i, k, True)
            expert0(NE // 2 - 1, 0, True)
            expert0(NE // 2 - 1, 1, False)

            batches(dve, 1, prologue, iteration)
            dve.wait_ge(s["slots_zero"], 16)
            route(1)
            for t in range(T):
                ins = dve.max(top[:, t, :], lg[:, t, :])
            link(ins)
            for t in range(T):
                ins = dve.max_index(top_i[:, t, :], top[:, t, :], lg[:, t, :])
            link(ins)
            link(dve.tensor_copy(pick[:, 0, :], top_i[:, :, 0]))
            link(dve.tensor_tensor(hot[:, 0, :, :], per_e(iota8[:, :]), bc(pick[:, 0, :]), ALU.is_equal))
            link(dve.tensor_copy(hot16[:, :, :], hot[:, 0, :, :]))
            assert route_count[0] == ROUTE1_HOT
            link(dve.tensor_tensor(gate[:, 1, :, :], lg[:, :, :], top[:, :, 0:1].broadcast_to([P, T, NE]), ALU.subtract))
            assert route_count[0] == ROUTE1_DIFF
            dve.wait_ge(s["route_act"], 2)
            link(dve.tensor_reduce(wts[:, 0, :], gate[:, 0, :, :], AX_X, ALU.add))
            link(dve.reciprocal(wts[:, 1, :], wts[:, 0, :]))
            dve.wait_ge(s["route_pe"], 1)
            link(dve.tensor_copy(cnt[:, 0, :, :], ps[5][:, 0:T * NE].rearrange("p (t e) -> p t e", t=T)))
            cur = 0
            step = 1
            while step < T:
                link(dve.tensor_tensor(cnt[:, 1 - cur, step:T, :], cnt[:, cur, step:T, :], cnt[:, cur, 0:T - step, :], ALU.add))
                link(dve.tensor_copy(cnt[:, 1 - cur, 0:step, :], cnt[:, cur, 0:step, :]))
                cur, step = 1 - cur, step * 2
            link(dve.tensor_tensor(rank[:, :, :], cnt[:, cur, :, :], ps[5][:, 0:T * NE].rearrange("p (t e) -> p t e", t=T), ALU.subtract))
            link(dve.tensor_tensor(rank[:, :, :], rank[:, :, :], ps[4][:, 0:T * NE].rearrange("p (t e) -> p t e", t=T), ALU.add))
            link(dve.tensor_tensor(rank[:, :, :], rank[:, :, :], hot[:, 0, :, :], ALU.mult))
            link(dve.tensor_reduce(pos[:, 0, :], rank[:, :, :], AX_X, ALU.add))
            link(dve.tensor_scalar(pos[:, 1, :], pos[:, 0, :], float(CAP), None, ALU.is_lt))
            link(dve.tensor_scalar(pos[:, 2, :], pos[:, 0, :], float(CAP - 1), None, ALU.min))
            link(dve.scalar_tensor_tensor(out=pos[:, 2, :], in0=pick[:, 0, :], scalar=float(CAP), in1=pos[:, 2, :], op0=ALU.mult, op1=ALU.add))
            link(dve.tensor_scalar(pos[:, 3, :], pos[:, 1, :], -float(SKIP), float(SKIP), ALU.mult, ALU.add))
            link(dve.tensor_tensor(pos[:, 3, :], pos[:, 3, :], pos[:, 2, :], ALU.add))
            link(dve.tensor_copy(slot[:, 1, :], pos[:, 2, :]))
            link(dve.tensor_copy(slot[:, 0, :], pos[:, 3, :]))
            assert route_count[0] == ROUTE1_SLOTS
            link(dve.tensor_tensor(wts[:, 2, :], wts[:, 1, :], pos[:, 1, :], ALU.mult))
            link(dve.tensor_scalar(wts[:, 3, :], pos[:, 1, :], -1.0, 1.0, ALU.mult, ALU.add))

            for t in range(T):
                dve.scalar_tensor_tensor(out=xs[:, t, :], in0=xn_all[:, t, :], scalar=wts[:, 3, t:t + 1], in1=xs[:, t, :],
                                         op0=ALU.mult, op1=ALU.add).then_inc(s["x_plus"], 1)

            def w_low(e, w, piece):
                dve.wait_ge(s["w_high"], (e * 2 + w) * PIECES + piece + 1)
                part = slice(piece * PIECE, (piece + 1) * PIECE)
                dve.tensor_tensor(w_part[w][1][:, part], w_raw[:, w, part], w_part[w][0][:, part], ALU.subtract).then_inc(s["w_low"], 1)

            def rows_low(k, e):
                dve.wait_ge(s["eT_high"], e + 1)
                for c in range(C):
                    ins = dve.tensor_tensor(eT_part[1][:, k, c, :], ps[c][:, 0:CAP], eT_part[0][:, k, c, :], ALU.subtract)
                ins.then_inc(s["eT_low"], 1)

            def expert1(i, k, more):
                e = i * 2 + k
                for f in range(FF // P):
                    dve.wait_ge(s["hid_high"], e * (FF // P) + f + 1)
                    dve.scalar_tensor_tensor(out=hT_part[1][:, f, :], in0=hid_bank[f][:, 0:CAP], scalar=0.0, in1=hT_part[0][:, f, :],
                                             op0=ALU.max, op1=ALU.subtract).then_inc(s["hid_low"], 1)
                    if f % 2 == 0:
                        w_low(e, 1, f // 2)
                if more:
                    rows_low(1 - k, e + 1)
                    for piece in range(PIECES):
                        w_low(e + 1, 0, piece)

            for piece in range(PIECES):
                w_low(0, 0, piece)
            rows_low(0, 0)
            dve.wait_ge(s["scattered"], 16 * T)
            with dve.Fori(0, NE // 2 - 1) as i:
                for k in range(2):
                    expert1(i, k, True)
            expert1(NE // 2 - 1, 0, True)
            expert1(NE // 2 - 1, 1, False)
            dve.wait_ge(s["x_plus"], T)
            for t in range(T):
                dve.wait_ge(gathered[t % 8], 16 * (t // 8 + 1))
                if t >= 8:
                    dve.wait_ge(out_stored[t % 8], 16 * (t // 8))
                dve.scalar_tensor_tensor(out=fin[:, t % 8, :], in0=got[:, t % 8, :], scalar=wts[:, 2, t:t + 1], in1=xs[:, t, :],
                                         op0=ALU.mult, op1=ALU.add).then_inc(s["fin_done"], 1)


def _by_channel(w):
    return w.reshape(w.shape[:-1] + (H, HD)).swapaxes(-1, -2).reshape(w.shape)


def _by_pairs(w):
    return w.reshape(G // 2, 2, HG, HD, D).swapaxes(1, 2).reshape(D, D)


def kernel(**inputs):
    import concourse.bacc as _bacc
    from concourse.bass_utils import run_bass_kernel_spmd as _run

    nc = _bacc.Bacc("TRN2", target_bir_lowering=False, num_devices=1)
    a = {k: np.asarray(v) for k, v in inputs.items()}
    wkv, bkv = a["L1_xattn_Wkv"], a["L1_xattn_bkv"]
    lay = {
        "x": a["x"], "ctx_t": a["ctx_1024"].reshape(B * S, D).T,
        "mask": a["mask_Bx1xSxS2_ik1"][:, 0], "mask_t": a["mask_Bx1xSxS2_ik1"][:, 0].swapaxes(1, 2),
        "valid": a["mask_BxS2_bf1"],
        "wq0": _by_channel(a["L0_xattn_Wq"].T), "bq0": _by_channel(a["L0_xattn_bq"]),
        "wk0": _by_channel(a["L0_xattn_Wk"].T), "bk0": _by_channel(a["L0_xattn_bk"]),
        "wv0": a["L0_xattn_Wv"].T, "bv0": a["L0_xattn_bv"], "wo0": _by_pairs(a["L0_xattn_Wo"].T), "bo0": a["L0_xattn_bo"],
        "wq1": _by_channel(a["L1_xattn_Wq"]), "bq1": _by_channel(a["L1_xattn_bq"]),
        "wk1": _by_channel(wkv[:, :D]), "bk1": _by_channel(bkv[:D]),
        "wv1": wkv[:, D:], "bv1": bkv[D:], "wo1": _by_pairs(a["L1_xattn_Wp"]), "bo1": a["L1_xattn_bp"],
        "wr0": a["L0_ffn_router_w"], "br0": a["L0_ffn_router_b"],
        "gate": a["L0_ffn_we_gate"], "up": a["L0_ffn_we_up"], "down": a["L0_ffn_we_down"],
        "wr1": a["L1_ffn_Wr"], "w1": a["L1_ffn_W1"], "w2": a["L1_ffn_W2"],
    }
    arrays, ap = {}, {}
    for name, arr in lay.items():
        arr = np.ascontiguousarray(arr)
        arrays[f"in_{name}"] = arr
        ap[name] = nc.dram_tensor(f"in_{name}", arr.shape, mybir.dt.from_np(arr.dtype), kind="ExternalInput").ap()
    out = nc.dram_tensor("out_0", (B, S, D), F32, kind="ExternalOutput").ap()
    attn = [{k: ap[f"{k}{i}"] for k in ("wq", "bq", "wk", "bk", "wv", "bv", "wo", "bo")} for i in range(2)]
    l0 = {"wr": ap["wr0"], "br": ap["br0"], "gate": ap["gate"], "up": ap["up"], "down": ap["down"]}
    l1 = {"wr": ap["wr1"], "w1": ap["w1"], "w2": ap["w2"]}
    build(nc, ap["x"], ap["ctx_t"], ap["mask"], ap["mask_t"], ap["valid"], attn, l0, l1, out)
    r = _run(nc, [arrays], core_ids=[0])
    return r.results[0]["out_0"]
```
